# Optimizing a Trainium2 kernel written in Bass

```python
import numpy as np
import jax
import jax.numpy as jnp

def _softmax(x, axis=-1):
    return jax.nn.softmax(x, axis=axis)

def _gelu(x):
    return jax.nn.gelu(x, approximate=True)

def _silu(x):
    return jax.nn.silu(x)

def _sigmoid(x):
    return jax.nn.sigmoid(x)

def _layernorm(x, axis=-1, eps=1e-05):
    m = jnp.mean(x, axis=axis, keepdims=True)
    v = jnp.var(x, axis=axis, keepdims=True)
    return (x - m) / jnp.sqrt(v + eps)

def _scatter_add(tgt, idx, src, axis=0):
    return tgt.at[idx].add(src)

def _segment_sum(src, seg, n):
    return jax.ops.segment_sum(src, seg, n)
kernel_name = 'mk_gps_d1_gnn_r32_79edb9'

def setup_inputs(seed: int=0):
    np.random.seed(seed)
    _w = jnp.asarray

    def _rec_inputs():
        import jax
        import jax.numpy as jnp
        _gk = jax.random.key(seed)
        x = -0.0003713 + 1 * jax.random.normal(jax.random.fold_in(_gk, 1), (3125, 256), jnp.float32)
        _s = jax.random.randint(jax.random.fold_in(_gk, 2), (25000,), 0, 3125, jnp.int32)
        _d = jax.random.randint(jax.random.fold_in(_gk, 3), (25000,), 0, 3125, jnp.int32)
        _loop = jnp.arange(3125, dtype=jnp.int32)
        src = jnp.concatenate([_s, _d, _loop])
        dst = jnp.concatenate([_d, _s, _loop])
        _o = jnp.argsort(dst, stable=True)
        src = src[_o]
        dst = dst[_o]
        return (x, src, dst)
    x, src, dst = _rec_inputs()

    def _L0_gnn_setup():
        import jax, jax.numpy as jnp
        import numpy as np
        N_NODES = 50000
        N_EDGES = 312500
        WIDTH = 256
        LN_EPS = 1e-05

        def gcn_conv(x, edge_index, W, b):
            n = x.shape[0]
            loops = jnp.arange(n, dtype=edge_index.dtype)
            src = jnp.concatenate([edge_index[0], loops])
            dst = jnp.concatenate([edge_index[1], loops])
            deg = jax.ops.segment_sum(jnp.ones_like(dst, dtype=x.dtype), dst, num_segments=n)
            dinv = jnp.where(deg > 0, jax.lax.rsqrt(deg), 0.0)
            norm = dinv[src] * dinv[dst]
            h = x @ W.T
            msgs = norm[:, None] * h[src]
            out = jax.ops.segment_sum(msgs, dst, num_segments=n)
            return out + b

        def layer_norm(x, gamma, beta):
            mu = jnp.mean(x, axis=-1, keepdims=True)
            var = jnp.mean(jnp.square(x - mu), axis=-1, keepdims=True)
            return (x - mu) * jax.lax.rsqrt(var + LN_EPS) * gamma + beta
        key = jax.random.key(seed)
        k1, k2, k3, k4 = jax.random.split(key, 4)
        x = jax.random.normal(k1, (N_NODES, WIDTH), dtype=jnp.float32)
        edge_index = jax.random.randint(k2, (2, N_EDGES), 0, N_NODES, dtype=jnp.int64)
        W = jax.random.normal(k3, (WIDTH, WIDTH), dtype=jnp.float32) / np.sqrt(WIDTH)
        b = jax.random.normal(k4, (WIDTH,), dtype=jnp.float32) * 0.01
        gamma = jnp.ones((WIDTH,), dtype=jnp.float32)
        beta = jnp.zeros((WIDTH,), dtype=jnp.float32)
        return {'x': x, 'edge_index': edge_index, 'W': W, 'b': b, 'gamma': gamma, 'beta': beta}
    _L0_gnn_all = _L0_gnn_setup()
    _L0_gnn_in = {k: v for k, v in _L0_gnn_all.items() if k in ('W', 'b', 'gamma', 'beta')}
    del _L0_gnn_all

    def _L0_mix_setup():
        import jax, jax.numpy as jnp
        import numpy as np
        DIM = 256
        HEADS = 4
        HEAD_DIM = DIM // HEADS
        MLP_HIDDEN = DIM * 3
        B, N = (8, 128)
        EPS = 1e-05

        def _layernorm(x, g, b):
            mu = jnp.mean(x, axis=-1, keepdims=True)
            var = jnp.mean(jnp.square(x - mu), axis=-1, keepdims=True)
            return (x - mu) * jax.lax.rsqrt(var + EPS) * g + b
        key = jax.random.key(seed)
        ks = jax.random.split(key, 8)
        s = 0.02
        return {'x': jax.random.normal(ks[0], (B, N, DIM), dtype=jnp.float32), 'w_qkv': jax.random.normal(ks[1], (DIM, 3 * DIM), dtype=jnp.float32) * s, 'b_qkv': jnp.zeros((3 * DIM,), dtype=jnp.float32), 'norm_g': jnp.ones((DIM,), dtype=jnp.float32), 'norm_b': jnp.zeros((DIM,), dtype=jnp.float32), 'w_fc1': jax.random.normal(ks[2], (DIM, MLP_HIDDEN), dtype=jnp.float32) * s, 'b_fc1': jnp.zeros((MLP_HIDDEN,), dtype=jnp.float32), 'w_fc2': jax.random.normal(ks[3], (MLP_HIDDEN, DIM), dtype=jnp.float32) * s, 'b_fc2': jnp.zeros((DIM,), dtype=jnp.float32)}
    _L0_mix_all = _L0_mix_setup()
    _L0_mix_in = {k: v for k, v in _L0_mix_all.items() if k in ('w_qkv', 'b_qkv', 'norm_g', 'norm_b', 'w_fc1', 'b_fc1', 'w_fc2', 'b_fc2')}
    del _L0_mix_all

    def _L0_ffn_setup():
        import jax, jax.numpy as jnp
        import numpy as np
        TOP_K = 2
        LN_EPS = 1e-05
        key = jax.random.key(seed)
        ks = jax.random.split(key, 8)
        B, S, D, E, H = (16, 1024, 256, 8, 1024)
        x = jax.random.normal(ks[0], (B, S, D), dtype=jnp.float32)
        Wr = jax.random.normal(ks[1], (D, E), dtype=jnp.float32) * 0.1
        br = jnp.zeros((E,), dtype=jnp.float32)
        ln_g = jnp.ones((E, D), dtype=jnp.float32)
        ln_b = jnp.zeros((E, D), dtype=jnp.float32)
        W1 = jax.random.normal(ks[2], (E, D, H), dtype=jnp.float32) * (1.0 / np.sqrt(D))
        b1 = jnp.zeros((E, H), dtype=jnp.float32)
        W2 = jax.random.normal(ks[3], (E, H, D), dtype=jnp.float32) * (1.0 / np.sqrt(H))
        b2 = jnp.zeros((E, D), dtype=jnp.float32)
        return {'x': x, 'Wr': Wr, 'br': br, 'ln_g': ln_g, 'ln_b': ln_b, 'W1': W1, 'b1': b1, 'W2': W2, 'b2': b2}
    _L0_ffn_all = _L0_ffn_setup()
    _L0_ffn_in = {k: v for k, v in _L0_ffn_all.items() if k in ('Wr', 'br', 'ln_g', 'ln_b', 'W1', 'b1', 'W2', 'b2')}
    del _L0_ffn_all
    return {'x': x, 'src': src, 'dst': dst, 'L0_gnn_W': _L0_gnn_in['W'], 'L0_gnn_b': _L0_gnn_in['b'], 'L0_gnn_gamma': _L0_gnn_in['gamma'], 'L0_gnn_beta': _L0_gnn_in['beta'], 'L0_mix_w_qkv': _L0_mix_in['w_qkv'], 'L0_mix_b_qkv': _L0_mix_in['b_qkv'], 'L0_mix_norm_g': _L0_mix_in['norm_g'], 'L0_mix_norm_b': _L0_mix_in['norm_b'], 'L0_mix_w_fc1': _L0_mix_in['w_fc1'], 'L0_mix_b_fc1': _L0_mix_in['b_fc1'], 'L0_mix_w_fc2': _L0_mix_in['w_fc2'], 'L0_mix_b_fc2': _L0_mix_in['b_fc2'], 'L0_ffn_Wr': _L0_ffn_in['Wr'], 'L0_ffn_br': _L0_ffn_in['br'], 'L0_ffn_ln_g': _L0_ffn_in['ln_g'], 'L0_ffn_ln_b': _L0_ffn_in['ln_b'], 'L0_ffn_W1': _L0_ffn_in['W1'], 'L0_ffn_b1': _L0_ffn_in['b1'], 'L0_ffn_W2': _L0_ffn_in['W2'], 'L0_ffn_b2': _L0_ffn_in['b2']}

def reference(x, src, dst, L0_gnn_W, L0_gnn_b, L0_gnn_gamma, L0_gnn_beta, L0_mix_w_qkv, L0_mix_b_qkv, L0_mix_norm_g, L0_mix_norm_b, L0_mix_w_fc1, L0_mix_b_fc1, L0_mix_w_fc2, L0_mix_b_fc2, L0_ffn_Wr, L0_ffn_br, L0_ffn_ln_g, L0_ffn_ln_b, L0_ffn_W1, L0_ffn_b1, L0_ffn_W2, L0_ffn_b2):
    import jax
    import jax.numpy as jnp

    def _L0_gnn_ref(x, edge_index, W, b, gamma, beta):
        import jax, jax.numpy as jnp
        import numpy as np
        N_NODES = 50000
        N_EDGES = 312500
        WIDTH = 256
        LN_EPS = 1e-05

        def gcn_conv(x, edge_index, W, b):
            n = x.shape[0]
            loops = jnp.arange(n, dtype=edge_index.dtype)
            src = jnp.concatenate([edge_index[0], loops])
            dst = jnp.concatenate([edge_index[1], loops])
            deg = jax.ops.segment_sum(jnp.ones_like(dst, dtype=x.dtype), dst, num_segments=n)
            dinv = jnp.where(deg > 0, jax.lax.rsqrt(deg), 0.0)
            norm = dinv[src] * dinv[dst]
            h = x @ W.T
            msgs = norm[:, None] * h[src]
            out = jax.ops.segment_sum(msgs, dst, num_segments=n)
            return out + b

        def layer_norm(x, gamma, beta):
            mu = jnp.mean(x, axis=-1, keepdims=True)
            var = jnp.mean(jnp.square(x - mu), axis=-1, keepdims=True)
            return (x - mu) * jax.lax.rsqrt(var + LN_EPS) * gamma + beta
        h = gcn_conv(x, edge_index, W, b)
        h = layer_norm(h, gamma, beta)
        h = jax.nn.relu(h)
        return h

    def _L0_mix_ref(x, w_qkv, b_qkv, norm_g, norm_b, w_fc1, b_fc1, w_fc2, b_fc2):
        import jax, jax.numpy as jnp
        import numpy as np
        DIM = 256
        HEADS = 4
        HEAD_DIM = DIM // HEADS
        MLP_HIDDEN = DIM * 3
        B, N = (8, 128)
        EPS = 1e-05

        def _layernorm(x, g, b):
            mu = jnp.mean(x, axis=-1, keepdims=True)
            var = jnp.mean(jnp.square(x - mu), axis=-1, keepdims=True)
            return (x - mu) * jax.lax.rsqrt(var + EPS) * g + b
        Bx, Nx, C = x.shape
        scale = HEAD_DIM ** (-0.5)
        qkv = (x @ w_qkv + b_qkv).reshape(Bx, Nx, 3, HEADS, HEAD_DIM)
        qkv = jnp.transpose(qkv, (2, 0, 3, 1, 4))
        q, k, v = (qkv[0], qkv[1], qkv[2])
        k = k * scale
        attn = jnp.einsum('bhnd,bhne->bhde', k, v)
        attn = jax.nn.softmax(attn, axis=-1)
        xf = jnp.einsum('bhde,bhne->bhnd', attn, q)
        xf = jnp.transpose(xf, (0, 2, 1, 3)).reshape(Bx, Nx, C)
        x = x + xf
        h = _layernorm(x, norm_g, norm_b)
        h = jax.nn.gelu(h @ w_fc1 + b_fc1, approximate=False) @ w_fc2 + b_fc2
        return x + h

    def _L0_ffn_ref(x, Wr, br, ln_g, ln_b, W1, b1, W2, b2):
        import jax, jax.numpy as jnp
        import numpy as np
        TOP_K = 2
        LN_EPS = 1e-05
        B, S, D = x.shape
        N = B * S
        xt = x.reshape(N, D)
        logits = xt @ Wr + br
        probs = jax.nn.softmax(logits, axis=-1)
        top_p, top_idx = jax.lax.top_k(probs, TOP_K)
        weights = top_p / top_p.sum(axis=-1, keepdims=True)
        mu = xt.mean(axis=-1, keepdims=True)
        var = ((xt - mu) ** 2).mean(axis=-1, keepdims=True)
        xn = (xt - mu) * jax.lax.rsqrt(var + LN_EPS)
        xe = xn[None, :, :] * ln_g[:, None, :] + ln_b[:, None, :]
        h = jax.nn.gelu(jnp.einsum('end,edh->enh', xe, W1) + b1[:, None, :], approximate=False)
        y = jnp.einsum('enh,ehd->end', h, W2) + b2[:, None, :]
        y_tok = jnp.transpose(y, (1, 0, 2))
        sel = jnp.take_along_axis(y_tok, top_idx[:, :, None], axis=1)
        out = (weights[:, :, None] * sel).sum(axis=1)
        return out.reshape(B, S, D)
    edge_index = jnp.stack([src, dst])
    xn = _layernorm(x, axis=-1)
    x = x + _L0_gnn_ref(xn, edge_index, L0_gnn_W, L0_gnn_b, L0_gnn_gamma, L0_gnn_beta) + _L0_mix_ref(xn[None], L0_mix_w_qkv, L0_mix_b_qkv, L0_mix_norm_g, L0_mix_norm_b, L0_mix_w_fc1, L0_mix_b_fc1, L0_mix_w_fc2, L0_mix_b_fc2)[0]
    x = x + _L0_ffn_ref(_layernorm(x, axis=-1)[None], L0_ffn_Wr, L0_ffn_br, L0_ffn_ln_g, L0_ffn_ln_b, L0_ffn_W1, L0_ffn_b1, L0_ffn_W2, L0_ffn_b2)[0]
    return x

_drawn_inputs = setup_inputs


def setup_inputs(seed=0):
    import zlib

    import numpy as np

    out = dict(_drawn_inputs(seed))
    spreads = {'L0_gnn_gamma': (1.0, 0.2),
     'L0_gnn_beta': (0.0, 0.1),
     'L0_mix_b_qkv': (0.0, 0.1),
     'L0_mix_norm_g': (1.0, 0.6),
     'L0_mix_norm_b': (0.0, 0.574),
     'L0_mix_b_fc1': (0.0, 0.39),
     'L0_mix_b_fc2': (0.0, 0.1),
     'L0_ffn_br': (0.0, 0.1),
     'L0_ffn_ln_g': (1.0, 0.2),
     'L0_ffn_ln_b': (0.0, 0.329),
     'L0_ffn_b1': (0.0, 0.323),
     'L0_ffn_b2': (0.0, 0.1)}
    factors = {'L0_gnn_b': 2.983}
    for name, (base, spread) in spreads.items():
        noise = np.random.default_rng([zlib.crc32(name.encode()), seed]).standard_normal(out[name].shape)
        drawn = base * np.exp(spread * noise) if base else spread * noise
        out[name] = jnp.asarray(drawn.astype(out[name].dtype))
    for name, factor in factors.items():
        out[name] = (out[name] * factor).astype(out[name].dtype)
    return out
```

```python
from contextlib import ExitStack, contextmanager

import concourse.bass as bass
from concourse import mybir

F32 = mybir.dt.float32
BF16 = mybir.dt.bfloat16
I32 = mybir.dt.int32
U32 = mybir.dt.uint32
ALU = mybir.AluOpType
ACT = mybir.ActivationFunctionType
AX_X = mybir.AxisListType.X
RMAX = bass.bass_isa.ReduceOp.max

P = 128
EPS = 1e-5
CHUNK = 5
GT = 8
SLOTS = 4


def held(eng, passed, sem, value):
    eng.wait_ge(sem, value)
    if not isinstance(value, int):
        eng.sem_inc(passed, 1)


class Chain:

    def __init__(self, eng, sem, passed):
        self.eng, self.sem, self.passed = eng, sem, passed
        self.base = 0
        self.n = 0

    def __call__(self, ins):
        ins.then_inc(self.sem, 1)
        self.n += 1
        held(self.eng, self.passed, self.sem, self.base + self.n)

    @contextmanager
    def loop(self, trips, per):
        start = self.n
        with self.eng.Fori(0, trips) as i:
            self.base, self.n = i * per + start, 0
            yield i
            assert self.n == per, (self.n, per)
        self.base, self.n = 0, start + trips * per


def gps_layer(nc, x, src, dst, gW, gb, ggamma, gbeta, wqkv, bqkv, ng, nb, wfc1, bfc1, wfc2, bfc2,
              Wr, br, lng, lnb, W1, b1, W2, b2, out):
    N, D = x.shape
    NE = src.shape[0]
    E, _, H = W1.shape
    HID = wfc1.shape[1]
    K = D // P
    KM = HID // P
    KH = H // P
    T = -(-N // P)
    LAST = N - (T - 1) * P
    NC = T // CHUNK
    G = -(-NE // (P * GT))
    EG = P * GT
    EL = NE - (G - 1) * EG
    EROW, EREM = EL // GT, EL % GT
    HI = 32
    PAD_DST = P * HI + P - 1
    TOPK = 2
    HD = 64
    SCALE = float(HD) ** -0.5
    W = TOPK * N // P + E
    WC = K * H + KH * D
    EARLY = 1
    assert T == NC * CHUNK and D == K * P and 2 * T + 2 == G and G % SLOTS == 0 and G // 2 == T + 1

    table = nc.dram_tensor("h_table", (T * P, D), F32).ap()
    slots = nc.dram_tensor("slot_rows", ((W + 1) * P, D), F32).ap()
    yrows = nc.dram_tensor("expert_rows", (W * P, D), F32).ap()

    with ExitStack() as ctx:
        ctx.enter_context(nc.allow_non_contiguous_dma("index lists of eight edges a partition"))

        def sb(name, shape, dt=F32):
            return ctx.enter_context(nc.sbuf_tensor(name, shape, dt))

        def sem(name):
            return ctx.enter_context(nc.semaphore(name))

        wall = sb("wall", [P, E * WC])
        acc = sb("acc", [P, T + 1, D])
        xn = sb("xn", [P, T, D])
        cursor = [EARLY * WC]

        def room(cols):
            a = cursor[0]
            cursor[0] += cols
            assert cursor[0] <= E * WC
            return wall[:, a:a + cols]

        ring = room(SLOTS * GT * D).rearrange("p (s c) -> p s c", s=SLOTS * GT)
        hot = [room(GT // 2 * P).rearrange("p (j n) -> p j n", j=GT // 2) for _ in range(2)]
        hot_lo = [room(GT * P // 2).bitcast(BF16).rearrange("p (j n) -> p j n", j=GT) for _ in range(2)]
        hot_hi = [room(GT * HI // 2).bitcast(BF16).rearrange("p (j n) -> p j n", j=GT) for _ in range(2)]
        wqkv_s = room(K * 3 * D).rearrange("p (k n) -> p k n", k=K)
        wfc1_s = room(K * HID).rearrange("p (k n) -> p k n", k=K)
        wfc2_s = room(KM * D).rearrange("p (k n) -> p k n", k=KM)
        gW_s = room(K * D).rearrange("p (k n) -> p k n", k=K)
        gWT = room(K * D).rearrange("p (k n) -> p k n", k=K)
        wqT = room(K * D).rearrange("p (k n) -> p k n", k=K)
        gram = room(K * D).rearrange("p (k n) -> p k n", k=K)
        xtv = room(K * D).rearrange("p (k n) -> p k n", k=K)
        wqa = room(K * D).rearrange("p (k n) -> p k n", k=K)
        xs = room(D)
        xT_s = room(D).rearrange("p (k n) -> p k n", k=K)
        hn_s = room(D)
        hnT_s = room(D).rearrange("p (k n) -> p k n", k=K)
        h1T_s = room(HID).rearrange("p (m n) -> p m n", m=KM)
        att = room(K * HD).rearrange("p (k n) -> p k n", k=K)
        atb = room(K * P).rearrange("p (k n) -> p k n", k=K)
        atT = room(K * P).rearrange("p (k n) -> p k n", k=K)
        dst_i = room(G * GT).bitcast(I32)
        tmp_i = room(G * GT).bitcast(I32)
        hi_f = room(G * GT)

        NV = 2 * K + KM + K + 2 * E * K
        vrow = room(P)
        VNG, VNB, VF1, VBQ, VLG, VLB = 0, K, 2 * K, 2 * K + KM, 3 * K + KM, 3 * K + KM + E * K
        vcol = sb("vcol", [P, NV])
        bqkv_s = room(3 * D)
        bfc2_s = room(D)
        srow = room(D)
        urow = room(D)
        bqa = room(D)

        ident = sb("ident", [P, P])
        iota_i = room(P).bitcast(I32)
        iotap_i = sb("iotap_i", [P, 1], I32)
        iota_f = sb("iota_f", [P, P])
        iota_b = sb("iota_b", [P, P], BF16)
        iotap = sb("iotap", [P, 1])
        before = sb("before", [P, P])
        ones = sb("ones", [P, P])
        zeros = room(512)
        gb_b = sb("gb_b", [P, D])
        gg_b = sb("gg_b", [P, D])
        gbe_b = sb("gbe_b", [P, D])
        wr_s = sb("wr_s", [P, K, E])
        br_s = sb("br_s", [1, E])
        src_i = room(G * GT).bitcast(I32)
        lo_f = room(G * GT).rearrange("p (g j) -> p g j", j=GT)
        lo_b = room(G * GT // 2).bitcast(BF16).rearrange("p (g j) -> p g j", j=GT)
        hi_b = room(G * GT // 2).bitcast(BF16).rearrange("p (g j) -> p g j", j=GT)
        dst_f = room(G * GT).rearrange("p (g j) -> p g j", j=GT)
        shifted = room(GT)
        idx_s = [sb(f"idx_s{k}", [P, GT], I32) for k in range(SLOTS)]
        gm = sb("gm", [P, 2, G])
        gall = sb("gall", [P, 2, G])
        blk_i = sb("blk_i", [P, G], I32)
        blk_f = sb("blk_f", [P, G])
        wide_f = sb("wide_f", [P, 1])
        wide_i = sb("wide_i", [P, 1], I32)
        mhi = sb("mhi", [P, G])
        mlo = sb("mlo", [P, G])
        scol = sb("scol", [P, K])
        dinv = sb("dinv", [P, T])
        st = sb("st", [P, T, 6])
        small = sb("small", [P, 4, T])
        mean = sb("mean", [P, T])
        var = sb("var", [P, T])
        std = sb("std", [P, T])
        rstd = sb("rstd", [P, T])
        x2s = sb("x2s", [P, CHUNK, D])
        xre = sb("xre", [P, CHUNK, D])
        x2T = sb("x2T", [P, K, P])
        lg = sb("lg", [P, T, E])
        pr = sb("pr", [P, T, E])
        m1 = sb("m1", [P, T, E])
        m2 = sb("m2", [P, T, E])
        r1 = sb("r1", [P, T])
        r2 = sb("r2", [P, T])
        w1c = sb("w1c", [P, T])
        w2c = sb("w2c", [P, T])
        mneg = sb("mneg", [P, K])
        msum = sb("msum", [P, K])
        valid = sb("valid", [P, 1])
        cnt = x2s[:, 0, 0:E * T].rearrange("p (e t) -> p e t", e=E)
        inc = x2s[:, 1, 0:E * T].rearrange("p (e t) -> p e t", e=E)
        pos = x2s[:, 2, 0:E * T].rearrange("p (t e) -> p t e", t=T)
        tmpr = x2s[:, 3, 0:E * T].rearrange("p (t e) -> p t e", t=T)
        tl = sb("tl", [P, 4, E])
        tl_i = sb("tl_i", [P, E], I32)
        pos_i = sb("pos_i", [P, TOPK, T], I32)
        tile_f = sb("tile_f", [P, W + 1])
        tile_e = sb("tile_e", [P, W + 1], I32)

        acc_flat = acc[:, :, :].rearrange("p t d -> p (t d)")
        c2 = [0]

        def late(cols):
            a = c2[0]
            c2[0] += cols
            assert c2[0] <= (T + 1) * D
            return acc_flat[:, a:a + cols]

        xe = late(D)
        xeT = late(D).rearrange("p (k n) -> p k n", k=K)
        b1t = late(H)
        b2t = late(2 * D).rearrange("p (s d) -> p s d", s=2)
        hpre = late(H)
        hact = late(H)
        hT = late(H).rearrange("p (m n) -> p m n", m=KH)
        ys = late(D)
        gcol = late(2 * K)

        y1 = wall[:, 0:T * D].rearrange("p (t d) -> p t d", t=T)
        y2 = wall[:, T * D:2 * T * D].rearrange("p (t d) -> p t d", t=T)

        bank = [ctx.enter_context(nc.psum_tensor(f"bank{i}", [P, 512], F32)) for i in range(8)]
        w1e = wall[:, :].rearrange("p (e c) -> p e c", e=E)

        passed = sem("passed")
        cleared = sem("cleared")
        iotas = sem("iotas")
        x_in = sem("x_in")
        edges_in = sem("edges_in")
        weights_in = sem("weights_in")
        vrows_in = sem("vrows_in")
        rows_in = sem("rows_in")
        bcast_in = sem("bcast_in")
        early_in = sem("early_in")
        late_in = sem("late_in")
        slots_zeroed = sem("slots_zeroed")
        dve_step = sem("dve_step")
        act_step = sem("act_step")
        consts = sem("consts")
        vcol_ps = sem("vcol_ps")
        vcol_ok = sem("vcol_ok")
        wT_ps = sem("wT_ps")
        wT_ok = sem("wT_ok")
        var_ready = sem("var_ready")
        std_ready = sem("std_ready")
        ln1_done = sem("ln1_done")
        onehot_made = sem("onehot_made")
        onehot_used = sem("onehot_used")
        xs_ready = sem("xs_ready")
        xT_ps = sem("xT_ps")
        xT_ready = sem("xT_ready")
        xs_used = sem("xs_used")
        h_ps = sem("h_ps")
        h_ready = sem("h_ready")
        hist_done = sem("hist_done")
        table_ready = sem("table_ready")
        table_stored = sem("table_stored")
        extremes = sem("extremes")
        extremes_all = sem("extremes_all")
        sm_pe = sem("attention_pe")
        sm_dve = sem("attention_dve")
        sm_act = sem("attention_act")
        idx_ready = sem("idx_ready")
        gathered = [sem(f"gathered{k}") for k in range(SLOTS)]
        groups_ready = sem("groups_ready")
        hot_ready = sem("hot_ready")
        halves_summed = sem("halves_summed")
        groups_added = sem("groups_added")
        windows_known = sem("windows_known")
        wide_reloaded = sem("wide_reloaded")
        wide_gathered = sem("wide_gathered")
        wide_idx = sem("wide_idx")
        wide_hot = sem("wide_hot")
        wide_summed = sem("wide_summed")
        wide_added = sem("wide_added")
        wide_shifted = sem("wide_shifted")
        aggregated = sem("aggregated")
        m1_ps = sem("m1_ps")
        m1_added = sem("m1_added")
        hn_ready = sem("hn_ready")
        hnT_ps = sem("hnT_ps")
        hnT_ready = sem("hnT_ready")
        fc1_ps = sem("fc1_ps")
        fc1_ready = sem("fc1_ready")
        fc2_ps = sem("fc2_ps")
        mix_added = sem("mix_added")
        xre_in = sem("xre_in")
        xre_used = sem("xre_used")
        x2_ready = sem("x2_ready")
        x2T_ps = sem("x2T_ps")
        x2T_ready = sem("x2T_ready")
        lg_ps = sem("lg_ps")
        lg_ready = sem("lg_ready")
        rt_dve = sem("routing_dve")
        rt_act = sem("routing_act")
        rt_pe = sem("routing_pe")
        pos_ready = sem("pos_ready")
        rows_routed = sem("rows_routed")
        xe_in = sem("xe_in")
        bias_in = sem("bias_in")
        xe_transposed = sem("xe_transposed")
        xeT_ready = sem("xeT_ready")
        up_done = sem("up_done")
        biased = sem("biased")
        hidden = sem("hidden")
        hT_ps = sem("hT_ps")
        hT_act = sem("hT_act")
        hT_dve = sem("hT_dve")
        down_done = sem("down_done")
        y_ready = sem("y_ready")
        y_stored = sem("y_stored")
        picked = [sem(f"picked{c}") for c in range(NC)]
        out_ready = sem("out_ready")
        out_stored = sem("out_stored")

        NW = 5
        block = ctx.enter_context(nc.Block())

        @block.sync
        def _(sp):
            sp.wait_ge(cleared, 4)
            sp.dma_start(xn[:, 0:T - 1, :], x[0:(T - 1) * P, :].rearrange("(t p) d -> p t d", p=P)).then_inc(x_in, 16)
            sp.dma_start(xn[0:LAST, T - 1, :], x[(T - 1) * P:N, :]).then_inc(x_in, 16)
            for buf, vec in ((dst_i, dst), (src_i[:, :], src)):
                v = buf.rearrange("p (g j) -> p g j", j=GT)
                sp.dma_start(v[:, 0:G - 1, :], vec[0:(G - 1) * EG].rearrange("(g p j) -> p g j", p=P, j=GT)).then_inc(edges_in, 16)
                sp.dma_start(v[0:EROW, G - 1, :], vec[(G - 1) * EG:(G - 1) * EG + EROW * GT].rearrange("(p j) -> p j", j=GT)).then_inc(edges_in, 16)
                sp.dma_start(v[EROW:EROW + 1, G - 1, 0:EREM], vec[NE - EREM:NE].rearrange("(p j) -> p j", p=1)).then_inc(edges_in, 16)
            sp.dma_start(gW_s, gW.rearrange("(k p) n -> p k n", p=P)).then_inc(weights_in, 16)
            sp.dma_start(wqkv_s, wqkv.rearrange("(k p) n -> p k n", p=P)).then_inc(weights_in, 16)
            sp.dma_start(wfc1_s, wfc1.rearrange("(k p) n -> p k n", p=P)).then_inc(weights_in, 16)
            sp.dma_start(wfc2_s, wfc2.rearrange("(k p) n -> p k n", p=P)).then_inc(weights_in, 16)
            sp.dma_start(wr_s[:, :, :], Wr.rearrange("(k p) n -> p k n", p=P)).then_inc(weights_in, 16)

            def load_expert(e, done):
                sp.dma_start(w1e[:, e, 0:K * H].rearrange("p (k n) -> p k n", k=K),
                             W1[e].rearrange("(k p) n -> p k n", p=P)).then_inc(done, 16)
                sp.dma_start(w1e[:, e, K * H:WC].rearrange("p (k n) -> p k n", k=KH),
                             W2[e].rearrange("(k p) n -> p k n", p=P)).then_inc(done, 16)

            for e in range(EARLY):
                load_expert(e, early_in)
            sp.wait_ge(consts, 1)
            sp.dma_start(slots.rearrange("(w p) d -> p w d", p=P),
                         zeros[:, 0:D].unsqueeze(1).to_broadcast([P, W + 1, D])).then_inc(slots_zeroed, 16)
            for c in range(NC):
                sp.wait_ge(table_ready, c + 1)
                sp.dma_start(table[c * CHUNK * P:(c + 1) * CHUNK * P, :].rearrange("(t p) d -> p t d", p=P),
                             acc[:, c * CHUNK:(c + 1) * CHUNK, :]).then_inc(table_stored, 16)
            sp.wait_ge(aggregated, 1)
            sp.wait_ge(mix_added, T + 1)
            sp.wait_ge(slots_zeroed, 16)
            for e in range(EARLY, E):
                load_expert(e, late_in)
            for c in range(NC):
                if c:
                    sp.wait_ge(xre_used, c)
                a = c * CHUNK
                n = CHUNK if c < NC - 1 else CHUNK - 1
                sp.dma_start(xre[:, 0:n, :], x[a * P:(a + n) * P, :].rearrange("(t p) d -> p t d", p=P)).then_inc(xre_in, 16)
                if c == NC - 1:
                    sp.dma_start(xre[0:LAST, CHUNK - 1, :], x[(T - 1) * P:N, :]).then_inc(xre_in, 16)
            sp.wait_ge(rows_routed, 16 * TOPK * T)
            sp.sem_inc(xe_transposed, 1)
            sp.sem_inc(biased, 1)
            with sp.Fori(0, W) as w:
                held(sp, passed, xe_transposed, w + 1)
                sp.dma_start(xe, slots[bass.ts(w, P), :]).then_inc(xe_in, 16)
                e = sp.value_load(tile_e[0:1, bass.ds(w, 1)], min_val=0, max_val=E - 1)
                held(sp, passed, biased, w + 1)
                sp.dma_start(b1t, b1[e, :].partition_broadcast(P)).then_inc(bias_in, 16)
                held(sp, passed, y_ready, w + 1)
                sp.dma_start(b2t[:, w % 2, :], b2[e, :].partition_broadcast(P)).then_inc(bias_in, 16)
            sp.wait_ge(xe_transposed, W + 1)
            sp.dma_start(xe, slots[W * P:(W + 1) * P, :]).then_inc(xe_in, 16)
            for c in range(NC):
                a = c * CHUNK
                n = CHUNK if c < NC - 1 else CHUNK - 1
                sp.wait_ge(out_ready, c + 1)
                sp.dma_start(out[a * P:(a + n) * P, :].rearrange("(t p) d -> p t d", p=P), xn[:, a:a + n, :]).then_inc(out_stored, 16)
            sp.dma_start(out[(T - 1) * P:N, :], xn[0:LAST, T - 1, :]).then_inc(out_stored, 16)
            sp.wait_ge(out_stored, 16 * (NC + 1))

        @block.gpsimd
        def _(pool):
            g = nc.gpsimd
            g.memset(xn[:, T - 1, :], 0.0).then_inc(cleared, 1)
            g.memset(dst_i[:, (G - 1) * GT:], PAD_DST).then_inc(cleared, 1)
            g.memset(src_i[:, (G - 1) * GT:], 0).then_inc(cleared, 1)
            g.memset(xre[:, CHUNK - 1, :], 0.0).then_inc(cleared, 1)
            g.iota(iota_i, pattern=[[1, P]], base=0, channel_multiplier=0).then_inc(iotas, 1)
            g.iota(iotap_i[:, :], pattern=[[0, 1]], base=0, channel_multiplier=1).then_inc(iotas, 1)
            g.memset(acc[:, T, :], 0.0).then_inc(cleared, 1)
            pool.wait_ge(extremes, 1)
            g.partition_all_reduce(gall[:, :, :].rearrange("p a g -> p (a g)"), gm[:, :, :].rearrange("p a g -> p (a g)"), P, RMAX).then_inc(extremes_all, 1)
            pool.sem_inc(halves_summed, 2 * SLOTS)
            pool.wait_ge(edges_in, 96)
            pool.wait_ge(table_stored, 16 * NC)
            with pool.Fori(0, G // SLOTS) as r:
                for k in range(SLOTS):
                    held(pool, passed, halves_summed, 2 * SLOTS * r + 2 * k + 2)
                    g.tensor_copy(idx_s[k][:, :], src_i[:, bass.ds((SLOTS * r + k) * GT, GT)]).then_inc(idx_ready, 1)
                    held(pool, passed, idx_ready, SLOTS * r + k + 1)
                    for j in range(GT):
                        g.indirect_dma_start(ring[:, k * GT + j, :], None, table,
                                             bass.IndirectOffsetOnAxis(ap=idx_s[k][:, j:j + 1].bitcast(U32), axis=0)).then_inc(gathered[k], 16)
                    if k >= 1:
                        pool.wait_ge(gathered[k - 1], (r + 1) * (16 * GT))
                        pool.sem_inc(groups_ready, 1)
                pool.wait_ge(gathered[SLOTS - 1], (r + 1) * (16 * GT))
                pool.sem_inc(groups_ready, 1)
            pool.wait_ge(windows_known, 1)
            wide = pool.value_load(wide_i[0:1, 0:1], min_val=0, max_val=1)
            with pool.If(wide):
                pool.wait_ge(groups_added, G + 1)
                g.dma_start(acc[:, 0:T, :], table.rearrange("(t p) d -> p t d", p=P)).then_inc(wide_reloaded, 16)
                pool.sem_inc(wide_summed, 1)
                with pool.Fori(0, G) as q:
                    held(pool, passed, wide_summed, q * T + 1)
                    g.tensor_copy(idx_s[0][:, :], src_i[:, bass.ds(q * GT, GT)]).then_inc(wide_idx, 1)
                    held(pool, passed, wide_idx, q + 1)
                    for j in range(GT):
                        g.indirect_dma_start(ring[:, j, :], None, table,
                                             bass.IndirectOffsetOnAxis(ap=idx_s[0][:, j:j + 1].bitcast(U32), axis=0)).then_inc(wide_gathered, 16)
            pool.wait_ge(pos_ready, 1)
            pool.wait_ge(slots_zeroed, 16)
            for t in range(T):
                n = P if t < T - 1 else LAST
                for j in range(TOPK):
                    g.indirect_dma_start(slots, bass.IndirectOffsetOnAxis(ap=pos_i[0:n, j, t:t + 1].bitcast(U32), axis=0),
                                         acc[0:n, t, :], None).then_inc(rows_routed, 16)
            with pool.Fori(0, W) as w:
                held(pool, passed, y_ready, w + (TOPK + 1))
                g.dma_start(yrows[bass.ts(w, P), :], ys).then_inc(y_stored, 16)
            pool.wait_ge(y_stored, 16 * W)
            for t in range(T):
                n = P if t < T - 1 else LAST
                for j, y in enumerate((y1, y2)):
                    g.indirect_dma_start(y[0:n, t, :], None, yrows,
                                         bass.IndirectOffsetOnAxis(ap=pos_i[0:n, j, t:t + 1].bitcast(U32), axis=0)).then_inc(picked[t // CHUNK], 16)

        @block.scalar
        def _(act):
            s = nc.scalar
            for r, n, vec in ((VNG, K, ng), (VNB, K, nb), (VF1, KM, bfc1), (VBQ, K, bqkv[0:D])):
                act.dma_start(vrow[r:r + n, :], vec.rearrange("(r p) -> r p", p=P)).then_inc(vrows_in, 16)
            for r, mat in ((VLG, lng), (VLB, lnb)):
                act.dma_start(vrow[r:r + E * K, :], mat.rearrange("e (k p) -> (e k) p", p=P)).then_inc(vrows_in, 16)
            act.dma_start(bqkv_s[0:1, :], bqkv.unsqueeze(0)).then_inc(rows_in, 16)
            act.dma_start(bfc2_s[0:1, :], bfc2.unsqueeze(0)).then_inc(rows_in, 16)
            act.dma_start(br_s[:, :], br.unsqueeze(0)).then_inc(rows_in, 16)
            for buf, vec in ((gb_b, gb), (gg_b, ggamma), (gbe_b, gbeta)):
                act.dma_start(buf[:, :], vec.partition_broadcast(P)).then_inc(bcast_in, 16)
            act.wait_ge(vcol_ps, 1)
            s.activation(vcol[:, :], bank[7][:, 0:NV], ACT.Copy).then_inc(vcol_ok, 1)
            act.wait_ge(wT_ps, 1)
            s.activation(gWT, bank[6][:, :].rearrange("p (k n) -> p k n", k=K), ACT.Copy).then_inc(wT_ok, 1)
            act.wait_ge(wT_ps, 2)
            s.activation(wqT, bank[7][:, :].rearrange("p (k n) -> p k n", k=K), ACT.Copy).then_inc(wT_ok, 1)
            for c in range(NC):
                act.wait_ge(var_ready, c + 1)
                s.activation(std[:, c * CHUNK:(c + 1) * CHUNK], var[:, c * CHUNK:(c + 1) * CHUNK], ACT.Sqrt).then_inc(std_ready, 1)
            act.wait_ge(ln1_done, NC)
            act.wait_ge(cleared, 5)
            act.sem_inc(xs_used, 1)
            with act.Fori(0, T) as t:
                held(act, passed, xs_used, t + 1)
                s.activation(xs, xn[:, t, :], ACT.Copy).then_inc(xs_ready, 1)
                held(act, passed, xT_ps, t + 1)
                s.activation(xT_s, bank[2][:, 0:D].rearrange("p (k n) -> p k n", k=K), ACT.Copy).then_inc(xT_ready, 1)
                held(act, passed, h_ps, t + 1)
                s.activation(acc[:, t, :], bank[4][:, 0:D], ACT.Copy).then_inc(h_ready, 1)
            act.wait_ge(var_ready, NC + 1)
            s.activation(std[:, :], var[:, :], ACT.Sqrt).then_inc(std_ready, 1)
            act.wait_ge(sm_pe, 1)
            s.activation(srow[0:1, :], bank[6][0:1, 0:D], ACT.Copy).then_inc(sm_act, 1)
            act.wait_ge(sm_pe, 3)
            s.activation(xtv, bank[7][:, :].rearrange("p (k n) -> p k n", k=K), ACT.Copy).then_inc(sm_act, 1)
            act.wait_ge(sm_dve, 3)
            for k in range(K):
                s.activation(atb[:, k, 0:HD], att[:, k, :], ACT.Exp, bias=mneg[:, k:k + 1], accum_out=msum[:, k:k + 1]).then_inc(sm_act, 1)
            act.wait_ge(sm_pe, 5)
            s.activation(atT, bank[6][:, 0:K * P].rearrange("p (k n) -> p k n", k=K), ACT.Copy).then_inc(sm_act, 1)
            act.wait_ge(sm_pe, 6)
            s.activation(wqa, bank[7][:, :].rearrange("p (k n) -> p k n", k=K), ACT.Copy).then_inc(sm_act, 1)
            act.wait_ge(sm_pe, 7)
            s.activation(bqa[0:1, :], bank[6][0:1, 0:D], ACT.Copy).then_inc(sm_act, 1)
            act.wait_ge(xs_used, T + 1)
            with act.Fori(0, T) as t:
                s.activation(xs, xn[:, t, :], ACT.Copy).then_inc(xs_ready, 1)
                held(act, passed, xT_ps, t + (T + 1))
                s.activation(xT_s, bank[2][:, 0:D].rearrange("p (k n) -> p k n", k=K), ACT.Copy).then_inc(xT_ready, 1)
            act.wait_ge(var_ready, NC + 2)
            s.activation(std[:, :], var[:, :], ACT.Sqrt).then_inc(std_ready, 1)
            with act.Fori(0, T) as t:
                held(act, passed, hnT_ps, t + 1)
                for k in range(K):
                    ins = s.activation(hnT_s[:, k, :], bank[4][:, k * P:(k + 1) * P], ACT.Identity,
                                       bias=vcol[:, VNB + k:VNB + k + 1], scale=vcol[:, VNG + k:VNG + k + 1])
                ins.then_inc(hnT_ready, 1)
                held(act, passed, fc1_ps, t + 1)
                for m in range(KM):
                    ins = s.activation(h1T_s[:, m, :], bank[2 + m // 4][:, m % 4 * P:(m % 4 + 1) * P], ACT.Gelu,
                                       bias=vcol[:, VF1 + m:VF1 + m + 1])
                ins.then_inc(fc1_ready, 1)
            for c in range(NC):
                for b in range(3):
                    act.wait_ge(var_ready, NC + 3 + 3 * c + b)
                    s.activation(std[:, 0:CHUNK], var[:, 0:CHUNK], ACT.Sqrt).then_inc(std_ready, 1)
                for u in range(CHUNK):
                    t = c * CHUNK + u
                    act.wait_ge(x2T_ps, t + 1)
                    s.activation(x2T[:, :, :], bank[2][:, 0:D].rearrange("p (k n) -> p k n", k=K), ACT.Copy).then_inc(x2T_ready, 1)
                    act.wait_ge(lg_ps, t + 1)
                    s.activation(lg[:, t, :], bank[4][:, 0:E], ACT.Copy).then_inc(lg_ready, 1)
            act.wait_ge(rt_dve, 1)
            s.activation(pr[:, :, :], lg[:, :, :], ACT.Exp).then_inc(rt_act, 1)
            act.wait_ge(rows_routed, 16 * TOPK * T)
            act.wait_ge(biased, 2)
            s.activation(hact, hpre, ACT.Gelu).then_inc(hidden, 1)
            half = KH // 2
            hTv = hT[:, 0:half, :]
            with act.Fori(1, W) as w:
                held(act, passed, hT_ps, w)
                s.activation(hTv, bank[2][:, :].rearrange("p (m n) -> p m n", m=half), ACT.Copy).then_inc(hT_act, 1)
                held(act, passed, biased, w + 2)
                s.activation(hact, hpre, ACT.Gelu).then_inc(hidden, 1)
            act.wait_ge(hT_ps, W)
            s.activation(hTv, bank[2][:, :].rearrange("p (m n) -> p m n", m=half), ACT.Copy).then_inc(hT_act, 1)

        @block.tensor
        def _(pe):
            t_ = nc.tensor
            mm = t_.matmul

            def blocks(bk, n=K):
                return bank[bk][:, 0:n * P].rearrange("p (k n) -> p k n", k=n)

            pe.wait_ge(consts, 1)
            pe.wait_ge(vrows_in, 96)
            t_.transpose(bank[7][:, 0:NV], vrow[0:NV, :], ident[0:NV, 0:NV]).then_inc(vcol_ps, 1)
            pe.wait_ge(weights_in, 80)
            for k in range(K):
                for o in range(K):
                    ins = t_.transpose(bank[6][:, k * D + o * P:k * D + (o + 1) * P], gW_s[:, o, k * P:(k + 1) * P], ident[:, :])
            ins.then_inc(wT_ps, 1)
            pe.wait_ge(vcol_ok, 1)
            for q in range(K):
                for k in range(K):
                    ins = t_.transpose(bank[7][:, q * D + k * P:q * D + (k + 1) * P], wqkv_s[:, k, q * P:(q + 1) * P], ident[:, :])
            ins.then_inc(wT_ps, 1)
            pe.wait_ge(wT_ok, 2)

            for b in range(2):
                mm(bank[b][:, :], zeros[:, 0:P], zeros[:, :], start=True, stop=False)
            pe.sem_inc(h_ready, 1)

            def histogram(b):
                for h in range(2):
                    held(pe, passed, onehot_made, 2 * b + h + 1)
                    for j in range(GT):
                        ins = mm(bank[1][:, HI:2 * HI], hot_lo[h][:, j, :], hot_hi[h][:, j, :], start=False, stop=False, skip_group_check=True)
                    ins.then_inc(onehot_used, 1)

            with pe.Fori(0, T) as t:
                held(pe, passed, xs_ready, t + 1)
                for k in range(K):
                    ins = t_.transpose(bank[2][:, k * P:(k + 1) * P], xs[:, k * P:(k + 1) * P], ident[:, :])
                ins.then_inc(xT_ps, 1)
                histogram(t)
                for k in range(K):
                    mm(bank[0][:, k * D:(k + 1) * D], xs[:, k * P:(k + 1) * P], xs, start=False, stop=False, skip_group_check=True)
                    ins = mm(bank[1][:, k:k + 1], xs[:, k * P:(k + 1) * P], ones[:, 0:1], start=False, stop=False, skip_group_check=True)
                ins.then_inc(xs_used, 1)
                held(pe, passed, xT_ready, t + 1)
                held(pe, passed, h_ready, t + 1)
                for k in range(K):
                    ins = mm(bank[4][:, 0:D], xT_s[:, k, :], gWT[:, k, :], start=(k == 0), stop=(k == K - 1))
                ins.then_inc(h_ps, 1)
            histogram(T)
            for b in range(2):
                ins = mm(bank[b][:, :], zeros[:, 0:P], zeros[:, :], start=False, stop=True)
            ins.then_inc(hist_done, 1)

            pe.wait_ge(rows_in, 48)
            pe.wait_ge(sm_dve, 1)
            for k in range(K):
                ins = mm(bank[6][0:1, k * P:(k + 1) * P], scol[:, k:k + 1], ident[:, :], start=True, stop=True)
            ins.then_inc(sm_pe, 1)
            for k in range(K):
                ins = mm(bank[5][0:1, 0:D], scol[:, k:k + 1], wqkv_s[:, k, 2 * D:3 * D], start=(k == 0), stop=(k == K - 1))
            ins.then_inc(sm_pe, 1)
            pe.wait_ge(sm_act, 1)
            for k in range(K):
                for j in range(K):
                    mm(bank[7][:, k * D:(k + 1) * D], gram[:, j, k * P:(k + 1) * P], wqkv_s[:, j, 2 * D:3 * D], start=(j == 0), stop=False)
                ins = mm(bank[7][:, k * D:(k + 1) * D], srow[0:1, k * P:(k + 1) * P], bqkv_s[0:1, 2 * D:3 * D], start=False, stop=True)
            ins.then_inc(sm_pe, 1)
            pe.wait_ge(sm_act, 2)
            pe.wait_ge(sm_dve, 2)
            for q in range(K):
                a = slice(q * P, (q + 1) * P)
                for k in range(K):
                    mm(bank[6][:, a], wqkv_s[:, k, D + q * P:D + (q + 1) * P], xtv[:, k, a], start=(k == 0), stop=False)
                ins = mm(bank[6][:, a], bqkv_s[0:1, D + q * P:D + (q + 1) * P], urow[0:1, a], start=False, stop=True)
            ins.then_inc(sm_pe, 1)
            pe.wait_ge(sm_dve, 4)
            for q in range(K):
                ins = t_.transpose(bank[6][:, q * P:(q + 1) * P], atb[:, q, :], ident[:, :])
            ins.then_inc(sm_pe, 1)
            pe.wait_ge(sm_act, 5)
            for k in range(K):
                for q in range(K):
                    ins = mm(bank[7][:, k * D + q * P:k * D + (q + 1) * P], wqT[:, q, k * P:(k + 1) * P], atT[:, q, :], start=True, stop=True)
            ins.then_inc(sm_pe, 1)
            for q in range(K):
                ins = mm(bank[6][0:1, q * P:(q + 1) * P], vcol[:, VBQ + q:VBQ + q + 1], atT[:, q, :], start=True, stop=True)
            ins.then_inc(sm_pe, 1)
            pe.wait_ge(sm_act, 7)

            def group(g):
                held(pe, passed, groups_ready, g + 1)
                held(pe, passed, groups_added, g + 1)
                half = GT // 2
                for h in range(2):
                    held(pe, passed, hot_ready, 2 * g + h + 1)
                    for j in range(half):
                        ins = mm(bank[0][:, 0:D], hot[h][:, j, :], ring[:, g % SLOTS * GT + (h * half + j), :],
                                 start=(h == 0 and j == 0), stop=(h == 1 and j == half - 1))
                    ins.then_inc(halves_summed, 1)

            pe.sem_inc(m1_added, 1)
            pe.sem_inc(mix_added, 1)
            with pe.Fori(0, T) as t:
                held(pe, passed, xs_ready, t + (T + 1))
                for k in range(K):
                    ins = t_.transpose(bank[2][:, k * P:(k + 1) * P], xs[:, k * P:(k + 1) * P], ident[:, :])
                ins.then_inc(xT_ps, 1)
                group(t)
                held(pe, passed, xT_ready, t + (T + 1))
                held(pe, passed, m1_added, t + 1)
                for k in range(K):
                    mm(bank[5][:, 0:D], xT_s[:, k, :], wqa[:, k, :], start=(k == 0), stop=False)
                mm(bank[5][:, 0:D], ones[0:1, :], bqa[0:1, :], start=False, stop=True).then_inc(m1_ps, 1)
            with pe.Fori(0, T) as t:
                held(pe, passed, hn_ready, t + 1)
                for k in range(K):
                    ins = t_.transpose(bank[4][:, k * P:(k + 1) * P], hn_s[:, k * P:(k + 1) * P], ident[:, :])
                ins.then_inc(hnT_ps, 1)
                held(pe, passed, hnT_ready, t + 1)
                for m in range(KM):
                    for k in range(K):
                        ins = mm(bank[2 + m // 4][:, m % 4 * P:(m % 4 + 1) * P], wfc1_s[:, k, m * P:(m + 1) * P], hnT_s[:, k, :],
                                 start=(k == 0), stop=(k == K - 1))
                ins.then_inc(fc1_ps, 1)
                group(t + T)
                held(pe, passed, fc1_ready, t + 1)
                held(pe, passed, mix_added, t + 1)
                for m in range(KM):
                    mm(bank[5][:, 0:D], h1T_s[:, m, :], wfc2_s[:, m, :], start=(m == 0), stop=False)
                mm(bank[5][:, 0:D], ones[0:1, :], bfc2_s[0:1, :], start=False, stop=True).then_inc(fc2_ps, 1)
            group(G - 2)
            group(G - 1)
            pe.wait_ge(windows_known, 1)
            wide = pe.value_load(wide_i[0:1, 0:1], min_val=0, max_val=1)
            with pe.If(wide):
                pe.sem_inc(wide_added, 1)
                with pe.Fori(0, G) as q:
                    held(pe, passed, wide_gathered, q * (16 * GT) + 16 * GT)
                    with pe.Fori(0, T) as b:
                        n = q * T + b
                        held(pe, passed, wide_hot, n + 1)
                        held(pe, passed, wide_added, n + 1)
                        for j in range(GT):
                            ins = mm(bank[0][:, 0:D], hot[j // (GT // 2)][:, j % (GT // 2), :], ring[:, j, :],
                                     start=(j == 0), stop=(j == GT - 1))
                        ins.then_inc(wide_summed, 1)

            for t in range(T):
                c, u = divmod(t, CHUNK)
                pe.wait_ge(x2_ready, c + 1)
                for k in range(K):
                    ins = t_.transpose(bank[2][:, k * P:(k + 1) * P], x2s[:, u, k * P:(k + 1) * P], ident[:, :])
                ins.then_inc(x2T_ps, 1)
                pe.wait_ge(x2T_ready, t + 1)
                if t:
                    pe.wait_ge(lg_ready, t)
                for k in range(K):
                    mm(bank[4][:, 0:E], x2T[:, k, :], wr_s[:, k, :], start=(k == 0), stop=False)
                mm(bank[4][:, 0:E], ones[0:1, :], br_s[:, :], start=False, stop=True).then_inc(lg_ps, 1)
            pe.wait_ge(rt_dve, 2)
            taken = tmpr.rearrange("p t e -> p (t e)")
            mm(bank[2][:, 0:T * E], before[:, :], taken, start=True, stop=True).then_inc(rt_pe, 1)
            mm(bank[3][:, 0:T * E], ones[:, :], taken, start=True, stop=True).then_inc(rt_pe, 1)

            def transpose_rows(w):
                held(pe, passed, xe_in, 16 * w + 16)
                for k in range(K):
                    ins = t_.transpose(bank[6][:, k * P:(k + 1) * P], xe[:, k * P:(k + 1) * P], ident[:, :])
                ins.then_inc(xe_transposed, 1)

            def up(w):
                e = pe.value_load(tile_e[0:1, bass.ds(w, 1)], min_val=0, max_val=E - 1)
                held(pe, passed, xeT_ready, w + 1)
                held(pe, passed, biased, w + 1)
                for k in range(K):
                    for q in range(2):
                        ins = mm(bank[q][:, :], xeT[:, k, :], w1e[:, e, k * H + q * 512:k * H + (q + 1) * 512], start=(k == 0), stop=(k == K - 1))
                ins.then_inc(up_done, 1)

            def transpose_hidden(w):
                held(pe, passed, hidden, w + 1)
                for m in range(KH):
                    ins = t_.transpose(bank[2 + m // 4][:, m % 4 * P:(m % 4 + 1) * P], hact[:, m * P:(m + 1) * P], ident[:, :])
                ins.then_inc(hT_ps, 1)

            def down(w):
                e = pe.value_load(tile_e[0:1, bass.ds(w, 1)], min_val=0, max_val=E - 1)
                held(pe, passed, hT_act, w + 1)
                held(pe, passed, hT_dve, w + 1)
                held(pe, passed, y_ready, w + TOPK)
                for m in range(KH):
                    ins = mm(bank[7][:, 0:D], hT[:, m, :], w1e[:, e, K * H + m * D:K * H + (m + 1) * D], start=(m == 0), stop=(m == KH - 1))
                ins.then_inc(down_done, 1)

            pe.wait_ge(early_in, 32 * EARLY)
            pe.wait_ge(late_in, 32 * (E - EARLY))
            transpose_rows(0)
            up(0)
            transpose_rows(1)
            with pe.Fori(0, W - 1) as i:
                transpose_hidden(i)
                up(i + 1)
                transpose_rows(i + 2)
                down(i)
            transpose_hidden(W - 1)
            down(W - 1)

        @block.vector
        def _(dve):
            v = nc.vector
            step = Chain(dve, dve_step, passed)
            dve.wait_ge(iotas, 2)
            v.tensor_copy(iota_f[:, :], iota_i)
            v.tensor_copy(iota_b[:, :], iota_i)
            v.memset(ones[:, :], 1.0)
            v.memset(zeros[:, :], 0.0)
            step(v.tensor_copy(iotap[:, :], iotap_i[:, :]))
            v.tensor_scalar(valid[:, :], iotap[:, :], float(LAST), None, ALU.is_lt)
            v.tensor_scalar(before[:, :], iota_f[:, :], iotap[:, :], None, ALU.is_gt)
            v.tensor_scalar(ident[:, :], iota_f[:, :], iotap[:, :], None, ALU.is_equal).then_inc(consts, 1)

            def statistics(n, inv_n=1.0 / D):
                me, ve, mo, vo = (st[:, 0:n, q] for q in (1, 2, 4, 5))
                v.tensor_tensor(small[:, 0, 0:n], me, mo, ALU.add)
                v.tensor_tensor(small[:, 1, 0:n], me, mo, ALU.subtract)
                step(v.tensor_tensor(small[:, 2, 0:n], ve, vo, ALU.add))
                v.tensor_scalar(mean[:, 0:n], small[:, 0, 0:n], 0.5, None, ALU.mult)
                v.scalar_tensor_tensor(small[:, 3, 0:n], small[:, 1, 0:n], 0.25, small[:, 1, 0:n], ALU.mult, ALU.mult)
                step(v.tensor_scalar(small[:, 2, 0:n], small[:, 2, 0:n], inv_n, EPS, ALU.mult, ALU.add))
                v.tensor_tensor(var[:, 0:n], small[:, 2, 0:n], small[:, 3, 0:n], ALU.add).then_inc(var_ready, 1)

            def normalise(dest, source, n):
                for u in range(n):
                    ins = v.tensor_scalar(dest[:, u, :], source[:, u, :], mean[:, u:u + 1], rstd[:, u:u + 1],
                                          ALU.subtract, ALU.mult)
                return ins

            dve.wait_ge(edges_in, 96)
            lo3 = lo_f[:, :, :].rearrange("p g j -> p (g j)")
            step(v.tensor_scalar(tmp_i, dst_i, P - 1, None, ALU.bitwise_and))
            v.tensor_copy(lo3, tmp_i)
            step(v.tensor_copy(dst_f[:, :, :].rearrange("p g j -> p (g j)"), dst_i))
            step(v.tensor_scalar(tmp_i, dst_i, 7, None, ALU.logical_shift_right))
            step(v.tensor_copy(hi_f, tmp_i))
            v.tensor_copy(hi_b[:, :, :].rearrange("p g j -> p (g j)"), hi_f)
            step(v.tensor_scalar(hi_f, hi_f, float(T), float(P), ALU.is_ge, ALU.mult))
            step(v.tensor_tensor(lo3, lo3, hi_f, ALU.add))
            v.tensor_copy(lo_b[:, :, :].rearrange("p g j -> p (g j)"), lo3)
            step(v.tensor_reduce(gm[:, 0, :], dst_f[:, :, :], AX_X, ALU.min))
            v.tensor_scalar(gm[:, 0, :], gm[:, 0, :], -1.0, None, ALU.mult)
            step(v.tensor_scalar(hi_f, dst_f[:, :, :].rearrange("p g j -> p (g j)"), float(N), None, ALU.is_lt))
            step(v.tensor_tensor(hi_f, hi_f, dst_f[:, :, :].rearrange("p g j -> p (g j)"), ALU.mult))
            v.tensor_reduce(gm[:, 1, :], hi_f.rearrange("p (g j) -> p g j", j=GT), AX_X, ALU.max).then_inc(extremes, 1)

            dve.wait_ge(x_in, 32)
            for c in range(NC):
                xc = xn[:, c * CHUNK:(c + 1) * CHUNK, :]
                for u in range(CHUNK):
                    ins = v.bn_stats(st[:, u, :], xc[:, u, :])
                step(ins)
                me, ve, mo, vo = (st[:, 0:CHUNK, q] for q in (1, 2, 4, 5))
                n = CHUNK
                vc = var[:, c * n:(c + 1) * n]
                v.tensor_tensor(small[:, 0, 0:n], me, mo, ALU.add)
                v.tensor_tensor(small[:, 1, 0:n], me, mo, ALU.subtract)
                step(v.tensor_tensor(small[:, 2, 0:n], ve, vo, ALU.add))
                v.tensor_scalar(mean[:, 0:n], small[:, 0, 0:n], 0.5, None, ALU.mult)
                v.scalar_tensor_tensor(small[:, 3, 0:n], small[:, 1, 0:n], 0.25, small[:, 1, 0:n], ALU.mult, ALU.mult)
                step(v.tensor_scalar(small[:, 2, 0:n], small[:, 2, 0:n], 1.0 / D, EPS, ALU.mult, ALU.add))
                v.tensor_tensor(vc, small[:, 2, 0:n], small[:, 3, 0:n], ALU.add).then_inc(var_ready, 1)
                dve.wait_ge(std_ready, c + 1)
                step(v.reciprocal(rstd[:, 0:n], std[:, c * n:(c + 1) * n]))
                normalise(xc, xc, n).then_inc(ln1_done, 1)

            dve.sem_inc(onehot_used, 2)
            step(v.tensor_scalar(blk_f[:, :], gm[:, 0, :], -1.0, None, ALU.mult))
            with dve.Fori(0, G // 2) as b:
                for h in range(2):
                    held(dve, passed, onehot_used, 2 * b + h + 1)
                    io = iota_b[:, :].unsqueeze(1).to_broadcast([P, GT, P])
                    lo_g = lo_b[:, 2 * b + h, :].unsqueeze(2).to_broadcast([P, GT, P])
                    hi_g = hi_b[:, 2 * b + h, :].unsqueeze(2).to_broadcast([P, GT, HI])
                    v.tensor_tensor(hot_lo[h], lo_g, io, ALU.is_equal)
                    v.tensor_tensor(hot_hi[h], hi_g, io[:, :, 0:HI], ALU.is_equal).then_inc(onehot_made, 1)

            dve.wait_ge(hist_done, 1)
            v.tensor_scalar(var[:, :], bank[1][:, HI:HI + T], 1.0, None, ALU.add).then_inc(var_ready, 1)
            dve.wait_ge(std_ready, NC + 1)
            step(v.reciprocal(dinv[:, :], std[:, :]))
            dve.wait_ge(h_ready, T + 1)
            for c in range(NC):
                a = slice(c * CHUNK, (c + 1) * CHUNK)
                v.tensor_tensor(acc[:, a, :], acc[:, a, :], dinv[:, a].unsqueeze(2).to_broadcast([P, CHUNK, D]),
                                ALU.mult).then_inc(table_ready, 1)
            dve.wait_ge(extremes_all, 1)
            step(v.tensor_scalar(blk_f[:, :], gall[:, 0, :], -1.0, None, ALU.mult))
            step(v.tensor_copy(blk_i[:, :], blk_f[:, :]))
            step(v.tensor_scalar(blk_i[:, :], blk_i[:, :], 7, None, ALU.logical_shift_right))
            step(v.tensor_copy(mhi[:, :], blk_i[:, :]))
            step(v.scalar_tensor_tensor(blk_f[:, :], mhi[:, :], -float(P), blk_f[:, :], ALU.mult, ALU.add))
            step(v.tensor_scalar(mlo[:, :], blk_f[:, :], iotap[:, :], None, ALU.is_gt))
            step(v.tensor_scalar(mhi[:, :], mlo[:, :], -1.0, 1.0, ALU.mult, ALU.add))
            step(v.tensor_tensor(gm[:, 0, :], gall[:, 0, :], gall[:, 1, :], ALU.add))
            step(v.tensor_reduce(wide_f[:, :], gm[:, 0, :], AX_X, ALU.max))
            step(v.tensor_scalar(wide_f[:, :], wide_f[:, :], float(P), None, ALU.is_ge))
            v.tensor_copy(wide_i[:, :], wide_f[:, :]).then_inc(windows_known, 1)

            v.tensor_copy(scol[:, :], bank[1][:, 0:K])
            v.tensor_copy(gram, bank[0][:, :].rearrange("p (k n) -> p k n", k=K)).then_inc(sm_dve, 1)
            dve.wait_ge(sm_pe, 2)
            v.scalar_tensor_tensor(urow[0:1, :], bqkv_s[0:1, 2 * D:3 * D], float(N), bank[5][0:1, 0:D],
                                   ALU.mult, ALU.add).then_inc(sm_dve, 1)
            v.memset(atb, 0.0)
            dve.wait_ge(sm_pe, 4)
            for q in range(2):
                a = slice(q * HD, (q + 1) * HD)
                ins = v.tensor_scalar(att[a, :, :], bank[6][a, 0:K * P].rearrange("p (k n) -> p k n", k=K)[:, :, a],
                                      SCALE, None, ALU.mult)
            step(ins)
            step(v.tensor_reduce(mneg[:, :], att, AX_X, ALU.max))
            v.tensor_scalar(mneg[:, :], mneg[:, :], -1.0, None, ALU.mult).then_inc(sm_dve, 1)
            dve.wait_ge(sm_act, 4)
            step(v.reciprocal(msum[:, :], msum[:, :]))
            step(v.tensor_tensor(att, atb[:, :, 0:HD], msum[:, :].unsqueeze(2).to_broadcast([P, K, HD]), ALU.mult))
            step(v.memset(atb, 0.0))
            for q in range(2):
                a = slice(q * HD, (q + 1) * HD)
                ins = v.tensor_copy(atb[a, :, a], att[a, :, :])
            ins.then_inc(sm_dve, 1)

            def window_hots(g):
                for h in range(2):
                    held(dve, passed, halves_summed, 2 * SLOTS + 2 * g + h - 1)
                    v.tensor_tensor(hot[h], lo_f[:, g, h * (GT // 2):(h + 1) * (GT // 2)].unsqueeze(2).to_broadcast([P, GT // 2, P]),
                                    iota_f[:, :].unsqueeze(1).to_broadcast([P, GT // 2, P]), ALU.is_equal).then_inc(hot_ready, 1)

            def add_window(g):
                held(dve, passed, halves_summed, 2 * SLOTS + 2 * g + 2)
                held(dve, passed, groups_added, g + 1)
                b = dve.value_load(blk_i[0:1, bass.ds(g, 1)], min_val=0, max_val=T - 1)
                v.scalar_tensor_tensor(acc[:, b, :], bank[0][:, 0:D], mhi[:, bass.ds(g, 1)], acc[:, b, :], ALU.mult, ALU.add)
                v.scalar_tensor_tensor(acc[:, b + 1, :], bank[0][:, 0:D], mlo[:, bass.ds(g, 1)], acc[:, b + 1, :],
                                       ALU.mult, ALU.add).then_inc(groups_added, 1)

            dve.sem_inc(groups_added, 1)
            dve.wait_ge(table_stored, 16 * NC)
            window_hots(0)
            with step.loop(T, 1) as t:
                held(dve, passed, m1_ps, t + 1)
                step(v.tensor_tensor(xn[:, t, :], bank[5][:, 0:D], xn[:, t, :], ALU.add))
                v.bn_stats(st[:, t, :], xn[:, t, :]).then_inc(m1_added, 1)
                window_hots(t + 1)
                add_window(t)
            dve.wait_ge(m1_added, T + 1)
            statistics(T)
            dve.wait_ge(std_ready, NC + 2)
            step(v.reciprocal(rstd[:, :], std[:, :]))
            with dve.Fori(0, T) as t:
                v.tensor_scalar(hn_s, xn[:, t, :], mean[:, bass.ds(t, 1)], rstd[:, bass.ds(t, 1)], ALU.subtract, ALU.mult).then_inc(hn_ready, 1)
                window_hots(t + (T + 1))
                add_window(t + T)
                held(dve, passed, fc2_ps, t + 1)
                v.tensor_tensor(xn[:, t, :], xn[:, t, :], bank[5][:, 0:D], ALU.add).then_inc(mix_added, 1)
            window_hots(G - 1)
            add_window(G - 2)
            add_window(G - 1)
            dve.wait_ge(groups_added, G + 1)
            dve.wait_ge(windows_known, 1)
            wide = dve.value_load(wide_i[0:1, 0:1], min_val=0, max_val=1)
            with dve.If(wide):
                dve.wait_ge(wide_reloaded, 16)
                with dve.Fori(0, G) as q:
                    v.tensor_copy(shifted, dst_f[:, q, :]).then_inc(wide_shifted, 1)
                    with dve.Fori(0, T) as b:
                        n = q * T + b
                        held(dve, passed, wide_shifted, n + q + 1)
                        for h in range(2):
                            ins = v.tensor_tensor(hot[h], shifted[:, h * (GT // 2):(h + 1) * (GT // 2)].unsqueeze(2).to_broadcast([P, GT // 2, P]),
                                                  iota_f[:, :].unsqueeze(1).to_broadcast([P, GT // 2, P]), ALU.is_equal)
                        ins.then_inc(wide_hot, 1)
                        held(dve, passed, wide_summed, n + 2)
                        v.tensor_tensor(acc[:, b, :], acc[:, b, :], bank[0][:, 0:D], ALU.add).then_inc(wide_added, 1)
                        held(dve, passed, wide_added, n + 2)
                        v.tensor_scalar(shifted, shifted, -float(P), None, ALU.add).then_inc(wide_shifted, 1)
                    held(dve, passed, wide_shifted, q * (T + 1) + (T + 1))
            v.tensor_copy(wide_f[:, :], iotap[:, :]).then_inc(aggregated, 1)

            dve.wait_ge(groups_added, G + 1)
            dve.wait_ge(mix_added, T + 1)
            dve.wait_ge(bcast_in, 48)
            k = NC + 2
            for c in range(NC):
                a = slice(c * CHUNK, (c + 1) * CHUNK)
                z, xc = acc[:, a, :], xn[:, a, :]

                def wide(row):
                    return row[:, :].unsqueeze(1).to_broadcast([P, CHUNK, D])

                step(v.tensor_tensor(z, z, dinv[:, a].unsqueeze(2).to_broadcast([P, CHUNK, D]), ALU.mult))
                step(v.tensor_tensor(z, z, wide(gb_b), ALU.add))

                def layer_norm(dest, source, k):
                    for u in range(CHUNK):
                        ins = v.bn_stats(st[:, u, :], source[:, u, :])
                    step(ins)
                    statistics(CHUNK)
                    dve.wait_ge(std_ready, k)
                    step(v.reciprocal(rstd[:, 0:CHUNK], std[:, 0:CHUNK]))
                    return normalise(dest, source, CHUNK)

                k += 1
                step(layer_norm(z, z, k))
                step(v.tensor_tensor(z, z, wide(gg_b), ALU.mult))
                step(v.tensor_tensor(z, z, wide(gbe_b), ALU.add))
                step(v.scalar_tensor_tensor(xc, z, 0.0, xc, ALU.max, ALU.add))
                dve.wait_ge(xre_in, 16 * (c + 1) if c < NC - 1 else 16 * (NC + 1))
                v.tensor_tensor(xc, xc, xre[:, :, :], ALU.add).then_inc(xre_used, 1)
                dve.wait_ge(xre_used, c + 1)
                k += 1
                if c:
                    dve.wait_ge(x2T_ps, c * CHUNK)
                layer_norm(x2s, xc, k).then_inc(x2_ready, 1)
                dve.wait_ge(x2_ready, c + 1)
                k += 1
                step(layer_norm(z, x2s, k))

            dve.wait_ge(lg_ready, T)

            def per_tile(a):
                return a[:, :].unsqueeze(2).to_broadcast([P, T, E])

            io8 = iota_f[:, 0:E].unsqueeze(1).to_broadcast([P, T, E])
            step(v.tensor_reduce(r1[:, :], lg[:, :, :], AX_X, ALU.max))
            v.tensor_tensor(lg[:, :, :], lg[:, :, :], per_tile(r1), ALU.subtract).then_inc(rt_dve, 1)
            dve.wait_ge(rt_act, 1)
            step(v.tensor_reduce(r1[:, :], pr[:, :, :], AX_X, ALU.add))
            step(v.reciprocal(r1[:, :], r1[:, :]))
            step(v.tensor_tensor(pr[:, :, :], pr[:, :, :], per_tile(r1), ALU.mult))

            def largest(mask, top):
                step(v.tensor_reduce(top[:, :], pr[:, :, :], AX_X, ALU.max))
                step(v.tensor_tensor(tmpr, pr[:, :, :], per_tile(top), ALU.is_lt))
                step(v.scalar_tensor_tensor(tmpr, tmpr, float(E), io8, ALU.mult, ALU.add))
                step(v.tensor_reduce(r2[:, :], tmpr, AX_X, ALU.min))
                step(v.tensor_tensor(mask[:, :, :], io8, per_tile(r2), ALU.is_equal))

            largest(m1, w1c)
            step(v.scalar_tensor_tensor(pr[:, :, :], m1[:, :, :], -2.0, pr[:, :, :], ALU.mult, ALU.add))
            largest(m2, w2c)
            step(v.tensor_tensor(r1[:, :], w1c[:, :], w2c[:, :], ALU.add))
            step(v.reciprocal(r1[:, :], r1[:, :]))
            v.tensor_tensor(w1c[:, :], w1c[:, :], r1[:, :], ALU.mult)
            v.tensor_tensor(w2c[:, :], w2c[:, :], r1[:, :], ALU.mult)
            v.tensor_scalar(m1[:, T - 1, :], m1[:, T - 1, :], valid[:, :], None, ALU.mult)
            step(v.tensor_scalar(m2[:, T - 1, :], m2[:, T - 1, :], valid[:, :], None, ALU.mult))
            v.tensor_tensor(tmpr, m1[:, :, :], m2[:, :, :], ALU.add).then_inc(rt_dve, 1)
            dve.wait_ge(rt_pe, 2)
            cv = bank[3][:, 0:T * E].rearrange("p (t e) -> p e t", t=T)
            step(v.tensor_copy(cnt, cv))
            for e in range(E):
                ins = v.tensor_tensor_scan(inc[:, e, :], ones[:, 0:T], cnt[:, e, :], 0.0, ALU.mult, ALU.add)
            step(ins)
            step(v.tensor_scalar(tl[:, 0, :], inc[:, :, T - 1], float(P - 1), None, ALU.add))
            step(v.tensor_copy(tl_i[:, :], tl[:, 0, :]))
            step(v.tensor_scalar(tl_i[:, :], tl_i[:, :], 7, None, ALU.logical_shift_right))
            step(v.tensor_copy(tl[:, 1, :], tl_i[:, :]))
            step(v.tensor_tensor_scan(tl[:, 2, :], ones[:, 0:E], tl[:, 1, :], 0.0, ALU.mult, ALU.add))
            step(v.tensor_tensor(tl[:, 3, :], tl[:, 2, :], tl[:, 1, :], ALU.subtract))
            step(v.tensor_tensor(inc, inc, cnt, ALU.subtract))
            step(v.scalar_tensor_tensor(inc, tl[:, 3, :].unsqueeze(2).to_broadcast([P, E, T]), float(P), inc, ALU.mult, ALU.add))
            step(v.tensor_tensor(pos, bank[2][:, 0:T * E].rearrange("p (t e) -> p t e", t=T),
                                 inc.rearrange("p e t -> p t e"), ALU.add))
            for j, m in enumerate((m1, m2)):
                step(v.tensor_tensor(m[:, :, :], m[:, :, :], pos, ALU.mult))
                step(v.tensor_reduce(r1[:, :], m[:, :, :], AX_X, ALU.add))
                step(v.tensor_copy(pos_i[:, j, :], r1[:, :]))
            step(v.tensor_scalar(tile_f[:, :], iota_f[:, 0:W + 1], tl[:, 3, 1:2], None, ALU.is_ge))
            for e in range(2, E):
                step(v.scalar_tensor_tensor(tile_f[:, :], iota_f[:, 0:W + 1], tl[:, 3, e:e + 1], tile_f[:, :], ALU.is_ge, ALU.add))
            v.tensor_copy(tile_e[:, :], tile_f[:, :]).then_inc(pos_ready, 1)

            lg_cols = vcol[:, VLG:VLG + E * K].rearrange("p (e k) -> p e k", k=K)
            lb_cols = vcol[:, VLB:VLB + E * K].rearrange("p (e k) -> p e k", k=K)
            half = KH // 2
            dve.wait_ge(pos_ready, 1)
            dve.wait_ge(rows_routed, 16 * TOPK * T)

            def expert_input(w):
                e = dve.value_load(tile_e[0:1, bass.ds(w, 1)], min_val=0, max_val=E - 1)
                held(dve, passed, xe_transposed, w + 2)
                v.tensor_copy(gcol[:, 0:K], lg_cols[:, e, :])
                step(v.tensor_copy(gcol[:, K:2 * K], lb_cols[:, e, :]))
                for q in range(K):
                    ins = v.tensor_scalar(xeT[:, q, :], bank[6][:, q * P:(q + 1) * P], gcol[:, q:q + 1],
                                          gcol[:, K + q:K + q + 1], ALU.mult, ALU.add)
                ins.then_inc(xeT_ready, 1)

            def add_bias(w, first):
                held(dve, passed, up_done, w + 1)
                held(dve, passed, bias_in, 32 * w + 32)
                if not first:
                    held(dve, passed, hidden, w)
                for q in range(2):
                    ins = v.tensor_tensor(hpre[:, q * 512:(q + 1) * 512], bank[q][:, :], b1t[:, q * 512:(q + 1) * 512], ALU.add)
                ins.then_inc(biased, 1)

            def finish_tile(w, first=False):
                held(dve, passed, down_done, w + 1)
                if not first:
                    held(dve, passed, y_stored, 16 * w)
                v.tensor_tensor(ys, bank[7][:, 0:D], b2t[:, w % 2, :], ALU.add).then_inc(y_ready, 1)

            def evacuate_hidden(w):
                held(dve, passed, hT_ps, w + 1)
                v.tensor_copy(hT[:, half:KH, :], bank[3][:, :].rearrange("p (m n) -> p m n", m=half)).then_inc(hT_dve, 1)

            dve.sem_inc(y_ready, TOPK)
            expert_input(0)
            add_bias(0, True)
            expert_input(1)
            evacuate_hidden(0)
            add_bias(1, False)
            expert_input(2)
            finish_tile(0, True)
            with step.loop(W - 2, 1) as i:
                evacuate_hidden(i + 1)
                add_bias(i + 2, False)
                expert_input(i + 3)
                finish_tile(i + 1)
            evacuate_hidden(W - 1)
            finish_tile(W - 1)

            for c in range(NC):
                a = slice(c * CHUNK, (c + 1) * CHUNK)
                dve.wait_ge(picked[c], 16 * TOPK * CHUNK)
                for y, wc in ((y1, w1c), (y2, w2c)):
                    v.tensor_tensor(y[:, a, :], y[:, a, :], wc[:, a].unsqueeze(2).to_broadcast([P, CHUNK, D]), ALU.mult)
                step(v.tensor_copy(r1[:, 0:1], r2[:, 0:1]))
                step(v.tensor_tensor(xn[:, a, :], xn[:, a, :], y1[:, a, :], ALU.add))
                v.tensor_tensor(xn[:, a, :], xn[:, a, :], y2[:, a, :], ALU.add).then_inc(out_ready, 1)


INS = ['x', 'src', 'dst', 'L0_gnn_W', 'L0_gnn_b', 'L0_gnn_gamma', 'L0_gnn_beta', 'L0_mix_w_qkv', 'L0_mix_b_qkv',
       'L0_mix_norm_g', 'L0_mix_norm_b', 'L0_mix_w_fc1', 'L0_mix_b_fc1', 'L0_mix_w_fc2', 'L0_mix_b_fc2',
       'L0_ffn_Wr', 'L0_ffn_br', 'L0_ffn_ln_g', 'L0_ffn_ln_b', 'L0_ffn_W1', 'L0_ffn_b1', 'L0_ffn_W2', 'L0_ffn_b2']


def kernel(**inputs):
    import numpy as np
    import concourse.bacc as bacc
    from concourse.bass_utils import run_bass_kernel_spmd

    nc = bacc.Bacc("TRN2", target_bir_lowering=False, num_devices=1)
    arrays, args = {}, []
    for name in INS:
        a = np.ascontiguousarray(inputs[name])
        arrays[f"in_{name}"] = a
        args.append(nc.dram_tensor(f"in_{name}", a.shape, mybir.dt.from_np(a.dtype), kind="ExternalInput").ap())
    args.append(nc.dram_tensor("out_x", inputs["x"].shape, F32, kind="ExternalOutput").ap())
    gps_layer(nc, *args)
    r = run_bass_kernel_spmd(nc, [arrays], core_ids=[0])
    return r.results[0]["out_x"]
```

```python
from contextlib import ExitStack, contextmanager

import concourse.bass as bass
from concourse import mybir

F32 = mybir.dt.float32
BF16 = mybir.dt.bfloat16
F16 = mybir.dt.float16
I32 = mybir.dt.int32
U32 = mybir.dt.uint32
ALU = mybir.AluOpType
ACT = mybir.ActivationFunctionType
AX_X = mybir.AxisListType.X
RMAX = bass.bass_isa.ReduceOp.max

P = 128
EPS = 1e-5
CHUNK = 5
GT = 8
UP = 256.0
PARTS = ((0, 0), (0, 1), (1, 0))
SLOTS = 4


def held(eng, passed, sem, value):
    eng.wait_ge(sem, value)
    if not isinstance(value, int):
        eng.sem_inc(passed, 1)


class Chain:

    def __init__(self, eng, sem, passed):
        self.eng, self.sem, self.passed = eng, sem, passed
        self.base = 0
        self.n = 0

    def __call__(self, ins):
        ins.then_inc(self.sem, 1)
        self.n += 1
        held(self.eng, self.passed, self.sem, self.base + self.n)

    @contextmanager
    def loop(self, trips, per):
        start = self.n
        with self.eng.Fori(0, trips) as i:
            self.base, self.n = i * per + start, 0
            yield i
            assert self.n == per, (self.n, per)
        self.base, self.n = 0, start + trips * per


def gps_layer(nc, x, src, dst, gW, gb, ggamma, gbeta, wqkv, bqkv, ng, nb, wfc1, bfc1, wfc2, bfc2,
              Wr, br, lng, lnb, W1, b1, W2, b2, out):
    N, D = x.shape
    NE = src.shape[0]
    E, _, H = W1.shape
    HID = wfc1.shape[1]
    K = D // P
    KM = HID // P
    KH = H // P
    T = -(-N // P)
    LAST = N - (T - 1) * P
    NC = T // CHUNK
    G = -(-NE // (P * GT))
    EG = P * GT
    EL = NE - (G - 1) * EG
    EROW, EREM = EL // GT, EL % GT
    HI = 32
    PAD_DST = P * HI + P - 1
    TOPK = 2
    HD = 64
    SCALE = float(HD) ** -0.5
    W = TOPK * N // P + E
    WC = K * H + KH * D
    EARLY = 1
    assert T == NC * CHUNK and D == K * P and 2 * T + 2 == G and G % SLOTS == 0 and G // 2 == T + 1

    table = nc.dram_tensor("h_table", (T * P, D), F32).ap()
    slots = nc.dram_tensor("slot_rows", ((W + 1) * P, D), F32).ap()
    yrows = nc.dram_tensor("expert_rows", (W * P, D), F32).ap()

    with ExitStack() as ctx:
        ctx.enter_context(nc.allow_non_contiguous_dma("index lists of eight edges a partition"))

        def sb(name, shape, dt=F32):
            return ctx.enter_context(nc.sbuf_tensor(name, shape, dt))

        def sem(name):
            return ctx.enter_context(nc.semaphore(name))

        wall = sb("wall", [P, E * WC])
        acc = sb("acc", [P, T + 1, D])
        xn = sb("xn", [P, T, D])
        cursor = [EARLY * WC]

        def room(cols):
            a = cursor[0]
            cursor[0] += cols
            assert cursor[0] <= E * WC
            return wall[:, a:a + cols]

        ring = room(SLOTS * GT * D).rearrange("p (s c) -> p s c", s=SLOTS * GT)
        hot = [room(GT // 2 * P).rearrange("p (j n) -> p j n", j=GT // 2) for _ in range(2)]
        hot_lo = [room(GT * P // 2).bitcast(BF16).rearrange("p (j n) -> p j n", j=GT) for _ in range(2)]
        hot_hi = [room(GT * HI // 2).bitcast(BF16).rearrange("p (j n) -> p j n", j=GT) for _ in range(2)]
        wqkv_s = room(K * 3 * D).rearrange("p (k n) -> p k n", k=K)
        wfc = room(K * HID + KM * D)
        wfc1_s = wfc[:, 0:K * HID].rearrange("p (k n) -> p k n", k=K)
        wfc2_s = wfc[:, K * HID:].rearrange("p (k n) -> p k n", k=KM)
        wfc_pair = wfc.bitcast(F16).rearrange("p (n h) -> p n h", h=2)
        wfc_hi = [room(1024 // 2).bitcast(F16) for _ in range(1)]
        gW_s = room(K * D).rearrange("p (k n) -> p k n", k=K)
        gWT = room(K * D).rearrange("p (k n) -> p k n", k=K)
        wqT = room(K * D).rearrange("p (k n) -> p k n", k=K)
        gram = room(K * D).rearrange("p (k n) -> p k n", k=K)
        xtv = room(K * D).rearrange("p (k n) -> p k n", k=K)
        wqa = room(K * D).rearrange("p (k n) -> p k n", k=K)
        xs = room(D)
        xT_s = room(D).rearrange("p (k n) -> p k n", k=K)
        hn_s = room(D)
        hnT_f = room(D)
        hnT = [room(D // 2).bitcast(F16) for _ in range(2)]
        h1_f = room(HID)
        h1 = [room(HID // 2).bitcast(F16) for _ in range(2)]
        att = room(K * HD).rearrange("p (k n) -> p k n", k=K)
        atb = room(K * P).rearrange("p (k n) -> p k n", k=K)
        atT = room(K * P).rearrange("p (k n) -> p k n", k=K)
        dst_i = room(G * GT).bitcast(I32)
        tmp_i = room(G * GT).bitcast(I32)
        hi_f = room(G * GT)

        NV = 2 * K + KM + K + 2 * E * K + E * KH
        vrow = room(P)
        VNG, VNB, VF1, VBQ, VLG, VLB, VB1 = 0, K, 2 * K, 2 * K + KM, 3 * K + KM, 3 * K + KM + E * K, 3 * K + KM + 2 * E * K
        vcol = sb("vcol", [P, NV])
        bqkv_s = room(3 * D)
        bfc2_s = room(D)
        srow = room(D)
        urow = room(D)
        bqa = room(D)

        ident = sb("ident", [P, P])
        iota_i = room(P).bitcast(I32)
        iotap_i = sb("iotap_i", [P, 1], I32)
        iota_f = sb("iota_f", [P, P])
        iota_b = sb("iota_b", [P, P], BF16)
        iotap = sb("iotap", [P, 1])
        before = sb("before", [P, P])
        ones = sb("ones", [P, P])
        zeros = room(512)
        gb_b = sb("gb_b", [P, D])
        gg_b = sb("gg_b", [P, D])
        gbe_b = sb("gbe_b", [P, D])
        wr_s = sb("wr_s", [P, K, E])
        br_s = sb("br_s", [1, E])
        src_i = room((G + 1) * GT).bitcast(I32)
        lo_f = room(G * GT).rearrange("p (g j) -> p g j", j=GT)
        lo_b = room(G * GT // 2).bitcast(BF16).rearrange("p (g j) -> p g j", j=GT)
        hi_b = room(G * GT // 2).bitcast(BF16).rearrange("p (g j) -> p g j", j=GT)
        dst_f = room(G * GT).rearrange("p (g j) -> p g j", j=GT)
        shifted = room(GT)
        idx_s = [sb(f"idx_s{k}", [P, GT], I32) for k in range(SLOTS)]
        gm = sb("gm", [P, 2, G])
        gall = sb("gall", [P, 2, G])
        blk_i = sb("blk_i", [P, G], I32)
        blk_f = sb("blk_f", [P, G])
        wide_f = sb("wide_f", [P, 1])
        wide_i = sb("wide_i", [P, 1], I32)
        mhi = sb("mhi", [P, G])
        mlo = sb("mlo", [P, G])
        scol = sb("scol", [P, K])
        dinv = sb("dinv", [P, T])
        st = sb("st", [P, T, 6])
        small = sb("small", [P, 4, T])
        mean = sb("mean", [P, T])
        var = sb("var", [P, T])
        std = sb("std", [P, T])
        rstd = sb("rstd", [P, T])
        x2s = sb("x2s", [P, CHUNK, D])
        xre = sb("xre", [P, CHUNK, D])
        x2T = sb("x2T", [P, K, P])
        lg = sb("lg", [P, T, E])
        pr = sb("pr", [P, T, E])
        m1 = sb("m1", [P, T, E])
        m2 = sb("m2", [P, T, E])
        r1 = sb("r1", [P, T])
        r2 = sb("r2", [P, T])
        w1c = sb("w1c", [P, T])
        w2c = sb("w2c", [P, T])
        mneg = sb("mneg", [P, K])
        msum = sb("msum", [P, K])
        valid = sb("valid", [P, 1])
        cnt = x2s[:, 0, 0:E * T].rearrange("p (e t) -> p e t", e=E)
        inc = x2s[:, 1, 0:E * T].rearrange("p (e t) -> p e t", e=E)
        pos = x2s[:, 2, 0:E * T].rearrange("p (t e) -> p t e", t=T)
        tmpr = x2s[:, 3, 0:E * T].rearrange("p (t e) -> p t e", t=T)
        tl = sb("tl", [P, 4, E])
        tl_i = sb("tl_i", [P, E], I32)
        pos_i = sb("pos_i", [P, TOPK, T], I32)
        tile_f = sb("tile_f", [P, W + 1])
        tile_e = sb("tile_e", [P, W + 1], I32)

        acc_flat = acc[:, :, :].rearrange("p t d -> p (t d)")
        c2 = [0]

        def late(cols):
            a = c2[0]
            c2[0] += cols
            assert c2[0] <= (T + 1) * D
            return acc_flat[:, a:a + cols]

        xe = late(D)
        xeT_f = late(D)
        xeT = [late(D // 2).bitcast(F16) for _ in range(2)]
        b2t = late(2 * D).rearrange("p (s d) -> p s d", s=2)
        h_f = late(H)
        h_pair = [late(H // 2).bitcast(F16) for _ in range(2)]
        bcol = late(KH)
        ys = late(D)
        gcol = late(2 * K)

        y1 = wall[:, 0:T * D].rearrange("p (t d) -> p t d", t=T)
        y2 = wall[:, T * D:2 * T * D].rearrange("p (t d) -> p t d", t=T)

        bank = [ctx.enter_context(nc.psum_tensor(f"bank{i}", [P, 512], F32)) for i in range(8)]
        w1e = wall[:, :].rearrange("p (e c) -> p e c", e=E)
        wpair = wall[:, :].bitcast(F16).rearrange("p (n h) -> p n h", h=2)
        NFC = (K * HID + KM * D) // 1024
        CC = 1024
        split_hi = [xre[:, 2 * b:2 * b + 2, :].rearrange("p u d -> p (u d)").bitcast(F16) for b in range(2)]

        passed = sem("passed")
        cleared = sem("cleared")
        iotas = sem("iotas")
        x_in = sem("x_in")
        edges_in = sem("edges_in")
        weights_in = sem("weights_in")
        vrows_in = sem("vrows_in")
        rows_in = sem("rows_in")
        bcast_in = sem("bcast_in")
        early_in = sem("early_in")
        late_in = sem("late_in")
        slots_zeroed = sem("slots_zeroed")
        dve_step = sem("dve_step")
        act_step = sem("act_step")
        consts = sem("consts")
        vcol_ps = sem("vcol_ps")
        vcol_ok = sem("vcol_ok")
        wT_ps = sem("wT_ps")
        wT_ok = sem("wT_ok")
        var_ready = sem("var_ready")
        std_ready = sem("std_ready")
        ln1_done = sem("ln1_done")
        onehot_made = sem("onehot_made")
        onehot_used = sem("onehot_used")
        xs_ready = sem("xs_ready")
        xT_ps = sem("xT_ps")
        xT_ready = sem("xT_ready")
        xs_used = sem("xs_used")
        h_ps = sem("h_ps")
        h_ready = sem("h_ready")
        hist_done = sem("hist_done")
        table_ready = sem("table_ready")
        table_stored = sem("table_stored")
        extremes = sem("extremes")
        extremes_all = sem("extremes_all")
        sm_pe = sem("attention_pe")
        sm_dve = sem("attention_dve")
        sm_act = sem("attention_act")
        idx_ready = sem("idx_ready")
        gathered = [sem(f"gathered{k}") for k in range(SLOTS)]
        groups_ready = sem("groups_ready")
        hot_ready = sem("hot_ready")
        halves_summed = sem("halves_summed")
        groups_added = sem("groups_added")
        windows_known = sem("windows_known")
        wide_reloaded = sem("wide_reloaded")
        wide_gathered = sem("wide_gathered")
        wide_idx = sem("wide_idx")
        wide_hot = sem("wide_hot")
        wide_summed = sem("wide_summed")
        wide_added = sem("wide_added")
        wide_shifted = sem("wide_shifted")
        aggregated = sem("aggregated")
        m1_ps = sem("m1_ps")
        m1_added = sem("m1_added")
        hn_ready = sem("hn_ready")
        hnT_ps = sem("hnT_ps")
        hnT_ready = sem("hnT_ready")
        fc1_ps = sem("fc1_ps")
        fc1_act = sem("fc1_act")
        fc1_hi = sem("fc1_hi")
        fc1_lo = sem("fc1_lo")
        fc2_ps = sem("fc2_ps")
        mix_added = sem("mix_added")
        xre_in = sem("xre_in")
        xre_used = sem("xre_used")
        x2_ready = sem("x2_ready")
        x2T_ps = sem("x2T_ps")
        x2T_ready = sem("x2T_ready")
        lg_ps = sem("lg_ps")
        lg_ready = sem("lg_ready")
        rt_dve = sem("routing_dve")
        rt_act = sem("routing_act")
        rt_pe = sem("routing_pe")
        pos_ready = sem("pos_ready")
        rows_routed = sem("rows_routed")
        xe_in = sem("xe_in")
        bias_in = sem("bias_in")
        fc_hi = sem("fc_hi")
        fc_bias = sem("fc_bias")
        fc_lo = sem("fc_lo")
        fc_split = sem("fc_split")
        split_cast = sem("split_cast")
        split_low = sem("split_low")
        weights_split = sem("weights_split")
        xe_transposed = sem("xe_transposed")
        xeT_ready = sem("xeT_ready")
        up_done = sem("up_done")
        activated = sem("activated")
        hidden_hi = sem("hidden_hi")
        hidden_lo = sem("hidden_lo")
        down_done = sem("down_done")
        y_ready = sem("y_ready")
        y_stored = sem("y_stored")
        picked = [sem(f"picked{c}") for c in range(NC)]
        out_ready = sem("out_ready")
        out_stored = sem("out_stored")

        NW = 5
        block = ctx.enter_context(nc.Block())

        @block.sync
        def _(sp):
            sp.wait_ge(cleared, 4)
            sp.dma_start(xn[:, 0:T - 1, :], x[0:(T - 1) * P, :].rearrange("(t p) d -> p t d", p=P)).then_inc(x_in, 16)
            sp.dma_start(xn[0:LAST, T - 1, :], x[(T - 1) * P:N, :]).then_inc(x_in, 16)
            for buf, vec in ((dst_i, dst), (src_i[:, :], src)):
                v = buf[:, 0:G * GT].rearrange("p (g j) -> p g j", j=GT)
                sp.dma_start(v[:, 0:G - 1, :], vec[0:(G - 1) * EG].rearrange("(g p j) -> p g j", p=P, j=GT)).then_inc(edges_in, 16)
                sp.dma_start(v[0:EROW, G - 1, :], vec[(G - 1) * EG:(G - 1) * EG + EROW * GT].rearrange("(p j) -> p j", j=GT)).then_inc(edges_in, 16)
                sp.dma_start(v[EROW:EROW + 1, G - 1, 0:EREM], vec[NE - EREM:NE].rearrange("(p j) -> p j", p=1)).then_inc(edges_in, 16)
            sp.dma_start(gW_s, gW.rearrange("(k p) n -> p k n", p=P)).then_inc(weights_in, 16)
            sp.dma_start(wqkv_s, wqkv.rearrange("(k p) n -> p k n", p=P)).then_inc(weights_in, 16)
            sp.dma_start(wfc1_s, wfc1.rearrange("(k p) n -> p k n", p=P)).then_inc(weights_in, 16)
            sp.dma_start(wfc2_s, wfc2.rearrange("(k p) n -> p k n", p=P)).then_inc(weights_in, 16)
            sp.dma_start(wr_s[:, :, :], Wr.rearrange("(k p) n -> p k n", p=P)).then_inc(weights_in, 16)

            def load_expert(e, done):
                sp.dma_start(w1e[:, e, 0:K * H].rearrange("p (k n) -> p k n", k=K),
                             W1[e].rearrange("(k p) n -> p k n", p=P)).then_inc(done, 16)
                sp.dma_start(w1e[:, e, K * H:WC].rearrange("p (k n) -> p k n", k=KH),
                             W2[e].rearrange("(k p) n -> p k n", p=P)).then_inc(done, 16)

            for e in range(EARLY):
                load_expert(e, early_in)
            sp.wait_ge(consts, 1)
            sp.dma_start(slots.rearrange("(w p) d -> p w d", p=P),
                         zeros[:, 0:D].unsqueeze(1).to_broadcast([P, W + 1, D])).then_inc(slots_zeroed, 16)
            for c in range(NC):
                sp.wait_ge(table_ready, c + 1)
                sp.dma_start(table[c * CHUNK * P:(c + 1) * CHUNK * P, :].rearrange("(t p) d -> p t d", p=P),
                             acc[:, c * CHUNK:(c + 1) * CHUNK, :]).then_inc(table_stored, 16)
            sp.wait_ge(aggregated, 1)
            sp.wait_ge(mix_added, T + 1)
            sp.wait_ge(idx_ready, G + 1)
            sp.wait_ge(slots_zeroed, 16)
            for e in range(EARLY, E):
                load_expert(e, late_in)
            for c in range(NC):
                if c:
                    sp.wait_ge(xre_used, c)
                a = c * CHUNK
                n = CHUNK if c < NC - 1 else CHUNK - 1
                sp.dma_start(xre[:, 0:n, :], x[a * P:(a + n) * P, :].rearrange("(t p) d -> p t d", p=P)).then_inc(xre_in, 16)
                if c == NC - 1:
                    sp.dma_start(xre[0:LAST, CHUNK - 1, :], x[(T - 1) * P:N, :]).then_inc(xre_in, 16)
            sp.wait_ge(rows_routed, 16 * TOPK * T)
            sp.sem_inc(xe_transposed, 1)
            with sp.Fori(0, W) as w:
                held(sp, passed, xe_transposed, w + 1)
                sp.dma_start(xe, slots[bass.ts(w, P), :]).then_inc(xe_in, 16)
                e = sp.value_load(tile_e[0:1, bass.ds(w, 1)], min_val=0, max_val=E - 1)
                held(sp, passed, y_ready, w + 1)
                sp.dma_start(b2t[:, w % 2, :], b2[e, :].partition_broadcast(P)).then_inc(bias_in, 16)
            sp.wait_ge(xe_transposed, W + 1)
            sp.dma_start(xe, slots[W * P:(W + 1) * P, :]).then_inc(xe_in, 16)
            for c in range(NC):
                a = c * CHUNK
                n = CHUNK if c < NC - 1 else CHUNK - 1
                sp.wait_ge(out_ready, c + 1)
                sp.dma_start(out[a * P:(a + n) * P, :].rearrange("(t p) d -> p t d", p=P), xn[:, a:a + n, :]).then_inc(out_stored, 16)
            sp.dma_start(out[(T - 1) * P:N, :], xn[0:LAST, T - 1, :]).then_inc(out_stored, 16)
            sp.wait_ge(out_stored, 16 * (NC + 1))

        @block.gpsimd
        def _(pool):
            g = nc.gpsimd
            g.memset(xn[:, T - 1, :], 0.0).then_inc(cleared, 1)
            g.memset(dst_i[:, (G - 1) * GT:], PAD_DST).then_inc(cleared, 1)
            g.memset(src_i[:, (G - 1) * GT:], 0).then_inc(cleared, 1)
            g.memset(xre[:, CHUNK - 1, :], 0.0).then_inc(cleared, 1)
            g.iota(iota_i, pattern=[[1, P]], base=0, channel_multiplier=0).then_inc(iotas, 1)
            g.iota(iotap_i[:, :], pattern=[[0, 1]], base=0, channel_multiplier=1).then_inc(iotas, 1)
            g.memset(acc[:, T, :], 0.0).then_inc(cleared, 1)
            pool.wait_ge(extremes, 1)
            g.partition_all_reduce(gall[:, :, :].rearrange("p a g -> p (a g)"), gm[:, :, :].rearrange("p a g -> p (a g)"), P, RMAX).then_inc(extremes_all, 1)
            pool.sem_inc(halves_summed, 2 * SLOTS)
            pool.wait_ge(edges_in, 96)
            g.tensor_copy(idx_s[0][:, :], src_i[:, 0:GT]).then_inc(idx_ready, 1)
            pool.wait_ge(table_stored, 16 * NC)

            def gather(g_, slot, turn_before):
                held(pool, passed, halves_summed, 2 * g_ + 2)
                held(pool, passed, idx_ready, g_ + 1)
                for j in range(GT):
                    g.indirect_dma_start(ring[:, slot * GT + j, :], None, table,
                                         bass.IndirectOffsetOnAxis(ap=idx_s[slot][:, j:j + 1].bitcast(U32), axis=0)).then_inc(gathered[slot], 16)
                    if j == GT // 2 - 1:
                        if turn_before is not None:
                            held(pool, passed, gathered[slot - 1], turn_before * (16 * GT))
                            pool.sem_inc(groups_ready, 1)
                        g.tensor_copy(idx_s[(slot + 1) % SLOTS][:, :], src_i[:, bass.ds((g_ + 1) * GT, GT)]).then_inc(idx_ready, 1)

            gather(0, 0, None)
            TURNS = (G - 1) // SLOTS
            with pool.Fori(0, TURNS) as r:
                for k in range(1, SLOTS + 1):
                    gather(SLOTS * r + k, k % SLOTS, r + 1)
            for g_ in range(SLOTS * TURNS + 1, G):
                gather(g_, g_ % SLOTS, TURNS + 1)
            pool.wait_ge(gathered[(G - 1) % SLOTS], G // SLOTS * (16 * GT))
            pool.sem_inc(groups_ready, 1)
            pool.wait_ge(windows_known, 1)
            wide = pool.value_load(wide_i[0:1, 0:1], min_val=0, max_val=1)
            with pool.If(wide):
                pool.wait_ge(groups_added, G + 1)
                g.dma_start(acc[:, 0:T, :], table.rearrange("(t p) d -> p t d", p=P)).then_inc(wide_reloaded, 16)
                pool.wait_ge(idx_ready, G + 1)
                pool.sem_inc(wide_summed, 1)
                with pool.Fori(0, G) as q:
                    held(pool, passed, wide_summed, q * T + 1)
                    g.tensor_copy(idx_s[0][:, :], src_i[:, bass.ds(q * GT, GT)]).then_inc(wide_idx, 1)
                    held(pool, passed, wide_idx, q + 1)
                    for j in range(GT):
                        g.indirect_dma_start(ring[:, j, :], None, table,
                                             bass.IndirectOffsetOnAxis(ap=idx_s[0][:, j:j + 1].bitcast(U32), axis=0)).then_inc(wide_gathered, 16)
            pool.wait_ge(pos_ready, 1)
            pool.wait_ge(slots_zeroed, 16)
            for t in range(T):
                n = P if t < T - 1 else LAST
                for j in range(TOPK):
                    g.indirect_dma_start(slots, bass.IndirectOffsetOnAxis(ap=pos_i[0:n, j, t:t + 1].bitcast(U32), axis=0),
                                         acc[0:n, t, :], None).then_inc(rows_routed, 16)
            with pool.Fori(0, W) as w:
                held(pool, passed, y_ready, w + (TOPK + 1))
                g.dma_start(yrows[bass.ts(w, P), :], ys).then_inc(y_stored, 16)
            pool.wait_ge(y_stored, 16 * W)
            for t in range(T):
                n = P if t < T - 1 else LAST
                for j, y in enumerate((y1, y2)):
                    g.indirect_dma_start(y[0:n, t, :], None, yrows,
                                         bass.IndirectOffsetOnAxis(ap=pos_i[0:n, j, t:t + 1].bitcast(U32), axis=0)).then_inc(picked[t // CHUNK], 16)

        @block.scalar
        def _(act):
            s = nc.scalar
            for r, n, vec in ((VNG, K, ng), (VNB, K, nb), (VF1, KM, bfc1), (VBQ, K, bqkv[0:D])):
                act.dma_start(vrow[r:r + n, :], vec.rearrange("(r p) -> r p", p=P)).then_inc(vrows_in, 16)
            for r, mat in ((VLG, lng), (VLB, lnb)):
                act.dma_start(vrow[r:r + E * K, :], mat.rearrange("e (k p) -> (e k) p", p=P)).then_inc(vrows_in, 16)
            act.dma_start(vrow[VB1:VB1 + E * KH, :], b1.rearrange("e (k p) -> (e k) p", p=P)).then_inc(vrows_in, 16)
            act.dma_start(bqkv_s[0:1, :], bqkv.unsqueeze(0)).then_inc(rows_in, 16)
            act.dma_start(bfc2_s[0:1, :], bfc2.unsqueeze(0)).then_inc(rows_in, 16)
            act.dma_start(br_s[:, :], br.unsqueeze(0)).then_inc(rows_in, 16)
            for buf, vec in ((gb_b, gb), (gg_b, ggamma), (gbe_b, gbeta)):
                act.dma_start(buf[:, :], vec.partition_broadcast(P)).then_inc(bcast_in, 16)
            act.wait_ge(vcol_ps, 1)
            s.activation(vcol[:, :], bank[7][:, 0:NV], ACT.Copy).then_inc(vcol_ok, 1)
            act.wait_ge(wT_ps, 1)
            s.activation(gWT, bank[6][:, :].rearrange("p (k n) -> p k n", k=K), ACT.Copy).then_inc(wT_ok, 1)
            act.wait_ge(wT_ps, 2)
            s.activation(wqT, bank[7][:, :].rearrange("p (k n) -> p k n", k=K), ACT.Copy).then_inc(wT_ok, 1)
            for c in range(NC):
                act.wait_ge(var_ready, c + 1)
                s.activation(std[:, c * CHUNK:(c + 1) * CHUNK], var[:, c * CHUNK:(c + 1) * CHUNK], ACT.Sqrt).then_inc(std_ready, 1)
            act.wait_ge(ln1_done, NC)
            act.wait_ge(cleared, 5)
            act.wait_ge(weights_in, 80)
            for c in range(NFC):
                a = slice(c * CC, (c + 1) * CC)
                if c:
                    act.wait_ge(fc_split, c)
                s.activation(wfc_hi[0], wfc[:, a], ACT.Copy, scale=UP).then_inc(fc_hi, 1)
                act.wait_ge(fc_lo, c + 1)
                s.activation(wfc_pair[:, a, 0], wfc_hi[0], ACT.Copy).then_inc(fc_split, 1)
            act.sem_inc(xs_used, 1)
            with act.Fori(0, T) as t:
                held(act, passed, xs_used, t + 1)
                s.activation(xs, xn[:, t, :], ACT.Copy).then_inc(xs_ready, 1)
                held(act, passed, xT_ps, t + 1)
                s.activation(xT_s, bank[2][:, 0:D].rearrange("p (k n) -> p k n", k=K), ACT.Copy).then_inc(xT_ready, 1)
                held(act, passed, h_ps, t + 1)
                s.activation(acc[:, t, :], bank[4][:, 0:D], ACT.Copy).then_inc(h_ready, 1)
            act.wait_ge(var_ready, NC + 1)
            s.activation(std[:, :], var[:, :], ACT.Sqrt).then_inc(std_ready, 1)
            act.wait_ge(sm_pe, 1)
            s.activation(srow[0:1, :], bank[6][0:1, 0:D], ACT.Copy).then_inc(sm_act, 1)
            act.wait_ge(sm_pe, 3)
            s.activation(xtv, bank[7][:, :].rearrange("p (k n) -> p k n", k=K), ACT.Copy).then_inc(sm_act, 1)
            act.wait_ge(sm_dve, 3)
            for k in range(K):
                s.activation(atb[:, k, 0:HD], att[:, k, :], ACT.Exp, bias=mneg[:, k:k + 1], accum_out=msum[:, k:k + 1]).then_inc(sm_act, 1)
            act.wait_ge(sm_pe, 5)
            s.activation(atT, bank[6][:, 0:K * P].rearrange("p (k n) -> p k n", k=K), ACT.Copy).then_inc(sm_act, 1)
            act.wait_ge(sm_pe, 6)
            s.activation(wqa, bank[7][:, :].rearrange("p (k n) -> p k n", k=K), ACT.Copy).then_inc(sm_act, 1)
            act.wait_ge(sm_pe, 7)
            s.activation(bqa[0:1, :], bank[6][0:1, 0:D], ACT.Copy).then_inc(sm_act, 1)
            act.wait_ge(xs_used, T + 1)
            with act.Fori(0, T) as t:
                s.activation(xs, xn[:, t, :], ACT.Copy).then_inc(xs_ready, 1)
                held(act, passed, xT_ps, t + (T + 1))
                s.activation(xT_s, bank[2][:, 0:D].rearrange("p (k n) -> p k n", k=K), ACT.Copy).then_inc(xT_ready, 1)
            act.wait_ge(var_ready, NC + 2)
            s.activation(std[:, :], var[:, :], ACT.Sqrt).then_inc(std_ready, 1)
            def mixer_activate(t):
                held(act, passed, fc1_ps, t + 1)
                held(act, passed, fc1_lo, t + 1)
                for m in range(KM):
                    ins = s.activation(h1_f[:, m * P:(m + 1) * P], bank[2 + m // 4][:, m % 4 * P:(m % 4 + 1) * P], ACT.Gelu,
                                       bias=vcol[:, VF1 + m:VF1 + m + 1], scale=1.0 / UP)
                ins.then_inc(fc1_act, 1)
                held(act, passed, fc1_act, t + 1)

            mixer_activate(0)
            s.activation(h1[0], h1_f, ACT.Copy).then_inc(fc1_hi, 1)
            with act.Fori(0, T - 1) as i:
                mixer_activate(i + 1)
                held(act, passed, fc2_ps, i + 1)
                s.activation(h1[0], h1_f, ACT.Copy).then_inc(fc1_hi, 1)
            for c in range(NC):
                for b in range(3):
                    act.wait_ge(var_ready, NC + 3 + 3 * c + b)
                    s.activation(std[:, 0:CHUNK], var[:, 0:CHUNK], ACT.Sqrt).then_inc(std_ready, 1)
                for u in range(CHUNK):
                    t = c * CHUNK + u
                    act.wait_ge(x2T_ps, t + 1)
                    s.activation(x2T[:, :, :], bank[2][:, 0:D].rearrange("p (k n) -> p k n", k=K), ACT.Copy).then_inc(x2T_ready, 1)
                    act.wait_ge(lg_ps, t + 1)
                    s.activation(lg[:, t, :], bank[4][:, 0:E], ACT.Copy).then_inc(lg_ready, 1)
            act.wait_ge(rt_dve, 1)
            s.activation(pr[:, :, :], lg[:, :, :], ACT.Exp).then_inc(rt_act, 1)
            act.wait_ge(early_in, 32 * EARLY)
            act.wait_ge(late_in, 32 * (E - EARLY))
            act.sem_inc(split_low, 1)
            with act.Fori(0, E * WC // CC // 2) as i:
                for b in range(2):
                    c = 2 * i + b
                    s.activation(split_hi[b], wall[:, bass.ts(c, CC)], ACT.Copy, scale=UP).then_inc(split_cast, 1)
                for b in range(2):
                    c = 2 * i + b
                    held(act, passed, split_low, c + 2)
                    s.activation(wpair[:, bass.ts(c, CC), 0], split_hi[b], ACT.Copy).then_inc(weights_split, 1)
                held(act, passed, weights_split, 2 * i + 2)
            b1_cols = vcol[:, VB1:VB1 + E * KH].rearrange("p (e k) -> p e k", k=KH)
            act.wait_ge(rows_routed, 16 * TOPK * T)
            act.sem_inc(hidden_lo, 1)

            def activate(w):
                e = act.value_load(tile_e[0:1, bass.ds(w, 1)], min_val=0, max_val=E - 1)
                s.activation(bcol, b1_cols[:, e, :], ACT.Copy).then_inc(act_step, 1)
                held(act, passed, act_step, w + 1)
                held(act, passed, up_done, w + 1)
                held(act, passed, hidden_lo, w + 1)
                for m in range(KH):
                    ins = s.activation(h_f[:, m * P:(m + 1) * P], bank[m // 4][:, m % 4 * P:(m % 4 + 1) * P], ACT.Gelu,
                                       bias=bcol[:, m:m + 1], scale=1.0 / UP)
                ins.then_inc(activated, 1)
                held(act, passed, activated, w + 1)

            activate(0)
            s.activation(h_pair[0], h_f, ACT.Copy).then_inc(hidden_hi, 1)
            with act.Fori(0, W - 1) as i:
                activate(i + 1)
                held(act, passed, down_done, i + 1)
                s.activation(h_pair[0], h_f, ACT.Copy).then_inc(hidden_hi, 1)

        @block.tensor
        def _(pe):
            t_ = nc.tensor
            mm = t_.matmul

            def blocks(bk, n=K):
                return bank[bk][:, 0:n * P].rearrange("p (k n) -> p k n", k=n)

            pe.wait_ge(consts, 1)
            pe.wait_ge(vrows_in, 112)
            t_.transpose(bank[7][:, 0:NV], vrow[0:NV, :], ident[0:NV, 0:NV]).then_inc(vcol_ps, 1)
            pe.wait_ge(weights_in, 80)
            for k in range(K):
                for o in range(K):
                    ins = t_.transpose(bank[6][:, k * D + o * P:k * D + (o + 1) * P], gW_s[:, o, k * P:(k + 1) * P], ident[:, :])
            ins.then_inc(wT_ps, 1)
            pe.wait_ge(vcol_ok, 1)
            for q in range(K):
                for k in range(K):
                    ins = t_.transpose(bank[7][:, q * D + k * P:q * D + (k + 1) * P], wqkv_s[:, k, q * P:(q + 1) * P], ident[:, :])
            ins.then_inc(wT_ps, 1)
            pe.wait_ge(wT_ok, 2)

            for b in range(2):
                mm(bank[b][:, :], zeros[:, 0:P], zeros[:, :], start=True, stop=False)
            pe.sem_inc(h_ready, 1)

            def histogram(b):
                for h in range(2):
                    held(pe, passed, onehot_made, 2 * b + h + 1)
                    for j in range(GT):
                        ins = mm(bank[1][:, HI:2 * HI], hot_lo[h][:, j, :], hot_hi[h][:, j, :], start=False, stop=False, skip_group_check=True)
                    ins.then_inc(onehot_used, 1)

            with pe.Fori(0, T) as t:
                held(pe, passed, xs_ready, t + 1)
                for k in range(K):
                    ins = t_.transpose(bank[2][:, k * P:(k + 1) * P], xs[:, k * P:(k + 1) * P], ident[:, :])
                ins.then_inc(xT_ps, 1)
                histogram(t)
                for k in range(K):
                    mm(bank[0][:, k * D:(k + 1) * D], xs[:, k * P:(k + 1) * P], xs, start=False, stop=False, skip_group_check=True)
                    ins = mm(bank[1][:, k:k + 1], xs[:, k * P:(k + 1) * P], ones[:, 0:1], start=False, stop=False, skip_group_check=True)
                ins.then_inc(xs_used, 1)
                held(pe, passed, xT_ready, t + 1)
                held(pe, passed, h_ready, t + 1)
                for k in range(K):
                    ins = mm(bank[4][:, 0:D], xT_s[:, k, :], gWT[:, k, :], start=(k == 0), stop=(k == K - 1))
                ins.then_inc(h_ps, 1)
            histogram(T)
            for b in range(2):
                ins = mm(bank[b][:, :], zeros[:, 0:P], zeros[:, :], start=False, stop=True)
            ins.then_inc(hist_done, 1)

            pe.wait_ge(rows_in, 48)
            pe.wait_ge(sm_dve, 1)
            for k in range(K):
                ins = mm(bank[6][0:1, k * P:(k + 1) * P], scol[:, k:k + 1], ident[:, :], start=True, stop=True)
            ins.then_inc(sm_pe, 1)
            for k in range(K):
                ins = mm(bank[5][0:1, 0:D], scol[:, k:k + 1], wqkv_s[:, k, 2 * D:3 * D], start=(k == 0), stop=(k == K - 1))
            ins.then_inc(sm_pe, 1)
            pe.wait_ge(sm_act, 1)
            for k in range(K):
                for j in range(K):
                    mm(bank[7][:, k * D:(k + 1) * D], gram[:, j, k * P:(k + 1) * P], wqkv_s[:, j, 2 * D:3 * D], start=(j == 0), stop=False)
                ins = mm(bank[7][:, k * D:(k + 1) * D], srow[0:1, k * P:(k + 1) * P], bqkv_s[0:1, 2 * D:3 * D], start=False, stop=True)
            ins.then_inc(sm_pe, 1)
            pe.wait_ge(sm_act, 2)
            pe.wait_ge(sm_dve, 2)
            for q in range(K):
                a = slice(q * P, (q + 1) * P)
                for k in range(K):
                    mm(bank[6][:, a], wqkv_s[:, k, D + q * P:D + (q + 1) * P], xtv[:, k, a], start=(k == 0), stop=False)
                ins = mm(bank[6][:, a], bqkv_s[0:1, D + q * P:D + (q + 1) * P], urow[0:1, a], start=False, stop=True)
            ins.then_inc(sm_pe, 1)
            pe.wait_ge(sm_dve, 4)
            for q in range(K):
                ins = t_.transpose(bank[6][:, q * P:(q + 1) * P], atb[:, q, :], ident[:, :])
            ins.then_inc(sm_pe, 1)
            pe.wait_ge(sm_act, 5)
            for k in range(K):
                for q in range(K):
                    ins = mm(bank[7][:, k * D + q * P:k * D + (q + 1) * P], wqT[:, q, k * P:(k + 1) * P], atT[:, q, :], start=True, stop=True)
            ins.then_inc(sm_pe, 1)
            for q in range(K):
                ins = mm(bank[6][0:1, q * P:(q + 1) * P], vcol[:, VBQ + q:VBQ + q + 1], atT[:, q, :], start=True, stop=True)
            ins.then_inc(sm_pe, 1)
            pe.wait_ge(sm_act, 7)

            def group(g):
                held(pe, passed, groups_ready, g + 1)
                held(pe, passed, groups_added, g + 1)
                half = GT // 2
                for h in range(2):
                    held(pe, passed, hot_ready, 2 * g + h + 1)
                    for j in range(half):
                        ins = mm(bank[0][:, 0:D], hot[h][:, j, :], ring[:, g % SLOTS * GT + (h * half + j), :],
                                 start=(h == 0 and j == 0), stop=(h == 1 and j == half - 1))
                    ins.then_inc(halves_summed, 1)

            pe.sem_inc(m1_added, 1)
            pe.sem_inc(mix_added, 1)
            with pe.Fori(0, T) as t:
                held(pe, passed, xs_ready, t + (T + 1))
                for k in range(K):
                    ins = t_.transpose(bank[2][:, k * P:(k + 1) * P], xs[:, k * P:(k + 1) * P], ident[:, :])
                ins.then_inc(xT_ps, 1)
                group(t)
                held(pe, passed, xT_ready, t + (T + 1))
                held(pe, passed, m1_added, t + 1)
                for k in range(K):
                    mm(bank[5][:, 0:D], xT_s[:, k, :], wqa[:, k, :], start=(k == 0), stop=False)
                mm(bank[5][:, 0:D], ones[0:1, :], bqa[0:1, :], start=False, stop=True).then_inc(m1_ps, 1)
            pe.wait_ge(fc_split, NFC)
            pe.wait_ge(fc_bias, 1)
            fc1_pair = wfc_pair[:, 0:K * HID, :].rearrange("p (k n) h -> p k n h", k=K)
            fc2_pair = wfc_pair[:, K * HID:, :].rearrange("p (k n) h -> p k n h", k=KM)

            def mixer_up(t):
                held(pe, passed, hn_ready, t + 1)
                for k in range(K):
                    ins = t_.transpose(bank[4][:, k * P:(k + 1) * P], hn_s[:, k * P:(k + 1) * P], ident[:, :])
                ins.then_inc(hnT_ps, 1)

            def mixer_hidden(t):
                held(pe, passed, hnT_ready, t + 1)
                if not isinstance(t, int) or t > 0:
                    held(pe, passed, fc1_act, t)
                for m in range(KM):
                    n = 0
                    for k in range(K):
                        for wh, xh in PARTS:
                            n += 1
                            ins = mm(bank[2 + m // 4][:, m % 4 * P:(m % 4 + 1) * P], fc1_pair[:, k, m * P:(m + 1) * P, wh],
                                     hnT[xh][:, k * P:(k + 1) * P], start=(n == 1), stop=(n == K * len(PARTS)))
                ins.then_inc(fc1_ps, 1)

            def mixer_down(t):
                held(pe, passed, fc1_lo, t + 2)
                held(pe, passed, mix_added, t + 1)
                for m in range(KM):
                    for wh, xh in PARTS:
                        mm(bank[5][:, 0:D], h1[xh][:, m * P:(m + 1) * P], fc2_pair[:, m, :, wh], start=(m == 0 and wh == 0 and xh == 0), stop=False)
                mm(bank[5][:, 0:D], ones[0:1, :], bfc2_s[0:1, :], start=False, stop=True).then_inc(fc2_ps, 1)

            mixer_up(0)
            mixer_hidden(0)
            mixer_up(1)
            group(T)
            with pe.Fori(0, T - 2) as t:
                mixer_hidden(t + 1)
                mixer_up(t + 2)
                mixer_down(t)
                group(t + (T + 1))
            mixer_hidden(T - 1)
            mixer_down(T - 2)
            group(G - 3)
            mixer_down(T - 1)
            group(G - 2)
            group(G - 1)
            pe.wait_ge(windows_known, 1)
            wide = pe.value_load(wide_i[0:1, 0:1], min_val=0, max_val=1)
            with pe.If(wide):
                pe.sem_inc(wide_added, 1)
                with pe.Fori(0, G) as q:
                    held(pe, passed, wide_gathered, q * (16 * GT) + 16 * GT)
                    with pe.Fori(0, T) as b:
                        n = q * T + b
                        held(pe, passed, wide_hot, n + 1)
                        held(pe, passed, wide_added, n + 1)
                        for j in range(GT):
                            ins = mm(bank[0][:, 0:D], hot[j // (GT // 2)][:, j % (GT // 2), :], ring[:, j, :],
                                     start=(j == 0), stop=(j == GT - 1))
                        ins.then_inc(wide_summed, 1)

            for t in range(T):
                c, u = divmod(t, CHUNK)
                pe.wait_ge(x2_ready, c + 1)
                for k in range(K):
                    ins = t_.transpose(bank[2][:, k * P:(k + 1) * P], x2s[:, u, k * P:(k + 1) * P], ident[:, :])
                ins.then_inc(x2T_ps, 1)
                pe.wait_ge(x2T_ready, t + 1)
                if t:
                    pe.wait_ge(lg_ready, t)
                for k in range(K):
                    mm(bank[4][:, 0:E], x2T[:, k, :], wr_s[:, k, :], start=(k == 0), stop=False)
                mm(bank[4][:, 0:E], ones[0:1, :], br_s[:, :], start=False, stop=True).then_inc(lg_ps, 1)
            pe.wait_ge(rt_dve, 2)
            taken = tmpr.rearrange("p t e -> p (t e)")
            mm(bank[2][:, 0:T * E], before[:, :], taken, start=True, stop=True).then_inc(rt_pe, 1)
            mm(bank[3][:, 0:T * E], ones[:, :], taken, start=True, stop=True).then_inc(rt_pe, 1)

            def transpose_rows(w):
                held(pe, passed, xe_in, 16 * w + 16)
                for k in range(K):
                    ins = t_.transpose(bank[6][:, k * P:(k + 1) * P], xe[:, k * P:(k + 1) * P], ident[:, :])
                ins.then_inc(xe_transposed, 1)

            pairs = wpair.rearrange("p (e n) h -> p e n h", e=E)

            def up(w):
                e = pe.value_load(tile_e[0:1, bass.ds(w, 1)], min_val=0, max_val=E - 1)
                held(pe, passed, xeT_ready, w + 1)
                if not isinstance(w, int):
                    held(pe, passed, activated, w)
                for m in range(KH):
                    n = 0
                    for k in range(K):
                        for wh, xh in PARTS:
                            n += 1
                            c = k * H + m * P
                            ins = mm(bank[m // 4][:, m % 4 * P:(m % 4 + 1) * P], pairs[:, e, c:c + P, wh],
                                     xeT[xh][:, k * P:(k + 1) * P], start=(n == 1), stop=(n == K * len(PARTS)))
                ins.then_inc(up_done, 1)

            def down(w):
                e = pe.value_load(tile_e[0:1, bass.ds(w, 1)], min_val=0, max_val=E - 1)
                held(pe, passed, hidden_lo, w + 2)
                held(pe, passed, y_ready, w + TOPK)
                n = 0
                for m in range(KH):
                    for wh, xh in PARTS:
                        n += 1
                        c = K * H + m * D
                        ins = mm(bank[7][:, 0:D], h_pair[xh][:, m * P:(m + 1) * P], pairs[:, e, c:c + D, wh],
                                 start=(n == 1), stop=(n == KH * len(PARTS)))
                ins.then_inc(down_done, 1)

            pe.wait_ge(weights_split, E * WC // CC)
            transpose_rows(0)
            up(0)
            transpose_rows(1)
            with pe.Fori(0, W - 1) as i:
                up(i + 1)
                transpose_rows(i + 2)
                down(i)
            down(W - 1)

        @block.vector
        def _(dve):
            v = nc.vector
            step = Chain(dve, dve_step, passed)
            dve.wait_ge(iotas, 2)
            v.tensor_copy(iota_f[:, :], iota_i)
            v.tensor_copy(iota_b[:, :], iota_i)
            v.memset(ones[:, :], 1.0)
            v.memset(zeros[:, :], 0.0)
            step(v.tensor_copy(iotap[:, :], iotap_i[:, :]))
            v.tensor_scalar(valid[:, :], iotap[:, :], float(LAST), None, ALU.is_lt)
            v.tensor_scalar(before[:, :], iota_f[:, :], iotap[:, :], None, ALU.is_gt)
            v.tensor_scalar(ident[:, :], iota_f[:, :], iotap[:, :], None, ALU.is_equal).then_inc(consts, 1)

            def statistics(n, inv_n=1.0 / D):
                me, ve, mo, vo = (st[:, 0:n, q] for q in (1, 2, 4, 5))
                v.tensor_tensor(small[:, 0, 0:n], me, mo, ALU.add)
                v.tensor_tensor(small[:, 1, 0:n], me, mo, ALU.subtract)
                step(v.tensor_tensor(small[:, 2, 0:n], ve, vo, ALU.add))
                v.tensor_scalar(mean[:, 0:n], small[:, 0, 0:n], 0.5, None, ALU.mult)
                v.scalar_tensor_tensor(small[:, 3, 0:n], small[:, 1, 0:n], 0.25, small[:, 1, 0:n], ALU.mult, ALU.mult)
                step(v.tensor_scalar(small[:, 2, 0:n], small[:, 2, 0:n], inv_n, EPS, ALU.mult, ALU.add))
                v.tensor_tensor(var[:, 0:n], small[:, 2, 0:n], small[:, 3, 0:n], ALU.add).then_inc(var_ready, 1)

            def normalise(dest, source, n):
                for u in range(n):
                    ins = v.tensor_scalar(dest[:, u, :], source[:, u, :], mean[:, u:u + 1], rstd[:, u:u + 1],
                                          ALU.subtract, ALU.mult)
                return ins

            dve.wait_ge(edges_in, 96)
            lo3 = lo_f[:, :, :].rearrange("p g j -> p (g j)")
            step(v.tensor_scalar(tmp_i, dst_i, P - 1, None, ALU.bitwise_and))
            v.tensor_copy(lo3, tmp_i)
            step(v.tensor_copy(dst_f[:, :, :].rearrange("p g j -> p (g j)"), dst_i))
            step(v.tensor_scalar(tmp_i, dst_i, 7, None, ALU.logical_shift_right))
            step(v.tensor_copy(hi_f, tmp_i))
            v.tensor_copy(hi_b[:, :, :].rearrange("p g j -> p (g j)"), hi_f)
            step(v.tensor_scalar(hi_f, hi_f, float(T), float(P), ALU.is_ge, ALU.mult))
            step(v.tensor_tensor(lo3, lo3, hi_f, ALU.add))
            v.tensor_copy(lo_b[:, :, :].rearrange("p g j -> p (g j)"), lo3)
            step(v.tensor_reduce(gm[:, 0, :], dst_f[:, :, :], AX_X, ALU.min))
            v.tensor_scalar(gm[:, 0, :], gm[:, 0, :], -1.0, None, ALU.mult)
            step(v.tensor_scalar(hi_f, dst_f[:, :, :].rearrange("p g j -> p (g j)"), float(N), None, ALU.is_lt))
            step(v.tensor_tensor(hi_f, hi_f, dst_f[:, :, :].rearrange("p g j -> p (g j)"), ALU.mult))
            v.tensor_reduce(gm[:, 1, :], hi_f.rearrange("p (g j) -> p g j", j=GT), AX_X, ALU.max).then_inc(extremes, 1)

            dve.wait_ge(rows_in, 48)
            v.tensor_scalar(bfc2_s[0:1, :], bfc2_s[0:1, :], UP, None, ALU.mult).then_inc(fc_bias, 1)

            dve.wait_ge(x_in, 32)
            for c in range(NC):
                xc = xn[:, c * CHUNK:(c + 1) * CHUNK, :]
                for u in range(CHUNK):
                    ins = v.bn_stats(st[:, u, :], xc[:, u, :])
                step(ins)
                me, ve, mo, vo = (st[:, 0:CHUNK, q] for q in (1, 2, 4, 5))
                n = CHUNK
                vc = var[:, c * n:(c + 1) * n]
                v.tensor_tensor(small[:, 0, 0:n], me, mo, ALU.add)
                v.tensor_tensor(small[:, 1, 0:n], me, mo, ALU.subtract)
                step(v.tensor_tensor(small[:, 2, 0:n], ve, vo, ALU.add))
                v.tensor_scalar(mean[:, 0:n], small[:, 0, 0:n], 0.5, None, ALU.mult)
                v.scalar_tensor_tensor(small[:, 3, 0:n], small[:, 1, 0:n], 0.25, small[:, 1, 0:n], ALU.mult, ALU.mult)
                step(v.tensor_scalar(small[:, 2, 0:n], small[:, 2, 0:n], 1.0 / D, EPS, ALU.mult, ALU.add))
                v.tensor_tensor(vc, small[:, 2, 0:n], small[:, 3, 0:n], ALU.add).then_inc(var_ready, 1)
                dve.wait_ge(std_ready, c + 1)
                step(v.reciprocal(rstd[:, 0:n], std[:, c * n:(c + 1) * n]))
                normalise(xc, xc, n).then_inc(ln1_done, 1)

            for c in range(NFC):
                a = slice(c * CC, (c + 1) * CC)
                dve.wait_ge(fc_hi, c + 1)
                v.scalar_tensor_tensor(wfc_pair[:, a, 1], wfc[:, a], UP, wfc_hi[0], ALU.mult, ALU.subtract).then_inc(fc_lo, 1)

            dve.sem_inc(onehot_used, 2)
            step(v.tensor_scalar(blk_f[:, :], gm[:, 0, :], -1.0, None, ALU.mult))
            with dve.Fori(0, G // 2) as b:
                for h in range(2):
                    held(dve, passed, onehot_used, 2 * b + h + 1)
                    io = iota_b[:, :].unsqueeze(1).to_broadcast([P, GT, P])
                    lo_g = lo_b[:, 2 * b + h, :].unsqueeze(2).to_broadcast([P, GT, P])
                    hi_g = hi_b[:, 2 * b + h, :].unsqueeze(2).to_broadcast([P, GT, HI])
                    v.tensor_tensor(hot_lo[h], lo_g, io, ALU.is_equal)
                    v.tensor_tensor(hot_hi[h], hi_g, io[:, :, 0:HI], ALU.is_equal).then_inc(onehot_made, 1)

            dve.wait_ge(hist_done, 1)
            v.tensor_scalar(var[:, :], bank[1][:, HI:HI + T], 1.0, None, ALU.add).then_inc(var_ready, 1)
            dve.wait_ge(std_ready, NC + 1)
            step(v.reciprocal(dinv[:, :], std[:, :]))
            dve.wait_ge(h_ready, T + 1)
            for c in range(NC):
                a = slice(c * CHUNK, (c + 1) * CHUNK)
                v.tensor_tensor(acc[:, a, :], acc[:, a, :], dinv[:, a].unsqueeze(2).to_broadcast([P, CHUNK, D]),
                                ALU.mult).then_inc(table_ready, 1)
            dve.wait_ge(extremes_all, 1)
            step(v.tensor_scalar(blk_f[:, :], gall[:, 0, :], -1.0, None, ALU.mult))
            step(v.tensor_copy(blk_i[:, :], blk_f[:, :]))
            step(v.tensor_scalar(blk_i[:, :], blk_i[:, :], 7, None, ALU.logical_shift_right))
            step(v.tensor_copy(mhi[:, :], blk_i[:, :]))
            step(v.scalar_tensor_tensor(blk_f[:, :], mhi[:, :], -float(P), blk_f[:, :], ALU.mult, ALU.add))
            step(v.tensor_scalar(mlo[:, :], blk_f[:, :], iotap[:, :], None, ALU.is_gt))
            step(v.tensor_scalar(mhi[:, :], mlo[:, :], -1.0, 1.0, ALU.mult, ALU.add))
            step(v.tensor_tensor(gm[:, 0, :], gall[:, 0, :], gall[:, 1, :], ALU.add))
            step(v.tensor_reduce(wide_f[:, :], gm[:, 0, :], AX_X, ALU.max))
            step(v.tensor_scalar(wide_f[:, :], wide_f[:, :], float(P), None, ALU.is_ge))
            v.tensor_copy(wide_i[:, :], wide_f[:, :]).then_inc(windows_known, 1)

            v.tensor_copy(scol[:, :], bank[1][:, 0:K])
            v.tensor_copy(gram, bank[0][:, :].rearrange("p (k n) -> p k n", k=K)).then_inc(sm_dve, 1)
            dve.wait_ge(sm_pe, 2)
            v.scalar_tensor_tensor(urow[0:1, :], bqkv_s[0:1, 2 * D:3 * D], float(N), bank[5][0:1, 0:D],
                                   ALU.mult, ALU.add).then_inc(sm_dve, 1)
            v.memset(atb, 0.0)
            dve.wait_ge(sm_pe, 4)
            for q in range(2):
                a = slice(q * HD, (q + 1) * HD)
                ins = v.tensor_scalar(att[a, :, :], bank[6][a, 0:K * P].rearrange("p (k n) -> p k n", k=K)[:, :, a],
                                      SCALE, None, ALU.mult)
            step(ins)
            step(v.tensor_reduce(mneg[:, :], att, AX_X, ALU.max))
            v.tensor_scalar(mneg[:, :], mneg[:, :], -1.0, None, ALU.mult).then_inc(sm_dve, 1)
            dve.wait_ge(sm_act, 4)
            step(v.reciprocal(msum[:, :], msum[:, :]))
            step(v.tensor_tensor(att, atb[:, :, 0:HD], msum[:, :].unsqueeze(2).to_broadcast([P, K, HD]), ALU.mult))
            step(v.memset(atb, 0.0))
            for q in range(2):
                a = slice(q * HD, (q + 1) * HD)
                ins = v.tensor_copy(atb[a, :, a], att[a, :, :])
            ins.then_inc(sm_dve, 1)

            def window_hot(g, h):
                held(dve, passed, halves_summed, 2 * SLOTS + 2 * g + h - 1)
                v.tensor_tensor(hot[h], lo_f[:, g, h * (GT // 2):(h + 1) * (GT // 2)].unsqueeze(2).to_broadcast([P, GT // 2, P]),
                                iota_f[:, :].unsqueeze(1).to_broadcast([P, GT // 2, P]), ALU.is_equal).then_inc(hot_ready, 1)

            def window_hots(g):
                for h in range(2):
                    window_hot(g, h)

            def add_window(g):
                held(dve, passed, halves_summed, 2 * SLOTS + 2 * g + 2)
                held(dve, passed, groups_added, g + 1)
                b = dve.value_load(blk_i[0:1, bass.ds(g, 1)], min_val=0, max_val=T - 1)
                v.scalar_tensor_tensor(acc[:, b, :], bank[0][:, 0:D], mhi[:, bass.ds(g, 1)], acc[:, b, :], ALU.mult, ALU.add)
                v.scalar_tensor_tensor(acc[:, b + 1, :], bank[0][:, 0:D], mlo[:, bass.ds(g, 1)], acc[:, b + 1, :],
                                       ALU.mult, ALU.add).then_inc(groups_added, 1)

            dve.sem_inc(groups_added, 1)
            dve.wait_ge(table_stored, 16 * NC)
            window_hots(0)
            with step.loop(T, 1) as t:
                add_window(t)
                window_hots(t + 1)
                held(dve, passed, m1_ps, t + 1)
                step(v.tensor_tensor(xn[:, t, :], bank[5][:, 0:D], xn[:, t, :], ALU.add))
                v.bn_stats(st[:, t, :], xn[:, t, :]).then_inc(m1_added, 1)
            dve.wait_ge(m1_added, T + 1)
            statistics(T)
            dve.wait_ge(std_ready, NC + 2)
            step(v.reciprocal(rstd[:, :], std[:, :]))
            def normal_tile(t):
                v.tensor_scalar(hn_s, xn[:, t, :], mean[:, bass.ds(t, 1)], rstd[:, bass.ds(t, 1)], ALU.subtract, ALU.mult).then_inc(hn_ready, 1)

            def split_tile(t, last=False):
                held(dve, passed, hnT_ps, t + 1)
                for k in range(K):
                    ins = v.tensor_scalar(hnT_f[:, k * P:(k + 1) * P], bank[4][:, k * P:(k + 1) * P],
                                          vcol[:, VNG + k:VNG + k + 1], vcol[:, VNB + k:VNB + k + 1], ALU.mult, ALU.add)
                step(ins)
                step(v.tensor_copy(hnT[0], hnT_f))
                v.tensor_tensor(hnT[1], hnT_f, hnT[0], ALU.subtract).then_inc(hnT_ready, 1)

            def low_hidden(t):
                held(dve, passed, fc1_hi, t + 1)
                v.tensor_tensor(h1[1], h1_f, h1[0], ALU.subtract).then_inc(fc1_lo, 1)

            def add_mixer(t):
                held(dve, passed, fc2_ps, t + 1)
                v.scalar_tensor_tensor(xn[:, t, :], bank[5][:, 0:D], 1.0 / UP, xn[:, t, :], ALU.mult, ALU.add).then_inc(mix_added, 1)

            dve.sem_inc(fc1_lo, 1)
            normal_tile(0)
            split_tile(0)
            normal_tile(1)
            split_tile(1)
            normal_tile(2)
            low_hidden(0)
            with step.loop(T - 3, 2) as i:
                add_window(i + T)
                window_hots(i + (T + 1))
                split_tile(i + 2)
                normal_tile(i + 3)
                add_mixer(i)
                low_hidden(i + 1)
            add_window(2 * T - 3)
            window_hots(2 * T - 2)
            split_tile(T - 1)
            add_mixer(T - 3)
            low_hidden(T - 2)
            add_window(2 * T - 2)
            window_hots(2 * T - 1)
            add_mixer(T - 2)
            low_hidden(T - 1)
            add_window(2 * T - 1)
            window_hots(2 * T)
            add_mixer(T - 1)
            window_hots(G - 1)
            add_window(G - 2)
            add_window(G - 1)
            dve.wait_ge(groups_added, G + 1)
            dve.wait_ge(windows_known, 1)
            wide = dve.value_load(wide_i[0:1, 0:1], min_val=0, max_val=1)
            with dve.If(wide):
                dve.wait_ge(wide_reloaded, 16)
                with dve.Fori(0, G) as q:
                    v.tensor_copy(shifted, dst_f[:, q, :]).then_inc(wide_shifted, 1)
                    with dve.Fori(0, T) as b:
                        n = q * T + b
                        held(dve, passed, wide_shifted, n + q + 1)
                        for h in range(2):
                            ins = v.tensor_tensor(hot[h], shifted[:, h * (GT // 2):(h + 1) * (GT // 2)].unsqueeze(2).to_broadcast([P, GT // 2, P]),
                                                  iota_f[:, :].unsqueeze(1).to_broadcast([P, GT // 2, P]), ALU.is_equal)
                        ins.then_inc(wide_hot, 1)
                        held(dve, passed, wide_summed, n + 2)
                        v.tensor_tensor(acc[:, b, :], acc[:, b, :], bank[0][:, 0:D], ALU.add).then_inc(wide_added, 1)
                        held(dve, passed, wide_added, n + 2)
                        v.tensor_scalar(shifted, shifted, -float(P), None, ALU.add).then_inc(wide_shifted, 1)
                    held(dve, passed, wide_shifted, q * (T + 1) + (T + 1))
            v.tensor_copy(wide_f[:, :], iotap[:, :]).then_inc(aggregated, 1)

            dve.wait_ge(groups_added, G + 1)
            dve.wait_ge(mix_added, T + 1)
            dve.wait_ge(bcast_in, 48)
            k = NC + 2
            for c in range(NC):
                a = slice(c * CHUNK, (c + 1) * CHUNK)
                z, xc = acc[:, a, :], xn[:, a, :]

                def wide(row):
                    return row[:, :].unsqueeze(1).to_broadcast([P, CHUNK, D])

                step(v.tensor_tensor(z, z, dinv[:, a].unsqueeze(2).to_broadcast([P, CHUNK, D]), ALU.mult))
                step(v.tensor_tensor(z, z, wide(gb_b), ALU.add))

                def layer_norm(dest, source, k):
                    for u in range(CHUNK):
                        ins = v.bn_stats(st[:, u, :], source[:, u, :])
                    step(ins)
                    statistics(CHUNK)
                    dve.wait_ge(std_ready, k)
                    step(v.reciprocal(rstd[:, 0:CHUNK], std[:, 0:CHUNK]))
                    return normalise(dest, source, CHUNK)

                k += 1
                step(layer_norm(z, z, k))
                step(v.tensor_tensor(z, z, wide(gg_b), ALU.mult))
                step(v.tensor_tensor(z, z, wide(gbe_b), ALU.add))
                step(v.scalar_tensor_tensor(xc, z, 0.0, xc, ALU.max, ALU.add))
                dve.wait_ge(xre_in, 16 * (c + 1) if c < NC - 1 else 16 * (NC + 1))
                v.tensor_tensor(xc, xc, xre[:, :, :], ALU.add).then_inc(xre_used, 1)
                dve.wait_ge(xre_used, c + 1)
                k += 1
                if c:
                    dve.wait_ge(x2T_ps, c * CHUNK)
                layer_norm(x2s, xc, k).then_inc(x2_ready, 1)
                dve.wait_ge(x2_ready, c + 1)
                k += 1
                step(layer_norm(z, x2s, k))

            dve.wait_ge(lg_ready, T)

            def per_tile(a):
                return a[:, :].unsqueeze(2).to_broadcast([P, T, E])

            io8 = iota_f[:, 0:E].unsqueeze(1).to_broadcast([P, T, E])
            step(v.tensor_reduce(r1[:, :], lg[:, :, :], AX_X, ALU.max))
            v.tensor_tensor(lg[:, :, :], lg[:, :, :], per_tile(r1), ALU.subtract).then_inc(rt_dve, 1)
            dve.wait_ge(rt_act, 1)
            step(v.tensor_reduce(r1[:, :], pr[:, :, :], AX_X, ALU.add))
            step(v.reciprocal(r1[:, :], r1[:, :]))
            step(v.tensor_tensor(pr[:, :, :], pr[:, :, :], per_tile(r1), ALU.mult))

            def largest(mask, top):
                step(v.tensor_reduce(top[:, :], pr[:, :, :], AX_X, ALU.max))
                step(v.tensor_tensor(tmpr, pr[:, :, :], per_tile(top), ALU.is_lt))
                step(v.scalar_tensor_tensor(tmpr, tmpr, float(E), io8, ALU.mult, ALU.add))
                step(v.tensor_reduce(r2[:, :], tmpr, AX_X, ALU.min))
                step(v.tensor_tensor(mask[:, :, :], io8, per_tile(r2), ALU.is_equal))

            largest(m1, w1c)
            step(v.scalar_tensor_tensor(pr[:, :, :], m1[:, :, :], -2.0, pr[:, :, :], ALU.mult, ALU.add))
            largest(m2, w2c)
            step(v.tensor_tensor(r1[:, :], w1c[:, :], w2c[:, :], ALU.add))
            step(v.reciprocal(r1[:, :], r1[:, :]))
            v.tensor_tensor(w1c[:, :], w1c[:, :], r1[:, :], ALU.mult)
            v.tensor_tensor(w2c[:, :], w2c[:, :], r1[:, :], ALU.mult)
            v.tensor_scalar(m1[:, T - 1, :], m1[:, T - 1, :], valid[:, :], None, ALU.mult)
            step(v.tensor_scalar(m2[:, T - 1, :], m2[:, T - 1, :], valid[:, :], None, ALU.mult))
            v.tensor_tensor(tmpr, m1[:, :, :], m2[:, :, :], ALU.add).then_inc(rt_dve, 1)
            dve.wait_ge(rt_pe, 2)
            cv = bank[3][:, 0:T * E].rearrange("p (t e) -> p e t", t=T)
            step(v.tensor_copy(cnt, cv))
            for e in range(E):
                ins = v.tensor_tensor_scan(inc[:, e, :], ones[:, 0:T], cnt[:, e, :], 0.0, ALU.mult, ALU.add)
            step(ins)
            step(v.tensor_scalar(tl[:, 0, :], inc[:, :, T - 1], float(P - 1), None, ALU.add))
            step(v.tensor_copy(tl_i[:, :], tl[:, 0, :]))
            step(v.tensor_scalar(tl_i[:, :], tl_i[:, :], 7, None, ALU.logical_shift_right))
            step(v.tensor_copy(tl[:, 1, :], tl_i[:, :]))
            step(v.tensor_tensor_scan(tl[:, 2, :], ones[:, 0:E], tl[:, 1, :], 0.0, ALU.mult, ALU.add))
            step(v.tensor_tensor(tl[:, 3, :], tl[:, 2, :], tl[:, 1, :], ALU.subtract))
            step(v.tensor_tensor(inc, inc, cnt, ALU.subtract))
            step(v.scalar_tensor_tensor(inc, tl[:, 3, :].unsqueeze(2).to_broadcast([P, E, T]), float(P), inc, ALU.mult, ALU.add))
            step(v.tensor_tensor(pos, bank[2][:, 0:T * E].rearrange("p (t e) -> p t e", t=T),
                                 inc.rearrange("p e t -> p t e"), ALU.add))
            for j, m in enumerate((m1, m2)):
                step(v.tensor_tensor(m[:, :, :], m[:, :, :], pos, ALU.mult))
                step(v.tensor_reduce(r1[:, :], m[:, :, :], AX_X, ALU.add))
                step(v.tensor_copy(pos_i[:, j, :], r1[:, :]))
            step(v.tensor_scalar(tile_f[:, :], iota_f[:, 0:W + 1], tl[:, 3, 1:2], None, ALU.is_ge))
            for e in range(2, E):
                step(v.scalar_tensor_tensor(tile_f[:, :], iota_f[:, 0:W + 1], tl[:, 3, e:e + 1], tile_f[:, :], ALU.is_ge, ALU.add))
            v.tensor_copy(tile_e[:, :], tile_f[:, :]).then_inc(pos_ready, 1)

            dve.wait_ge(pos_ready, 1)
            with dve.Fori(0, E * WC // CC // 2) as i:
                for b in range(2):
                    c = 2 * i + b
                    held(dve, passed, split_cast, c + 1)
                    v.scalar_tensor_tensor(wpair[:, bass.ts(c, CC), 1], wall[:, bass.ts(c, CC)], UP, split_hi[b], ALU.mult, ALU.subtract).then_inc(split_low, 1)

            lg_cols = vcol[:, VLG:VLG + E * K].rearrange("p (e k) -> p e k", k=K)
            lb_cols = vcol[:, VLB:VLB + E * K].rearrange("p (e k) -> p e k", k=K)
            dve.wait_ge(rows_routed, 16 * TOPK * T)

            def expert_input(w):
                e = dve.value_load(tile_e[0:1, bass.ds(w, 1)], min_val=0, max_val=E - 1)
                v.tensor_copy(gcol[:, 0:K], lg_cols[:, e, :])
                step(v.tensor_copy(gcol[:, K:2 * K], lb_cols[:, e, :]))
                held(dve, passed, xe_transposed, w + 2)
                for dest in (xeT[0], xeT_f):
                    for q in range(K):
                        ins = v.tensor_scalar(dest[:, q * P:(q + 1) * P], bank[6][:, q * P:(q + 1) * P], gcol[:, q:q + 1],
                                              gcol[:, K + q:K + q + 1], ALU.mult, ALU.add)
                step(ins)
                v.tensor_tensor(xeT[1], xeT_f, xeT[0], ALU.subtract).then_inc(xeT_ready, 1)

            def low_part(w):
                held(dve, passed, hidden_hi, w + 1)
                v.tensor_tensor(h_pair[1], h_f, h_pair[0], ALU.subtract).then_inc(hidden_lo, 1)

            def finish_tile(w, first=False):
                held(dve, passed, down_done, w + 1)
                held(dve, passed, bias_in, 16 * w + 16)
                if not first:
                    held(dve, passed, y_stored, 16 * w)
                v.scalar_tensor_tensor(ys, bank[7][:, 0:D], 1.0 / UP, b2t[:, w % 2, :], ALU.mult, ALU.add).then_inc(y_ready, 1)

            dve.sem_inc(y_ready, TOPK)
            expert_input(0)
            expert_input(1)
            low_part(0)
            expert_input(2)
            finish_tile(0, True)
            low_part(1)
            with step.loop(W - 2, 2) as i:
                expert_input(i + 3)
                finish_tile(i + 1)
                low_part(i + 2)
            finish_tile(W - 1)

            for c in range(NC):
                a = slice(c * CHUNK, (c + 1) * CHUNK)
                dve.wait_ge(picked[c], 16 * TOPK * CHUNK)
                for y, wc in ((y1, w1c), (y2, w2c)):
                    v.tensor_tensor(y[:, a, :], y[:, a, :], wc[:, a].unsqueeze(2).to_broadcast([P, CHUNK, D]), ALU.mult)
                step(v.tensor_copy(r1[:, 0:1], r2[:, 0:1]))
                step(v.tensor_tensor(xn[:, a, :], xn[:, a, :], y1[:, a, :], ALU.add))
                v.tensor_tensor(xn[:, a, :], xn[:, a, :], y2[:, a, :], ALU.add).then_inc(out_ready, 1)


INS = ['x', 'src', 'dst', 'L0_gnn_W', 'L0_gnn_b', 'L0_gnn_gamma', 'L0_gnn_beta', 'L0_mix_w_qkv', 'L0_mix_b_qkv',
       'L0_mix_norm_g', 'L0_mix_norm_b', 'L0_mix_w_fc1', 'L0_mix_b_fc1', 'L0_mix_w_fc2', 'L0_mix_b_fc2',
       'L0_ffn_Wr', 'L0_ffn_br', 'L0_ffn_ln_g', 'L0_ffn_ln_b', 'L0_ffn_W1', 'L0_ffn_b1', 'L0_ffn_W2', 'L0_ffn_b2']


def kernel(**inputs):
    import numpy as np
    import concourse.bacc as bacc
    from concourse.bass_utils import run_bass_kernel_spmd

    nc = bacc.Bacc("TRN2", target_bir_lowering=False, num_devices=1)
    arrays, args = {}, []
    for name in INS:
        a = np.ascontiguousarray(inputs[name])
        arrays[f"in_{name}"] = a
        args.append(nc.dram_tensor(f"in_{name}", a.shape, mybir.dt.from_np(a.dtype), kind="ExternalInput").ap())
    args.append(nc.dram_tensor("out_x", inputs["x"].shape, F32, kind="ExternalOutput").ap())
    gps_layer(nc, *args)
    r = run_bass_kernel_spmd(nc, [arrays], core_ids=[0])
    return r.results[0]["out_x"]
```

```python
from contextlib import ExitStack, contextmanager

import concourse.bass as bass
from concourse import mybir

F32 = mybir.dt.float32
BF16 = mybir.dt.bfloat16
F16 = mybir.dt.float16
I32 = mybir.dt.int32
U32 = mybir.dt.uint32
ALU = mybir.AluOpType
ACT = mybir.ActivationFunctionType
AX_X = mybir.AxisListType.X
RMAX = bass.bass_isa.ReduceOp.max

P = 128
EPS = 1e-5
CHUNK = 5
GT = 8
UP = 256.0
PARTS = ((0, 0), (0, 1), (1, 0))
AHEAD = 2
UNROLL = 4
SLOTS = 4


def held(eng, passed, sem, value):
    eng.wait_ge(sem, value)
    if not isinstance(value, int):
        eng.sem_inc(passed, 1)


class Chain:

    def __init__(self, eng, sem, passed):
        self.eng, self.sem, self.passed = eng, sem, passed
        self.base = 0
        self.n = 0

    def __call__(self, ins):
        ins.then_inc(self.sem, 1)
        self.n += 1
        held(self.eng, self.passed, self.sem, self.base + self.n)

    @contextmanager
    def loop(self, trips, per):
        start = self.n
        with self.eng.Fori(0, trips) as i:
            self.base, self.n = i * per + start, 0
            yield i
            assert self.n == per, (self.n, per)
        self.base, self.n = 0, start + trips * per


def gps_layer(nc, x, src, dst, gW, gb, ggamma, gbeta, wqkv, bqkv, ng, nb, wfc1, bfc1, wfc2, bfc2,
              Wr, br, lng, lnb, W1, b1, W2, b2, out):
    N, D = x.shape
    NE = src.shape[0]
    E, _, H = W1.shape
    HID = wfc1.shape[1]
    K = D // P
    KM = HID // P
    KH = H // P
    T = -(-N // P)
    LAST = N - (T - 1) * P
    NC = T // CHUNK
    G = -(-NE // (P * GT))
    EG = P * GT
    EL = NE - (G - 1) * EG
    EROW, EREM = EL // GT, EL % GT
    HALF = P // 2
    HCOLS = 2 * T
    HAT = 64
    PAD_DST = P * (T + 7) + P - 1
    TOPK = 2
    HD = 64
    SCALE = float(HD) ** -0.5
    W = TOPK * N // P + E
    WC = K * H + KH * D
    EARLY = 1
    assert (W - 4) % UNROLL == 0 and W % 2 == 0
    assert T == NC * CHUNK and D == K * P and 2 * T + 2 == G and G % SLOTS == 0 and G // 2 == T + 1

    table = nc.dram_tensor("h_table", (T * P, D), F32).ap()
    slots = nc.dram_tensor("slot_rows", (W * P, D + 1), F32).ap()
    yrows = nc.dram_tensor("expert_rows", (TOPK * T * P + TOPK * P, D), F32).ap()

    with ExitStack() as ctx:
        ctx.enter_context(nc.allow_non_contiguous_dma("index lists of eight edges a partition"))

        def sb(name, shape, dt=F32):
            return ctx.enter_context(nc.sbuf_tensor(name, shape, dt))

        def sem(name):
            return ctx.enter_context(nc.semaphore(name))

        wall = sb("wall", [P, E * WC])
        acc = sb("acc", [P, T + 1, D])
        xn = sb("xn", [P, T, D])
        cursor = [EARLY * WC]

        def room(cols):
            a = cursor[0]
            cursor[0] += cols
            assert cursor[0] <= E * WC
            return wall[:, a:a + cols]

        ring = room(SLOTS * GT * D).rearrange("p (s c) -> p s c", s=SLOTS * GT)
        hot = [room(GT // 2 * P).rearrange("p (j n) -> p j n", j=GT // 2) for _ in range(2)]
        hot_lo = [room(GT * HALF // 2).bitcast(BF16).rearrange("p (j n) -> p j n", j=GT) for _ in range(2)]
        hot_hi = [room(GT * HCOLS // 2).bitcast(BF16).rearrange("p (j n) -> p j n", j=GT) for _ in range(2)]
        wqkv_s = room(K * 3 * D).rearrange("p (k n) -> p k n", k=K)
        wfc = room(K * HID + KM * D)
        wfc1_s = wfc[:, 0:K * HID].rearrange("p (k n) -> p k n", k=K)
        wfc2_s = wfc[:, K * HID:].rearrange("p (k n) -> p k n", k=KM)
        wfc_pair = wfc.bitcast(F16).rearrange("p (n h) -> p n h", h=2)
        wfc_hi = [room(1024 // 2).bitcast(F16) for _ in range(1)]
        gW_s = room(K * D).rearrange("p (k n) -> p k n", k=K)
        gWT = room(K * D).rearrange("p (k n) -> p k n", k=K)
        wqT = room(K * D).rearrange("p (k n) -> p k n", k=K)
        gram = room(K * D).rearrange("p (k n) -> p k n", k=K)
        xtv = room(K * D).rearrange("p (k n) -> p k n", k=K)
        wqa = room(K * D).rearrange("p (k n) -> p k n", k=K)
        xs = [room(D) for _ in range(2)]
        xT_s = [room(D).rearrange("p (k n) -> p k n", k=K) for _ in range(2)]
        hn_s = room(D)
        hnT_f = room(D)
        hnT = [room(D // 2).bitcast(F16) for _ in range(2)]
        h1_f = room(HID)
        h1 = [room(HID // 2).bitcast(F16) for _ in range(2)]
        att = room(K * HD).rearrange("p (k n) -> p k n", k=K)
        atb = room(K * P).rearrange("p (k n) -> p k n", k=K)
        atT = room(K * P).rearrange("p (k n) -> p k n", k=K)
        dst_i = room(G * GT).bitcast(I32)
        tmp_i = room(G * GT).bitcast(I32)
        hi_f = room(G * GT)

        NV = 2 * K + KM + K + 2 * E * K + E * KH
        vrow = room(P)
        VNG, VNB, VF1, VBQ, VLG, VLB, VB1 = 0, K, 2 * K, 2 * K + KM, 3 * K + KM, 3 * K + KM + E * K, 3 * K + KM + 2 * E * K
        vcol = sb("vcol", [P, NV])
        bqkv_s = room(3 * D)
        bfc2_s = room(D)
        srow = room(D)
        urow = room(D)
        bqa = room(D)

        ident = sb("ident", [P, P])
        iota_i = room(P).bitcast(I32)
        iotap_i = sb("iotap_i", [P, 1], I32)
        iota_f = sb("iota_f", [P, P])
        iota_b = sb("iota_b", [P, P], BF16)
        iotap = sb("iotap", [P, 1])
        before = sb("before", [P, P])
        ones = sb("ones", [P, P])
        zeros = room(512)
        blank = room(D + 1)
        twice = sb("twice", [HALF, P])
        counts_s = sb("counts_s", [HALF, HCOLS])
        gb_b = sb("gb_b", [P, D])
        gg_b = sb("gg_b", [P, D])
        gbe_b = sb("gbe_b", [P, D])
        wr_s = sb("wr_s", [P, K, E])
        br_s = sb("br_s", [1, E])
        src_i = room(G * GT).bitcast(I32)
        lo_f = room(G * GT).rearrange("p (g j) -> p g j", j=GT)
        lo_b = room(G * GT // 2).bitcast(BF16).rearrange("p (g j) -> p g j", j=GT)
        hi_b = room(G * GT // 2).bitcast(BF16).rearrange("p (g j) -> p g j", j=GT)
        dst_f = room(G * GT).rearrange("p (g j) -> p g j", j=GT)
        shifted = room(GT)
        idx_s = sb("idx_s", [P, SLOTS, GT], I32)
        gm = sb("gm", [P, 2, G])
        gall = sb("gall", [P, 2, G])
        blk_i = sb("blk_i", [P, G], I32)
        blk_f = sb("blk_f", [P, G])
        wide_f = sb("wide_f", [P, 1])
        wide_i = sb("wide_i", [P, 1], I32)
        mhi = sb("mhi", [P, G])
        mlo = sb("mlo", [P, G])
        scol = sb("scol", [P, K])
        deg_root = sb("deg_root", [P, T])
        dinv = sb("dinv", [P, T])
        st = sb("st", [P, T, 6])
        small = sb("small", [P, 4, T])
        mean = sb("mean", [P, T])
        var = sb("var", [P, T])
        std = sb("std", [P, T])
        rstd = sb("rstd", [P, T])
        x2s = sb("x2s", [P, CHUNK, D])
        xtile = sb("xtile", [P, 2, D])
        x2T = sb("x2T", [P, CHUNK * K, P])
        mean2 = sb("mean2", [P, T])
        raw2 = sb("raw2", [P, T])
        var_b = sb("var_b", [P, T])
        std_b = sb("std_b", [P, T])
        scale2 = sb("scale2", [P, T])
        bias2 = sb("bias2", [P, T])
        scale3 = sb("scale3", [P, T])
        lg = sb("lg", [P, T, E])
        pr = sb("pr", [P, T, E])
        m1 = sb("m1", [P, T, E])
        m2 = sb("m2", [P, T, E])
        r1 = sb("r1", [P, T])
        r2 = sb("r2", [P, T])
        w1c = sb("w1c", [P, T])
        w2c = sb("w2c", [P, T])
        mneg = sb("mneg", [P, K])
        msum = sb("msum", [P, K])
        valid = sb("valid", [P, 1])
        cnt = gb_b[:, 0:E * T].rearrange("p (e t) -> p e t", e=E)
        inc = gg_b[:, 0:E * T].rearrange("p (e t) -> p e t", e=E)
        pos = gbe_b[:, 0:E * T].rearrange("p (t e) -> p t e", t=T)
        tmpr = xtile[:, 0, 0:E * T].rearrange("p (t e) -> p t e", t=T)
        tl = sb("tl", [P, 4, E])
        tl_i = sb("tl_i", [P, E], I32)
        pos_i = sb("pos_i", [P, TOPK, T], I32)
        tile_f = sb("tile_f", [P, W])
        tile_e = sb("tile_e", [P, W], I32)

        acc_flat = acc[:, :, :].rearrange("p t d -> p (t d)")
        c2 = [0]

        def late(cols):
            a = c2[0]
            c2[0] += cols
            assert c2[0] <= (T + 1) * D
            return acc_flat[:, a:a + cols]

        xe = late(D + 1)
        xeT_f = late(D)
        xeT = [[late(D // 2).bitcast(F16) for _ in range(2)] for _ in range(2)]
        b2t = late(2 * D).rearrange("p (s d) -> p s d", s=2)
        h_f = [late(H) for _ in range(2)]
        h_pair = [[late(H // 2).bitcast(F16) for _ in range(2)] for _ in range(2)]
        bcol = late(KH)
        ys = late(D)
        gcol = late(2 * K)
        code_i = late(1).bitcast(I32)
        code_e = late(2).bitcast(I32)
        code_f = late(2)
        dest_f = late(1)
        dest_all = late(W).bitcast(I32)
        dest_i = sb("dest_i", [P, 1], I32)

        routed = acc_flat[:, 0:T * (D + 1)].rearrange("p (t d) -> p t d", d=D + 1)

        y12 = wall[:, 0:TOPK * T * D].rearrange("p (t j d) -> p t j d", t=T, j=TOPK)

        bank = [ctx.enter_context(nc.psum_tensor(f"bank{i}", [P, 512], F32)) for i in range(8)]
        w1e = wall[:, :].rearrange("p (e c) -> p e c", e=E)
        wpair = wall[:, :].bitcast(F16).rearrange("p (n h) -> p n h", h=2)
        ROUTER_BANKS = tuple(zip(range(0, CHUNK * K, 4), (2, 3, 5)))
        NFC = (K * HID + KM * D) // 1024
        CC = 1024
        CS = 2048
        EARLY_PAIRS = EARLY * WC // CS // 2
        PAIRS = E * WC // CS // 2
        split_hi = [x2T[:, 0:CS // 2 // P, :].rearrange("p u d -> p (u d)").bitcast(F16),
                    x2s[:, 0:CS // 2 // D, :].rearrange("p u d -> p (u d)").bitcast(F16)]

        passed = sem("passed")
        cleared = sem("cleared")
        iotas = sem("iotas")
        x_in = [sem(f"x_in{c}") for c in range(NC)]
        edges_in = sem("edges_in")
        weights_in = sem("weights_in")
        vrows_in = sem("vrows_in")
        rows_in = sem("rows_in")
        bcast_in = sem("bcast_in")
        early_in = sem("early_in")
        late_in = sem("late_in")
        slots_zeroed = sem("slots_zeroed")
        dve_step = sem("dve_step")
        act_step = sem("act_step")
        consts = sem("consts")
        vcol_ps = sem("vcol_ps")
        vcol_ok = sem("vcol_ok")
        wT_ps = sem("wT_ps")
        wT_ok = sem("wT_ok")
        var_ready = sem("var_ready")
        std_ready = sem("std_ready")
        ln1_done = sem("ln1_done")
        onehot_made = sem("onehot_made")
        onehot_used = sem("onehot_used")
        xs_ready = sem("xs_ready")
        xT_ps = sem("xT_ps")
        xT_ready = sem("xT_ready")
        xs_used = sem("xs_used")
        h_ps = sem("h_ps")
        h_ready = sem("h_ready")
        hist_done = sem("hist_done")
        counts_copied = sem("counts_copied")
        counts_spread = sem("counts_spread")
        table_ready = sem("table_ready")
        table_ready_act = sem("table_ready_act")
        dinv_ready = sem("dinv_ready")
        table_stored = sem("table_stored")
        extremes = sem("extremes")
        extremes_all = sem("extremes_all")
        sm_pe = sem("attention_pe")
        sm_dve = sem("attention_dve")
        sm_act = sem("attention_act")
        idx_ready = sem("idx_ready")
        gathered = [sem(f"gathered{k}") for k in range(SLOTS)]
        groups_ready = sem("groups_ready")
        hot_ready = sem("hot_ready")
        halves_summed = sem("halves_summed")
        groups_added = sem("groups_added")
        windows_known = sem("windows_known")
        wide_reloaded = sem("wide_reloaded")
        wide_gathered = sem("wide_gathered")
        wide_biased = sem("wide_biased")
        wide_idx = sem("wide_idx")
        wide_hot = sem("wide_hot")
        wide_summed = sem("wide_summed")
        wide_added = sem("wide_added")
        wide_shifted = sem("wide_shifted")
        aggregated = sem("aggregated")
        m1_ps = sem("m1_ps")
        m1_added = sem("m1_added")
        hn_ready = sem("hn_ready")
        hnT_ps = sem("hnT_ps")
        hnT_ready = sem("hnT_ready")
        fc1_ps = sem("fc1_ps")
        fc1_act = sem("fc1_act")
        fc1_hi = sem("fc1_hi")
        fc1_lo = sem("fc1_lo")
        fc2_ps = sem("fc2_ps")
        mix_added = sem("mix_added")
        xtile_in = sem("xtile_in")
        x2_ready = sem("x2_ready")
        x2T_ps = sem("x2T_ps")
        x2T_ready = sem("x2T_ready")
        lg_ps = sem("lg_ps")
        lg_ready = sem("lg_ready")
        scale3_ready = sem("scale3_ready")
        x3_ready = sem("x3_ready")
        rt_dve = sem("routing_dve")
        rt_act = sem("routing_act")
        rt_pe = sem("routing_pe")
        pos_ready = sem("pos_ready")
        rows_routed = sem("rows_routed")
        xe_in = sem("xe_in")
        bias_in = sem("bias_in")
        fc_hi = sem("fc_hi")
        fc_bias = sem("fc_bias")
        fc_lo = sem("fc_lo")
        fc_split = sem("fc_split")
        split_cast = sem("split_cast")
        split_low = sem("split_low")
        split_even = sem("split_even")
        split_odd = sem("split_odd")
        xe_transposed = sem("xe_transposed")
        xeT_ready = sem("xeT_ready")
        up_done = sem("up_done")
        activated = sem("activated")
        hidden_hi = sem("hidden_hi")
        hidden_lo = sem("hidden_lo")
        down_done = sem("down_done")
        y_ready = sem("y_ready")
        code_read = sem("code_read")
        y_stored = sem("y_stored")
        picked = [sem(f"picked{c}") for c in range(NC)]
        out_ready = sem("out_ready")
        out_stored = sem("out_stored")

        block = ctx.enter_context(nc.Block())

        @block.sync
        def _(sp):
            sp.wait_ge(cleared, 3)
            for buf, vec in ((dst_i, dst), (src_i[:, :], src)):
                v = buf.rearrange("p (g j) -> p g j", j=GT)
                sp.dma_start(v[:, 0:G - 1, :], vec[0:(G - 1) * EG].rearrange("(g p j) -> p g j", p=P, j=GT)).then_inc(edges_in, 16)
                sp.dma_start(v[0:EROW, G - 1, :], vec[(G - 1) * EG:(G - 1) * EG + EROW * GT].rearrange("(p j) -> p j", j=GT)).then_inc(edges_in, 16)
                sp.dma_start(v[EROW:EROW + 1, G - 1, 0:EREM], vec[NE - EREM:NE].rearrange("(p j) -> p j", p=1)).then_inc(edges_in, 16)
            for c in range(NC):
                a = c * CHUNK
                n = CHUNK if c < NC - 1 else CHUNK - 1
                sp.dma_start(xn[:, a:a + n, :], x[a * P:(a + n) * P, :].rearrange("(t p) d -> p t d", p=P)).then_inc(x_in[c], 16)
            sp.dma_start(xn[0:LAST, T - 1, :], x[(T - 1) * P:N, :]).then_inc(x_in[NC - 1], 16)
            sp.dma_start(gW_s, gW.rearrange("(k p) n -> p k n", p=P)).then_inc(weights_in, 16)
            sp.dma_start(wqkv_s, wqkv.rearrange("(k p) n -> p k n", p=P)).then_inc(weights_in, 16)
            sp.dma_start(wfc1_s, wfc1.rearrange("(k p) n -> p k n", p=P)).then_inc(weights_in, 16)
            sp.dma_start(wfc2_s, wfc2.rearrange("(k p) n -> p k n", p=P)).then_inc(weights_in, 16)
            sp.dma_start(wr_s[:, :, :], Wr.rearrange("(k p) n -> p k n", p=P)).then_inc(weights_in, 16)

            def load_expert(e, done):
                sp.dma_start(w1e[:, e, 0:K * H].rearrange("p (k n) -> p k n", k=K),
                             W1[e].rearrange("(k p) n -> p k n", p=P)).then_inc(done, 16)
                sp.dma_start(w1e[:, e, K * H:WC].rearrange("p (k n) -> p k n", k=KH),
                             W2[e].rearrange("(k p) n -> p k n", p=P)).then_inc(done, 16)

            for e in range(EARLY):
                load_expert(e, early_in)
            sp.wait_ge(consts, 1)
            sp.dma_start(slots.rearrange("(w p) d -> p w d", p=P),
                         blank.unsqueeze(1).to_broadcast([P, W, D + 1])).then_inc(slots_zeroed, 16)
            for c in range(NC):
                sp.wait_ge((table_ready, table_ready_act)[c % 2], c // 2 + 1)
                sp.dma_start(table[c * CHUNK * P:(c + 1) * CHUNK * P, :].rearrange("(t p) d -> p t d", p=P),
                             acc[:, c * CHUNK:(c + 1) * CHUNK, :]).then_inc(table_stored, 16)
            sp.dma_start(xtile[:, 0, :], x[0:P, :]).then_inc(xtile_in, 16)
            with sp.Fori(0, T - 2) as t:
                held(sp, passed, xtile_in, 16 * t + 16)
                held(sp, passed, mix_added, t + 1)
                sp.dma_start(xtile[:, (t + 1) % 2, :], x[bass.ds((t + 1) * P, P), :]).then_inc(xtile_in, 16)
            sp.wait_ge(xtile_in, 16 * (T - 1))
            sp.wait_ge(mix_added, T - 1)
            sp.dma_start(xtile[0:LAST, (T - 1) % 2, :], x[(T - 1) * P:N, :]).then_inc(xtile_in, 16)
            sp.wait_ge(aggregated, 1)
            sp.wait_ge(mix_added, T + 1)
            sp.wait_ge(idx_ready, G)
            sp.wait_ge(slots_zeroed, 16)
            for e in range(EARLY, E):
                load_expert(e, late_in)
            def load_rows(w):
                sp.dma_start(xe, slots[bass.ts(w, P), :]).then_inc(xe_in, 16)

            def load_bias(w):
                e = sp.value_load(tile_e[0:1, bass.ds(w, 1)], min_val=0, max_val=E - 1)
                if not isinstance(w, int) or w:
                    held(sp, passed, bias_in, 16 * w)
                held(sp, passed, y_ready, w + 1)
                sp.dma_start(b2t[:, w % 2, :], b2[e, :].partition_broadcast(P)).then_inc(bias_in, 16)

            sp.wait_ge(rows_routed, 16 * TOPK * T)
            load_rows(0)
            for w in range(1, 3):
                sp.wait_ge(xe_transposed, w)
                sp.wait_ge(code_read, w)
                load_rows(w)
            load_bias(0)
            with sp.Fori(0, W - 3) as w:
                held(sp, passed, xe_transposed, w + 3)
                held(sp, passed, code_read, w + 3)
                load_rows(w + 3)
                load_bias(w + 1)
            for w in range(W - 2, W):
                load_bias(w)
            sp.wait_ge(y_stored, 16 * W)
            for c in range(NC):
                a = c * CHUNK
                n = CHUNK if c < NC - 1 else CHUNK - 1
                sp.dma_start(y12[:, a:a + n, :, :], yrows[TOPK * a * P:TOPK * (a + n) * P, :].rearrange("(t p j) d -> p t j d", p=P, j=TOPK)).then_inc(picked[c], 16)
            sp.dma_start(y12[0:LAST, T - 1, :, :], yrows[TOPK * (T - 1) * P:TOPK * N, :].rearrange("(p j) d -> p j d", j=TOPK)).then_inc(picked[NC - 1], 16)
            for c in range(NC):
                a = c * CHUNK
                n = CHUNK if c < NC - 1 else CHUNK - 1
                sp.wait_ge(out_ready, c + 1)
                sp.dma_start(out[a * P:(a + n) * P, :].rearrange("(t p) d -> p t d", p=P), xn[:, a:a + n, :]).then_inc(out_stored, 16)
            sp.dma_start(out[(T - 1) * P:N, :], xn[0:LAST, T - 1, :]).then_inc(out_stored, 16)
            sp.wait_ge(out_stored, 16 * (NC + 1))

        @block.gpsimd
        def _(pool):
            g = nc.gpsimd
            g.memset(xn[:, T - 1, :], 0.0).then_inc(cleared, 1)
            g.memset(dst_i[:, (G - 1) * GT:], PAD_DST).then_inc(cleared, 1)
            g.memset(src_i[:, (G - 1) * GT:], 0).then_inc(cleared, 1)
            g.iota(iota_i, pattern=[[1, P]], base=0, channel_multiplier=0).then_inc(iotas, 1)
            g.iota(iotap_i[:, :], pattern=[[0, 1]], base=0, channel_multiplier=1).then_inc(iotas, 1)
            g.memset(acc[:, T, :], 0.0).then_inc(cleared, 1)
            pool.wait_ge(extremes, 1)
            g.partition_all_reduce(gall[:, :, :].rearrange("p a g -> p (a g)"), gm[:, :, :].rearrange("p a g -> p (a g)"), P, RMAX).then_inc(extremes_all, 1)
            pool.sem_inc(halves_summed, 2 * SLOTS)
            pool.wait_ge(edges_in, 96)
            pool.wait_ge(table_stored, 16 * NC)

            def gather(g_, slot, turn_before):
                held(pool, passed, halves_summed, 2 * g_ + 2)
                held(pool, passed, idx_ready, g_ + 1)
                for j in range(GT):
                    g.indirect_dma_start(ring[:, slot * GT + j, :], None, table,
                                         bass.IndirectOffsetOnAxis(ap=idx_s[:, slot, j:j + 1].bitcast(U32), axis=0)).then_inc(gathered[slot], 16)
                    if j == GT // 2 - 1 and turn_before is not None:
                        held(pool, passed, gathered[slot - 1], turn_before * (16 * GT))
                        pool.sem_inc(groups_ready, 1)

            gather(0, 0, None)
            TURNS = (G - 1) // SLOTS
            with pool.Fori(0, TURNS) as r:
                for k in range(1, SLOTS + 1):
                    gather(SLOTS * r + k, k % SLOTS, r + 1)
            for g_ in range(SLOTS * TURNS + 1, G):
                gather(g_, g_ % SLOTS, TURNS + 1)
            pool.wait_ge(gathered[(G - 1) % SLOTS], G // SLOTS * (16 * GT))
            pool.sem_inc(groups_ready, 1)
            pool.wait_ge(windows_known, 1)
            wide = pool.value_load(wide_i[0:1, 0:1], min_val=0, max_val=1)
            with pool.If(wide):
                pool.wait_ge(groups_added, G + 1)
                g.dma_start(acc[:, 0:T, :], table.rearrange("(t p) d -> p t d", p=P)).then_inc(wide_reloaded, 16)
                pool.sem_inc(wide_summed, 1)
                with pool.Fori(0, G) as q:
                    held(pool, passed, wide_summed, q * T + 1)
                    g.tensor_copy(idx_s[:, 0, :], src_i[:, bass.ds(q * GT, GT)]).then_inc(wide_idx, 1)
                    held(pool, passed, wide_idx, q + 1)
                    for j in range(GT):
                        g.indirect_dma_start(ring[:, j, :], None, table,
                                             bass.IndirectOffsetOnAxis(ap=idx_s[:, 0, j:j + 1].bitcast(U32), axis=0)).then_inc(wide_gathered, 16)
            pool.wait_ge(x3_ready, NC)
            pool.wait_ge(pos_ready, 1)
            pool.wait_ge(slots_zeroed, 16)
            for t in range(T):
                n = P if t < T - 1 else LAST
                for j in range(TOPK):
                    g.indirect_dma_start(slots, bass.IndirectOffsetOnAxis(ap=pos_i[0:n, j, t:t + 1].bitcast(U32), axis=0),
                                         routed[0:n, t, :], None).then_inc(rows_routed, 16)
            with pool.Fori(0, W) as w:
                held(pool, passed, y_ready, w + (AHEAD + 1))
                g.indirect_dma_start(yrows, bass.IndirectOffsetOnAxis(ap=dest_i[:, 0:1].bitcast(U32), axis=0), ys, None).then_inc(y_stored, 16)

        @block.scalar
        def _(act):
            s = nc.scalar
            for r, n, vec in ((VNG, K, ng), (VNB, K, nb), (VF1, KM, bfc1), (VBQ, K, bqkv[0:D])):
                act.dma_start(vrow[r:r + n, :], vec.rearrange("(r p) -> r p", p=P)).then_inc(vrows_in, 16)
            for r, mat in ((VLG, lng), (VLB, lnb)):
                act.dma_start(vrow[r:r + E * K, :], mat.rearrange("e (k p) -> (e k) p", p=P)).then_inc(vrows_in, 16)
            act.dma_start(vrow[VB1:VB1 + E * KH, :], b1.rearrange("e (k p) -> (e k) p", p=P)).then_inc(vrows_in, 16)
            act.dma_start(bqkv_s[0:1, :], bqkv.unsqueeze(0)).then_inc(rows_in, 16)
            act.dma_start(bfc2_s[0:1, :], bfc2.unsqueeze(0)).then_inc(rows_in, 16)
            act.dma_start(br_s[:, :], br.unsqueeze(0)).then_inc(rows_in, 16)
            for buf, vec in ((gb_b, gb), (gg_b, ggamma), (gbe_b, gbeta)):
                act.dma_start(buf[:, :], vec.partition_broadcast(P)).then_inc(bcast_in, 16)
            act.wait_ge(vcol_ps, 1)
            s.activation(vcol[:, :], bank[7][:, 0:NV], ACT.Copy).then_inc(vcol_ok, 1)
            for c in range(NC):
                act.wait_ge(var_ready, c + 1)
                s.activation(std[:, c * CHUNK:(c + 1) * CHUNK], var[:, c * CHUNK:(c + 1) * CHUNK], ACT.Sqrt).then_inc(std_ready, 1)
            act.wait_ge(wT_ps, 1)
            s.activation(gWT, bank[6][:, :].rearrange("p (k n) -> p k n", k=K), ACT.Copy).then_inc(wT_ok, 1)
            act.wait_ge(wT_ps, 2)
            s.activation(wqT, bank[7][:, :].rearrange("p (k n) -> p k n", k=K), ACT.Copy).then_inc(wT_ok, 1)
            act.wait_ge(ln1_done, NC)
            act.wait_ge(cleared, 4)
            act.sem_inc(xs_used, 1)

            def fixed_tile(t, a):
                held(act, passed, xs_used, t)
                s.activation(xs[a], xn[:, t, :], ACT.Copy).then_inc(xs_ready, 1)

            def transposed_tile(t, a):
                held(act, passed, xT_ps, t + 1)
                s.activation(xT_s[a], bank[2 + a][:, 0:D].rearrange("p (k n) -> p k n", k=K), ACT.Copy).then_inc(xT_ready, 1)

            def h_tile(t, a):
                held(act, passed, h_ps, t + 1)
                s.activation(acc[:, t, :], bank[4 + a][:, 0:D], ACT.Copy).then_inc(h_ready, 1)

            s.activation(xs[0], xn[:, 0, :], ACT.Copy).then_inc(xs_ready, 1)
            fixed_tile(1, 1)
            transposed_tile(0, 0)
            with act.Fori(0, (T - 3) // 2) as i:
                for b in range(2):
                    t, a = 2 * i + (1 + b), 1 - b
                    fixed_tile(t + 1, 1 - a)
                    transposed_tile(t, a)
                    h_tile(2 * i + b, 1 - a)
            fixed_tile(T - 1, 0)
            transposed_tile(T - 2, 1)
            h_tile(T - 3, 0)
            transposed_tile(T - 1, 0)
            h_tile(T - 2, 1)
            h_tile(T - 1, 0)
            act.wait_ge(var_ready, NC + 1)
            s.activation(deg_root[:, :], var[:, :], ACT.Sqrt).then_inc(std_ready, 1)
            act.wait_ge(dinv_ready, 1)
            act.wait_ge(h_ready, T + 1)
            for c in range(1, NC, 2):
                for t in range(c * CHUNK, (c + 1) * CHUNK):
                    ins = s.activation(acc[:, t, :], acc[:, t, :], ACT.Copy, scale=dinv[:, t:t + 1])
                ins.then_inc(table_ready_act, 1)
            act.wait_ge(sm_pe, 1)
            s.activation(srow[0:1, :], bank[6][0:1, 0:D], ACT.Copy).then_inc(sm_act, 1)
            act.wait_ge(sm_pe, 3)
            s.activation(xtv, bank[7][:, :].rearrange("p (k n) -> p k n", k=K), ACT.Copy).then_inc(sm_act, 1)
            act.wait_ge(sm_dve, 3)
            for k in range(K):
                s.activation(atb[:, k, 0:HD], att[:, k, :], ACT.Exp, bias=mneg[:, k:k + 1], accum_out=msum[:, k:k + 1]).then_inc(sm_act, 1)
            act.wait_ge(sm_pe, 5)
            s.activation(atT, bank[6][:, 0:K * P].rearrange("p (k n) -> p k n", k=K), ACT.Copy).then_inc(sm_act, 1)
            act.wait_ge(sm_pe, 6)
            s.activation(wqa, bank[7][:, :].rearrange("p (k n) -> p k n", k=K), ACT.Copy).then_inc(sm_act, 1)
            act.wait_ge(sm_pe, 7)
            s.activation(bqa[0:1, :], bank[6][0:1, 0:D], ACT.Copy).then_inc(sm_act, 1)
            def split_pair(i):
                for b in range(2):
                    if not isinstance(i, int) or i:
                        held(act, passed, (split_even, split_odd)[b], i)
                    s.activation(split_hi[b], wall[:, bass.ts(2 * i + b, CS)], ACT.Copy, scale=UP).then_inc(split_cast, 1)
                held(act, passed, split_low, 2 * i + 1)
                s.activation(wpair[:, bass.ts(2 * i, CS), 0], split_hi[0], ACT.Copy).then_inc(split_even, 1)

            for c in range(NFC):
                a = slice(c * CC, (c + 1) * CC)
                if c:
                    act.wait_ge(fc_split, c)
                s.activation(wfc_hi[0], wfc[:, a], ACT.Copy, scale=UP).then_inc(fc_hi, 1)
                act.wait_ge(fc_lo, c + 1)
                s.activation(wfc_pair[:, a, 0], wfc_hi[0], ACT.Copy).then_inc(fc_split, 1)
            act.wait_ge(early_in, 32 * EARLY)
            for i in range(EARLY_PAIRS):
                split_pair(i)
            act.wait_ge(xs_used, T + 1)
            with act.Fori(0, T) as t:
                s.activation(xs[0], xn[:, t, :], ACT.Copy).then_inc(xs_ready, 1)
                held(act, passed, xT_ps, t + (T + 1))
                s.activation(xT_s[0], bank[2][:, 0:D].rearrange("p (k n) -> p k n", k=K), ACT.Copy).then_inc(xT_ready, 1)
            act.wait_ge(var_ready, NC + 2)
            s.activation(std[:, :], var[:, :], ACT.Sqrt).then_inc(std_ready, 1)
            def mixer_activate(t):
                held(act, passed, fc1_ps, t + 1)
                held(act, passed, fc1_lo, t + 1)
                for m in range(KM):
                    ins = s.activation(h1_f[:, m * P:(m + 1) * P], bank[2 + m // 4][:, m % 4 * P:(m % 4 + 1) * P], ACT.Gelu,
                                       bias=vcol[:, VF1 + m:VF1 + m + 1], scale=1.0 / UP)
                ins.then_inc(fc1_act, 1)
                held(act, passed, fc1_act, t + 1)

            mixer_activate(0)
            s.activation(h1[0], h1_f, ACT.Copy).then_inc(fc1_hi, 1)
            with act.Fori(0, T - 1) as i:
                mixer_activate(i + 1)
                held(act, passed, fc2_ps, i + 1)
                s.activation(h1[0], h1_f, ACT.Copy).then_inc(fc1_hi, 1)
            act.wait_ge(var_ready, NC + 3)
            s.activation(std[:, :], var[:, :], ACT.Sqrt).then_inc(std_ready, 1)
            def copy_logits(c):
                act.wait_ge(lg_ps, c + 1)
                s.activation(lg[:, c * CHUNK:(c + 1) * CHUNK, :], bank[4][:, 0:CHUNK * E].rearrange("p (t e) -> p t e", t=CHUNK),
                             ACT.Copy).then_inc(lg_ready, 1)

            for c in range(NC):
                a = slice(c * CHUNK, (c + 1) * CHUNK)
                act.wait_ge(var_ready, NC + 4 + 2 * c)
                s.activation(std[:, a], var[:, a], ACT.Sqrt).then_inc(std_ready, 1)
                act.wait_ge(var_ready, NC + 5 + 2 * c)
                s.activation(std_b[:, a], var_b[:, a], ACT.Sqrt).then_inc(std_ready, 1)
                if c:
                    act.wait_ge(x3_ready, c)
                for u in range(CHUNK):
                    t = c * CHUNK + u
                    s.activation(x2s[:, u, :], xn[:, t, :], ACT.Identity, bias=bias2[:, t:t + 1],
                                 scale=scale2[:, t:t + 1]).then_inc(x2_ready, 1)
                if c:
                    copy_logits(c - 1)
                for q, (k0, bk) in enumerate(ROUTER_BANKS):
                    n = min(4, CHUNK * K - k0)
                    act.wait_ge(x2T_ps, len(ROUTER_BANKS) * c + q + 1)
                    s.activation(x2T[:, k0:k0 + n, :], bank[bk][:, 0:n * P].rearrange("p (k n) -> p k n", k=n),
                                 ACT.Copy).then_inc(x2T_ready, 1)
                act.wait_ge(x2_ready, (c + 1) * CHUNK)
                act.wait_ge(scale3_ready, c + 1)
                for u in range(CHUNK):
                    t = c * CHUNK + u
                    ins = s.activation(routed[:, t, 0:D], x2s[:, u, :], ACT.Copy, scale=scale3[:, t:t + 1])
                ins.then_inc(x3_ready, 1)
            copy_logits(NC - 1)
            act.wait_ge(rt_dve, 1)
            s.activation(pr[:, :, :], lg[:, :, :], ACT.Exp).then_inc(rt_act, 1)
            act.wait_ge(late_in, 32 * (E - EARLY))
            with act.Fori(0, PAIRS - EARLY_PAIRS) as i:
                split_pair(i + EARLY_PAIRS)
            b1_cols = vcol[:, VB1:VB1 + E * KH].rearrange("p (e k) -> p e k", k=KH)
            act.wait_ge(rows_routed, 16 * TOPK * T)

            def activate(w, a):
                e = act.value_load(tile_e[0:1, bass.ds(w, 1)], min_val=0, max_val=E - 1)
                s.activation(bcol, b1_cols[:, e, :], ACT.Copy).then_inc(act_step, 1)
                held(act, passed, act_step, w + 1)
                held(act, passed, up_done, w + AHEAD + 1)
                held(act, passed, hidden_lo, w + 1)
                for m in range(KH):
                    ins = s.activation(h_f[a][:, m * P:(m + 1) * P], bank[2 * a + m // 4][:, m % 4 * P:(m % 4 + 1) * P], ACT.Gelu,
                                       bias=bcol[:, m:m + 1], scale=1.0 / UP)
                ins.then_inc(activated, 1)
                held(act, passed, activated, w + AHEAD + 1)
                held(act, passed, down_done, w + 1)
                s.activation(h_pair[a][0], h_f[a], ACT.Copy).then_inc(hidden_hi, 1)

            for w in range(2):
                activate(w, w)
            with act.Fori(0, W // 2 - 1) as i:
                for a in range(2):
                    activate(2 * i + (2 + a), a)

        @block.tensor
        def _(pe):
            t_ = nc.tensor
            mm = t_.matmul

            def blocks(bk, n=K):
                return bank[bk][:, 0:n * P].rearrange("p (k n) -> p k n", k=n)

            pe.wait_ge(consts, 1)
            pe.wait_ge(vrows_in, 112)
            t_.transpose(bank[7][:, 0:NV], vrow[0:NV, :], ident[0:NV, 0:NV]).then_inc(vcol_ps, 1)
            pe.wait_ge(weights_in, 80)
            for k in range(K):
                for o in range(K):
                    ins = t_.transpose(bank[6][:, k * D + o * P:k * D + (o + 1) * P], gW_s[:, o, k * P:(k + 1) * P], ident[:, :])
            ins.then_inc(wT_ps, 1)
            pe.wait_ge(vcol_ok, 1)
            for q in range(K):
                for k in range(K):
                    ins = t_.transpose(bank[7][:, q * D + k * P:q * D + (k + 1) * P], wqkv_s[:, k, q * P:(q + 1) * P], ident[:, :])
            ins.then_inc(wT_ps, 1)
            pe.wait_ge(wT_ok, 2)

            for b in range(2):
                mm(bank[b][:, :], zeros[:, 0:P], zeros[:, :], start=True, stop=False)
            pe.sem_inc(h_ready, 1)

            def histogram(b):
                for h in range(2):
                    held(pe, passed, onehot_made, 2 * b + h + 1)
                    for j in range(GT):
                        ins = mm(bank[1][0:HALF, HAT:HAT + HCOLS], hot_lo[h][:, j, :], hot_hi[h][:, j, :], start=False, stop=False,
                                 skip_group_check=True)
                    ins.then_inc(onehot_used, 1)

            def x_transposed(t, a):
                held(pe, passed, xs_ready, t + 1)
                for k in range(K):
                    ins = t_.transpose(bank[2 + a][:, k * P:(k + 1) * P], xs[a][:, k * P:(k + 1) * P], ident[:, :])
                ins.then_inc(xT_ps, 1)

            def x_products(t, a):
                histogram(t)
                for k in range(K):
                    mm(bank[0][:, k * D:(k + 1) * D], xs[a][:, k * P:(k + 1) * P], xs[a], start=False, stop=False, skip_group_check=True)
                    ins = mm(bank[1][:, k:k + 1], xs[a][:, k * P:(k + 1) * P], ones[:, 0:1], start=False, stop=False, skip_group_check=True)
                ins.then_inc(xs_used, 1)
                held(pe, passed, xT_ready, t + 1)
                if not isinstance(t, int) or t > 1:
                    held(pe, passed, h_ready, t)
                for k in range(K):
                    ins = mm(bank[4 + a][:, 0:D], xT_s[a][:, k, :], gWT[:, k, :], start=(k == 0), stop=(k == K - 1))
                ins.then_inc(h_ps, 1)

            x_transposed(0, 0)
            x_transposed(1, 1)
            x_products(0, 0)
            with pe.Fori(0, (T - 3) // 2) as i:
                for b in range(2):
                    t, a = 2 * i + (1 + b), 1 - b
                    x_transposed(t + 1, 1 - a)
                    x_products(t, a)
            x_transposed(T - 1, 0)
            x_products(T - 2, 1)
            x_products(T - 1, 0)
            histogram(T)
            for b in range(2):
                ins = mm(bank[b][:, :], zeros[:, 0:P], zeros[:, :], start=False, stop=True)
            ins.then_inc(hist_done, 1)
            pe.wait_ge(counts_copied, 1)
            mm(bank[6][:, 0:HCOLS], twice[:, :], counts_s[:, :], start=True, stop=True).then_inc(counts_spread, 1)

            pe.wait_ge(rows_in, 48)
            pe.wait_ge(sm_dve, 1)
            for k in range(K):
                ins = mm(bank[6][0:1, k * P:(k + 1) * P], scol[:, k:k + 1], ident[:, :], start=True, stop=True)
            ins.then_inc(sm_pe, 1)
            for k in range(K):
                ins = mm(bank[5][0:1, 0:D], scol[:, k:k + 1], wqkv_s[:, k, 2 * D:3 * D], start=(k == 0), stop=(k == K - 1))
            ins.then_inc(sm_pe, 1)
            pe.wait_ge(sm_act, 1)
            for k in range(K):
                for j in range(K):
                    mm(bank[7][:, k * D:(k + 1) * D], gram[:, j, k * P:(k + 1) * P], wqkv_s[:, j, 2 * D:3 * D], start=(j == 0), stop=False)
                ins = mm(bank[7][:, k * D:(k + 1) * D], srow[0:1, k * P:(k + 1) * P], bqkv_s[0:1, 2 * D:3 * D], start=False, stop=True)
            ins.then_inc(sm_pe, 1)
            pe.wait_ge(sm_act, 2)
            pe.wait_ge(sm_dve, 2)
            for q in range(K):
                a = slice(q * P, (q + 1) * P)
                for k in range(K):
                    mm(bank[6][:, a], wqkv_s[:, k, D + q * P:D + (q + 1) * P], xtv[:, k, a], start=(k == 0), stop=False)
                ins = mm(bank[6][:, a], bqkv_s[0:1, D + q * P:D + (q + 1) * P], urow[0:1, a], start=False, stop=True)
            ins.then_inc(sm_pe, 1)
            pe.wait_ge(sm_dve, 4)
            for q in range(K):
                ins = t_.transpose(bank[6][:, q * P:(q + 1) * P], atb[:, q, :], ident[:, :])
            ins.then_inc(sm_pe, 1)
            pe.wait_ge(sm_act, 5)
            for k in range(K):
                for q in range(K):
                    ins = mm(bank[7][:, k * D + q * P:k * D + (q + 1) * P], wqT[:, q, k * P:(k + 1) * P], atT[:, q, :], start=True, stop=True)
            ins.then_inc(sm_pe, 1)
            for q in range(K):
                ins = mm(bank[6][0:1, q * P:(q + 1) * P], vcol[:, VBQ + q:VBQ + q + 1], atT[:, q, :], start=True, stop=True)
            ins.then_inc(sm_pe, 1)
            pe.wait_ge(sm_act, 7)

            def group(g):
                held(pe, passed, groups_ready, g + 1)
                held(pe, passed, groups_added, g + 1)
                half = GT // 2
                for h in range(2):
                    held(pe, passed, hot_ready, 2 * g + h + 1)
                    for j in range(half):
                        ins = mm(bank[0][:, 0:D], hot[h][:, j, :], ring[:, g % SLOTS * GT + (h * half + j), :],
                                 start=(h == 0 and j == 0), stop=(h == 1 and j == half - 1))
                    ins.then_inc(halves_summed, 1)

            pe.sem_inc(m1_added, 1)
            pe.sem_inc(mix_added, 1)
            with pe.Fori(0, T) as t:
                held(pe, passed, xs_ready, t + (T + 1))
                for k in range(K):
                    ins = t_.transpose(bank[2][:, k * P:(k + 1) * P], xs[0][:, k * P:(k + 1) * P], ident[:, :])
                ins.then_inc(xT_ps, 1)
                group(t)
                held(pe, passed, xT_ready, t + (T + 1))
                held(pe, passed, m1_added, t + 1)
                for k in range(K):
                    mm(bank[5][:, 0:D], xT_s[0][:, k, :], wqa[:, k, :], start=(k == 0), stop=False)
                mm(bank[5][:, 0:D], ones[0:1, :], bqa[0:1, :], start=False, stop=True).then_inc(m1_ps, 1)
            pe.wait_ge(fc_split, NFC)
            pe.wait_ge(fc_bias, 1)
            fc1_pair = wfc_pair[:, 0:K * HID, :].rearrange("p (k n) h -> p k n h", k=K)
            fc2_pair = wfc_pair[:, K * HID:, :].rearrange("p (k n) h -> p k n h", k=KM)

            def mixer_up(t):
                held(pe, passed, hn_ready, t + 1)
                for k in range(K):
                    ins = t_.transpose(bank[4][:, k * P:(k + 1) * P], hn_s[:, k * P:(k + 1) * P], ident[:, :])
                ins.then_inc(hnT_ps, 1)

            def mixer_hidden(t):
                held(pe, passed, hnT_ready, t + 1)
                if not isinstance(t, int) or t > 0:
                    held(pe, passed, fc1_act, t)
                for m in range(KM):
                    n = 0
                    for k in range(K):
                        for wh, xh in PARTS:
                            n += 1
                            ins = mm(bank[2 + m // 4][:, m % 4 * P:(m % 4 + 1) * P], fc1_pair[:, k, m * P:(m + 1) * P, wh],
                                     hnT[xh][:, k * P:(k + 1) * P], start=(n == 1), stop=(n == K * len(PARTS)))
                ins.then_inc(fc1_ps, 1)

            def mixer_down(t):
                held(pe, passed, fc1_lo, t + 2)
                held(pe, passed, mix_added, t + 1)
                for m in range(KM):
                    for wh, xh in PARTS:
                        mm(bank[5][:, 0:D], h1[xh][:, m * P:(m + 1) * P], fc2_pair[:, m, :, wh], start=(m == 0 and wh == 0 and xh == 0), stop=False)
                mm(bank[5][:, 0:D], ones[0:1, :], bfc2_s[0:1, :], start=False, stop=True).then_inc(fc2_ps, 1)

            mixer_up(0)
            mixer_hidden(0)
            mixer_up(1)
            group(T)
            with pe.Fori(0, T - 2) as t:
                mixer_hidden(t + 1)
                mixer_up(t + 2)
                mixer_down(t)
                group(t + (T + 1))
            mixer_hidden(T - 1)
            mixer_down(T - 2)
            group(G - 3)
            mixer_down(T - 1)
            group(G - 2)
            group(G - 1)
            pe.wait_ge(windows_known, 1)
            wide = pe.value_load(wide_i[0:1, 0:1], min_val=0, max_val=1)
            with pe.If(wide):
                pe.sem_inc(wide_added, 1)
                with pe.Fori(0, G) as q:
                    held(pe, passed, wide_gathered, q * (16 * GT) + 16 * GT)
                    with pe.Fori(0, T) as b:
                        n = q * T + b
                        held(pe, passed, wide_hot, n + 1)
                        held(pe, passed, wide_added, n + 1)
                        for j in range(GT):
                            ins = mm(bank[0][:, 0:D], hot[j // (GT // 2)][:, j % (GT // 2), :], ring[:, j, :],
                                     start=(j == 0), stop=(j == GT - 1))
                        ins.then_inc(wide_summed, 1)

            for c in range(NC):
                for k0, bk in ROUTER_BANKS:
                    for i in range(k0, min(k0 + 4, CHUNK * K)):
                        u, k = divmod(i, K)
                        if k == 0:
                            pe.wait_ge(x2_ready, c * CHUNK + u + 1)
                        ins = t_.transpose(bank[bk][:, i % 4 * P:(i % 4 + 1) * P], x2s[:, u, k * P:(k + 1) * P], ident[:, :])
                    ins.then_inc(x2T_ps, 1)
                if c:
                    pe.wait_ge(lg_ready, c)
                for u in range(CHUNK):
                    if u * K % 4 == 0:
                        pe.wait_ge(x2T_ready, len(ROUTER_BANKS) * c + u * K // 4 + 1)
                    for k in range(K):
                        mm(bank[4][:, u * E:(u + 1) * E], x2T[:, u * K + k, :], wr_s[:, k, :], start=(k == 0), stop=False)
                    ins = mm(bank[4][:, u * E:(u + 1) * E], ones[0:1, :], br_s[:, :], start=False, stop=True)
                ins.then_inc(lg_ps, 1)
            pe.wait_ge(rt_dve, 2)
            taken = tmpr.rearrange("p t e -> p (t e)")
            mm(bank[2][:, 0:T * E], before[:, :], taken, start=True, stop=True).then_inc(rt_pe, 1)
            mm(bank[3][:, 0:T * E], ones[:, :], taken, start=True, stop=True).then_inc(rt_pe, 1)

            def transpose_rows(w):
                held(pe, passed, xe_in, 16 * w + 16)
                for k in range(K):
                    ins = t_.transpose(bank[6][:, k * P:(k + 1) * P], xe[:, k * P:(k + 1) * P], ident[:, :])
                ins.then_inc(xe_transposed, 1)

            pairs = wpair.rearrange("p (e n) h -> p e n h", e=E)

            def up_steps(w, a, e):
                for m in range(KH):
                    n = 0
                    for k in range(K):
                        for wh, xh in PARTS:
                            n += 1
                            c = k * H + m * P
                            ins = mm(bank[2 * a + m // 4][:, m % 4 * P:(m % 4 + 1) * P], pairs[:, e, c:c + P, wh],
                                     xeT[a][xh][:, k * P:(k + 1) * P], start=(n == 1), stop=(n == K * len(PARTS)))
                            if m == KH - 1 and n == K * len(PARTS):
                                ins.then_inc(up_done, 1)
                            yield

            def down_steps(w, a, e):
                n = 0
                for m in range(KH):
                    for wh, xh in PARTS:
                        n += 1
                        c = K * H + m * D
                        ins = mm(bank[4 + a][:, 0:D], h_pair[a][xh][:, m * P:(m + 1) * P], pairs[:, e, c:c + D, wh],
                                 start=(n == 1), stop=(n == KH * len(PARTS)))
                        if n == KH * len(PARTS):
                            ins.then_inc(down_done, 1)
                        yield

            def expert_of(w):
                return pe.value_load(tile_e[0:1, bass.ds(w, 1)], min_val=0, max_val=E - 1)

            def experts_of(w, n):
                return nc.values_load_multi_w_load_instructions(tile_e[0:1, bass.ds(w, n)], engines=[mybir.EngineType.PE],
                                                                min_val=0, max_val=E - 1, skip_runtime_bounds_check_because="a sum of seven comparisons lies in 0 to 7")[1]

            def hold_down(w):
                held(pe, passed, hidden_lo, w + AHEAD + 1)
                held(pe, passed, y_ready, w + 1)

            def hold_all(w):
                held(pe, passed, hidden_lo, w + 1)

            def up_and_down(w, a, e_down, e_up):
                down = down_steps(w - AHEAD, a, e_down)
                for n, _ in enumerate(up_steps(w, a, e_up)):
                    if n % 2:
                        next(down)
                for _ in down:
                    pass

            def alone(steps):
                for _ in steps:
                    pass

            pe.wait_ge(split_even, PAIRS)
            pe.wait_ge(split_odd, PAIRS)
            transpose_rows(0)
            for w in range(AHEAD):
                pe.wait_ge(xeT_ready, w + 1)
                transpose_rows(w + 1)
                alone(up_steps(w, w, expert_of(w)))
            with pe.Fori(0, (W - 4) // UNROLL) as i:
                experts = experts_of(UNROLL * i, UNROLL + AHEAD)
                for u in range(UNROLL):
                    hold_all(UNROLL * i + (AHEAD + u))
                    transpose_rows(UNROLL * i + (AHEAD + 1 + u))
                    up_and_down(UNROLL * i + (AHEAD + u), u % 2, experts[u], experts[u + AHEAD])
            experts = experts_of(W - 4, 4)
            for a in range(2):
                hold_all(W - 2 + a)
                if a == 0:
                    transpose_rows(W - 1)
                up_and_down(W - 2 + a, a, experts[a], experts[a + 2])
            for w in range(W - 2, W):
                hold_down(w)
                alone(down_steps(w, w % 2, expert_of(w)))

        @block.vector
        def _(dve):
            v = nc.vector
            step = Chain(dve, dve_step, passed)
            dve.wait_ge(iotas, 2)
            v.tensor_copy(iota_f[:, :], iota_i)
            v.tensor_copy(iota_b[:, :], iota_i)
            v.memset(ones[:, :], 1.0)
            v.memset(zeros[:, :], 0.0)
            step(v.tensor_copy(iotap[:, :], iotap_i[:, :]))
            v.memset(blank[:, 0:D], 0.0)
            v.tensor_scalar(blank[:, D:D + 1], iotap[:, :], float(TOPK * E), float(TOPK * E * T * P), ALU.mult, ALU.add)
            v.tensor_scalar(valid[:, :], iotap[:, :], float(LAST), None, ALU.is_lt)
            v.tensor_scalar(before[:, :], iota_f[:, :], iotap[:, :], None, ALU.is_gt)
            for q in range(2):
                v.tensor_scalar(twice[:, q * HALF:(q + 1) * HALF], iota_f[0:HALF, 0:HALF], iotap[0:HALF, :], None, ALU.is_equal)
            v.tensor_scalar(ident[:, :], iota_f[:, :], iotap[:, :], None, ALU.is_equal).then_inc(consts, 1)

            def statistics(n, inv_n=1.0 / D):
                me, ve, mo, vo = (st[:, 0:n, q] for q in (1, 2, 4, 5))
                v.tensor_tensor(small[:, 0, 0:n], me, mo, ALU.add)
                v.tensor_tensor(small[:, 1, 0:n], me, mo, ALU.subtract)
                step(v.tensor_tensor(small[:, 2, 0:n], ve, vo, ALU.add))
                v.tensor_scalar(mean[:, 0:n], small[:, 0, 0:n], 0.5, None, ALU.mult)
                v.scalar_tensor_tensor(small[:, 3, 0:n], small[:, 1, 0:n], 0.25, small[:, 1, 0:n], ALU.mult, ALU.mult)
                step(v.tensor_scalar(small[:, 2, 0:n], small[:, 2, 0:n], inv_n, EPS, ALU.mult, ALU.add))
                v.tensor_tensor(var[:, 0:n], small[:, 2, 0:n], small[:, 3, 0:n], ALU.add).then_inc(var_ready, 1)

            def normalise(dest, source, n):
                for u in range(n):
                    ins = v.tensor_scalar(dest[:, u, :], source[:, u, :], mean[:, u:u + 1], rstd[:, u:u + 1],
                                          ALU.subtract, ALU.mult)
                return ins

            dve.wait_ge(edges_in, 96)
            lo3 = lo_f[:, :, :].rearrange("p g j -> p (g j)")
            flat_dst = dst_f[:, :, :].rearrange("p g j -> p (g j)")
            v.tensor_copy(idx_s[:, :, :].rearrange("p s j -> p (s j)"), src_i[:, 0:SLOTS * GT]).then_inc(idx_ready, SLOTS)
            step(v.tensor_scalar(tmp_i, dst_i, P - 1, None, ALU.bitwise_and))
            v.tensor_copy(flat_dst, dst_i)
            step(v.tensor_copy(lo3, tmp_i))
            step(v.tensor_scalar(tmp_i, dst_i, HALF - 1, None, ALU.bitwise_and))
            step(v.tensor_copy(lo_b[:, :, :].rearrange("p g j -> p (g j)"), tmp_i))
            step(v.tensor_scalar(tmp_i, dst_i, 6, None, ALU.logical_shift_right))
            v.tensor_copy(hi_b[:, :, :].rearrange("p g j -> p (g j)"), tmp_i)
            step(v.tensor_scalar(hi_f, flat_dst, float(N), float(P), ALU.is_ge, ALU.mult))
            step(v.tensor_tensor(lo3, lo3, hi_f, ALU.add))
            step(v.tensor_reduce(gm[:, 0, :], dst_f[:, :, :], AX_X, ALU.min))
            v.tensor_scalar(gm[:, 0, :], gm[:, 0, :], -1.0, None, ALU.mult)
            step(v.tensor_scalar(hi_f, dst_f[:, :, :].rearrange("p g j -> p (g j)"), float(N), None, ALU.is_lt))
            step(v.tensor_tensor(hi_f, hi_f, dst_f[:, :, :].rearrange("p g j -> p (g j)"), ALU.mult))
            v.tensor_reduce(gm[:, 1, :], hi_f.rearrange("p (g j) -> p g j", j=GT), AX_X, ALU.max).then_inc(extremes, 1)

            for c in range(NC):
                dve.wait_ge(x_in[c], 16 if c < NC - 1 else 32)
                xc = xn[:, c * CHUNK:(c + 1) * CHUNK, :]
                for u in range(CHUNK):
                    ins = v.bn_stats(st[:, u, :], xc[:, u, :])
                step(ins)
                me, ve, mo, vo = (st[:, 0:CHUNK, q] for q in (1, 2, 4, 5))
                n = CHUNK
                vc = var[:, c * n:(c + 1) * n]
                v.tensor_tensor(small[:, 0, 0:n], me, mo, ALU.add)
                v.tensor_tensor(small[:, 1, 0:n], me, mo, ALU.subtract)
                step(v.tensor_tensor(small[:, 2, 0:n], ve, vo, ALU.add))
                v.tensor_scalar(mean[:, 0:n], small[:, 0, 0:n], 0.5, None, ALU.mult)
                v.scalar_tensor_tensor(small[:, 3, 0:n], small[:, 1, 0:n], 0.25, small[:, 1, 0:n], ALU.mult, ALU.mult)
                step(v.tensor_scalar(small[:, 2, 0:n], small[:, 2, 0:n], 1.0 / D, EPS, ALU.mult, ALU.add))
                v.tensor_tensor(vc, small[:, 2, 0:n], small[:, 3, 0:n], ALU.add).then_inc(var_ready, 1)
                dve.wait_ge(std_ready, c + 1)
                step(v.reciprocal(rstd[:, 0:n], std[:, c * n:(c + 1) * n]))
                normalise(xc, xc, n).then_inc(ln1_done, 1)

            dve.sem_inc(onehot_used, 2)
            io = iota_b[:, :].unsqueeze(1).to_broadcast([P, GT, P])
            with dve.Fori(0, G // 2) as b:
                for h in range(2):
                    held(dve, passed, onehot_used, 2 * b + h + 1)
                    v.tensor_tensor(hot_lo[h], lo_b[:, 2 * b + h, :].unsqueeze(2).to_broadcast([P, GT, HALF]), io[:, :, 0:HALF],
                                    ALU.is_equal)
                    v.tensor_tensor(hot_hi[h], hi_b[:, 2 * b + h, :].unsqueeze(2).to_broadcast([P, GT, HCOLS]), io[:, :, 0:HCOLS],
                                    ALU.is_equal).then_inc(onehot_made, 1)

            dve.wait_ge(hist_done, 1)
            v.tensor_copy(counts_s[:, :], bank[1][0:HALF, HAT:HAT + HCOLS]).then_inc(counts_copied, 1)
            dve.wait_ge(counts_spread, 1)
            counts = bank[6][:, 0:HCOLS].rearrange("p (t q) -> p t q", q=2)
            for q in range(2):
                rows = slice(q * HALF, (q + 1) * HALF)
                ins = v.tensor_scalar(var[rows, :], counts[rows, :, q], 1.0, None, ALU.add)
            ins.then_inc(var_ready, 1)
            dve.wait_ge(std_ready, NC + 1)
            v.reciprocal(dinv[:, :], deg_root[:, :]).then_inc(dinv_ready, 1)
            dve.wait_ge(dinv_ready, 1)
            dve.wait_ge(h_ready, T + 1)
            for c in range(0, NC, 2):
                a = slice(c * CHUNK, (c + 1) * CHUNK)
                v.tensor_tensor(acc[:, a, :], acc[:, a, :], dinv[:, a].unsqueeze(2).to_broadcast([P, CHUNK, D]),
                                ALU.mult).then_inc(table_ready, 1)
            dve.wait_ge(extremes_all, 1)
            step(v.tensor_scalar(blk_f[:, :], gall[:, 0, :], -1.0, None, ALU.mult))
            step(v.tensor_copy(blk_i[:, :], blk_f[:, :]))
            step(v.tensor_scalar(blk_i[:, :], blk_i[:, :], 7, None, ALU.logical_shift_right))
            step(v.tensor_copy(mhi[:, :], blk_i[:, :]))
            step(v.scalar_tensor_tensor(blk_f[:, :], mhi[:, :], -float(P), blk_f[:, :], ALU.mult, ALU.add))
            step(v.tensor_scalar(mlo[:, :], blk_f[:, :], iotap[:, :], None, ALU.is_gt))
            step(v.tensor_scalar(mhi[:, :], mlo[:, :], -1.0, 1.0, ALU.mult, ALU.add))
            step(v.tensor_tensor(gm[:, 0, :], gall[:, 0, :], gall[:, 1, :], ALU.add))
            step(v.tensor_reduce(wide_f[:, :], gm[:, 0, :], AX_X, ALU.max))
            step(v.tensor_scalar(wide_f[:, :], wide_f[:, :], float(P), None, ALU.is_ge))
            v.tensor_copy(wide_i[:, :], wide_f[:, :]).then_inc(windows_known, 1)

            v.tensor_copy(scol[:, :], bank[1][:, 0:K])
            v.tensor_copy(gram, bank[0][:, :].rearrange("p (k n) -> p k n", k=K)).then_inc(sm_dve, 1)
            dve.wait_ge(sm_pe, 2)
            v.scalar_tensor_tensor(urow[0:1, :], bqkv_s[0:1, 2 * D:3 * D], float(N), bank[5][0:1, 0:D],
                                   ALU.mult, ALU.add).then_inc(sm_dve, 1)
            v.memset(atb, 0.0)
            dve.wait_ge(sm_pe, 4)
            for q in range(2):
                a = slice(q * HD, (q + 1) * HD)
                ins = v.tensor_scalar(att[a, :, :], bank[6][a, 0:K * P].rearrange("p (k n) -> p k n", k=K)[:, :, a],
                                      SCALE, None, ALU.mult)
            step(ins)
            step(v.tensor_reduce(mneg[:, :], att, AX_X, ALU.max))
            v.tensor_scalar(mneg[:, :], mneg[:, :], -1.0, None, ALU.mult).then_inc(sm_dve, 1)
            dve.wait_ge(sm_act, 4)
            step(v.reciprocal(msum[:, :], msum[:, :]))
            step(v.tensor_tensor(att, atb[:, :, 0:HD], msum[:, :].unsqueeze(2).to_broadcast([P, K, HD]), ALU.mult))
            step(v.memset(atb, 0.0))
            for q in range(2):
                a = slice(q * HD, (q + 1) * HD)
                ins = v.tensor_copy(atb[a, :, a], att[a, :, :])
            ins.then_inc(sm_dve, 1)

            def window_hot(g, h):
                held(dve, passed, halves_summed, 2 * SLOTS + 2 * g + h - 1)
                v.tensor_tensor(hot[h], lo_f[:, g, h * (GT // 2):(h + 1) * (GT // 2)].unsqueeze(2).to_broadcast([P, GT // 2, P]),
                                iota_f[:, :].unsqueeze(1).to_broadcast([P, GT // 2, P]), ALU.is_equal).then_inc(hot_ready, 1)

            def window_hots(g):
                for h in range(2):
                    window_hot(g, h)

            def add_window(g):
                held(dve, passed, halves_summed, 2 * SLOTS + 2 * g + 2)
                held(dve, passed, groups_added, g + 1)
                if not isinstance(g, int) or g + SLOTS < G:
                    v.tensor_copy(idx_s[:, g % SLOTS, :], src_i[:, bass.ds((g + SLOTS) * GT, GT)]).then_inc(idx_ready, 1)
                b = dve.value_load(blk_i[0:1, bass.ds(g, 1)], min_val=0, max_val=T - 1)
                v.scalar_tensor_tensor(acc[:, b, :], bank[0][:, 0:D], mhi[:, bass.ds(g, 1)], acc[:, b, :], ALU.mult, ALU.add)
                v.scalar_tensor_tensor(acc[:, b + 1, :], bank[0][:, 0:D], mlo[:, bass.ds(g, 1)], acc[:, b + 1, :],
                                       ALU.mult, ALU.add).then_inc(groups_added, 1)

            def split_pair(i):
                for b in range(2):
                    c = 2 * i + b
                    held(dve, passed, split_cast, c + 1)
                    v.scalar_tensor_tensor(wpair[:, bass.ts(c, CS), 1], wall[:, bass.ts(c, CS)], UP, split_hi[b],
                                           ALU.mult, ALU.subtract).then_inc(split_low, 1)
                held(dve, passed, split_low, 2 * i + 2)
                v.tensor_copy(wpair[:, bass.ts(2 * i + 1, CS), 0], split_hi[1]).then_inc(split_odd, 1)

            dve.wait_ge(rows_in, 48)
            v.tensor_scalar(bfc2_s[0:1, :], bfc2_s[0:1, :], UP, None, ALU.mult).then_inc(fc_bias, 1)
            for c in range(NFC):
                a = slice(c * CC, (c + 1) * CC)
                dve.wait_ge(fc_hi, c + 1)
                v.scalar_tensor_tensor(wfc_pair[:, a, 1], wfc[:, a], UP, wfc_hi[0], ALU.mult, ALU.subtract).then_inc(fc_lo, 1)
            for i in range(EARLY_PAIRS):
                split_pair(i)
            dve.sem_inc(groups_added, 1)
            dve.wait_ge(table_stored, 16 * NC)
            window_hots(0)

            def add_bias(t):
                return v.scalar_tensor_tensor(acc[:, t, :], gb_b[:, :], deg_root[:, bass.ds(t, 1)], acc[:, t, :], ALU.mult, ALU.add)

            dve.wait_ge(bcast_in, 48)
            with step.loop(T, 2) as t:
                held(dve, passed, groups_added, t + 1)
                step(add_bias(t))
                add_window(t)
                window_hots(t + 1)
                held(dve, passed, m1_ps, t + 1)
                step(v.tensor_tensor(xn[:, t, :], bank[5][:, 0:D], xn[:, t, :], ALU.add))
                v.bn_stats(st[:, t, :], xn[:, t, :]).then_inc(m1_added, 1)
            dve.wait_ge(m1_added, T + 1)
            statistics(T)
            dve.wait_ge(std_ready, NC + 2)
            step(v.reciprocal(rstd[:, :], std[:, :]))
            def normal_tile(t):
                v.tensor_scalar(hn_s, xn[:, t, :], mean[:, bass.ds(t, 1)], rstd[:, bass.ds(t, 1)], ALU.subtract, ALU.mult).then_inc(hn_ready, 1)

            def split_tile(t, last=False):
                held(dve, passed, hnT_ps, t + 1)
                for k in range(K):
                    ins = v.tensor_scalar(hnT_f[:, k * P:(k + 1) * P], bank[4][:, k * P:(k + 1) * P],
                                          vcol[:, VNG + k:VNG + k + 1], vcol[:, VNB + k:VNB + k + 1], ALU.mult, ALU.add)
                step(ins)
                step(v.tensor_copy(hnT[0], hnT_f))
                v.tensor_tensor(hnT[1], hnT_f, hnT[0], ALU.subtract).then_inc(hnT_ready, 1)

            def low_hidden(t):
                held(dve, passed, fc1_hi, t + 1)
                v.tensor_tensor(h1[1], h1_f, h1[0], ALU.subtract).then_inc(fc1_lo, 1)

            def add_mixer(t):
                held(dve, passed, fc2_ps, t + 1)
                step(v.scalar_tensor_tensor(xn[:, t, :], bank[5][:, 0:D], 1.0 / UP, xn[:, t, :], ALU.mult, ALU.add))
                held(dve, passed, xtile_in, 16 * t + 16)
                v.tensor_tensor(xn[:, t, :], xn[:, t, :], xtile[:, t % 2, :], ALU.add).then_inc(mix_added, 1)

            dve.sem_inc(fc1_lo, 1)
            normal_tile(0)
            split_tile(0)
            normal_tile(1)
            split_tile(1)
            normal_tile(2)
            low_hidden(0)
            with step.loop(T - 3, 3) as i:
                add_window(i + T)
                window_hots(i + (T + 1))
                split_tile(i + 2)
                normal_tile(i + 3)
                add_mixer(i)
                low_hidden(i + 1)
            add_window(2 * T - 3)
            window_hots(2 * T - 2)
            split_tile(T - 1)
            add_mixer(T - 3)
            low_hidden(T - 2)
            add_window(2 * T - 2)
            window_hots(2 * T - 1)
            add_mixer(T - 2)
            low_hidden(T - 1)
            add_window(2 * T - 1)
            window_hots(2 * T)
            add_mixer(T - 1)
            window_hots(G - 1)
            add_window(G - 2)
            add_window(G - 1)
            dve.wait_ge(groups_added, G + 1)
            dve.wait_ge(windows_known, 1)
            wide = dve.value_load(wide_i[0:1, 0:1], min_val=0, max_val=1)
            with dve.If(wide):
                dve.wait_ge(wide_reloaded, 16)
                with dve.Fori(0, T) as t:
                    add_bias(t).then_inc(wide_biased, 1)
                    held(dve, passed, wide_biased, t + 1)
                with dve.Fori(0, G) as q:
                    v.tensor_copy(shifted, dst_f[:, q, :]).then_inc(wide_shifted, 1)
                    with dve.Fori(0, T) as b:
                        n = q * T + b
                        held(dve, passed, wide_shifted, n + q + 1)
                        for h in range(2):
                            ins = v.tensor_tensor(hot[h], shifted[:, h * (GT // 2):(h + 1) * (GT // 2)].unsqueeze(2).to_broadcast([P, GT // 2, P]),
                                                  iota_f[:, :].unsqueeze(1).to_broadcast([P, GT // 2, P]), ALU.is_equal)
                        ins.then_inc(wide_hot, 1)
                        held(dve, passed, wide_summed, n + 2)
                        v.tensor_tensor(acc[:, b, :], acc[:, b, :], bank[0][:, 0:D], ALU.add).then_inc(wide_added, 1)
                        held(dve, passed, wide_added, n + 2)
                        v.tensor_scalar(shifted, shifted, -float(P), None, ALU.add).then_inc(wide_shifted, 1)
                    held(dve, passed, wide_shifted, q * (T + 1) + (T + 1))
            v.tensor_copy(wide_f[:, :], iotap[:, :]).then_inc(aggregated, 1)

            dve.wait_ge(groups_added, G + 1)
            dve.wait_ge(mix_added, T + 1)
            dve.wait_ge(bcast_in, 48)
            for t in range(T):
                ins = v.bn_stats(st[:, t, :], acc[:, t, :])
            step(ins)
            me, ve, mo, vo = (st[:, :, q] for q in (1, 2, 4, 5))
            v.tensor_tensor(small[:, 0, :], me, mo, ALU.add)
            v.tensor_tensor(small[:, 1, :], me, mo, ALU.subtract)
            step(v.tensor_tensor(small[:, 2, :], ve, vo, ALU.add))
            v.tensor_scalar(mean[:, :], small[:, 0, :], 0.5, None, ALU.mult)
            step(v.scalar_tensor_tensor(small[:, 3, :], small[:, 1, :], 0.25, small[:, 1, :], ALU.mult, ALU.mult))
            step(v.scalar_tensor_tensor(raw2[:, :], small[:, 2, :], 1.0 / D, small[:, 3, :], ALU.mult, ALU.add))
            step(v.tensor_tensor(raw2[:, :], raw2[:, :], dinv[:, :], ALU.mult))
            step(v.tensor_tensor(raw2[:, :], raw2[:, :], dinv[:, :], ALU.mult))
            v.tensor_scalar(var[:, :], raw2[:, :], EPS, None, ALU.add).then_inc(var_ready, 1)
            dve.wait_ge(std_ready, NC + 3)
            step(v.reciprocal(rstd[:, :], std[:, :]))
            step(v.tensor_tensor(rstd[:, :], rstd[:, :], dinv[:, :], ALU.mult))

            def graph_branch(c):
                tiles = range(c * CHUNK, (c + 1) * CHUNK)
                for t in tiles:
                    ins = v.scalar_tensor_tensor(acc[:, t, :], acc[:, t, :], mean[:, t:t + 1], gg_b[:, :], ALU.subtract, ALU.mult)
                step(ins)
                for t in tiles:
                    ins = v.scalar_tensor_tensor(acc[:, t, :], acc[:, t, :], rstd[:, t:t + 1], gbe_b[:, :], ALU.mult, ALU.add)
                step(ins)
                a = slice(c * CHUNK, (c + 1) * CHUNK)
                step(v.scalar_tensor_tensor(xn[:, a, :], acc[:, a, :], 0.0, xn[:, a, :], ALU.max, ALU.add))

            def second_statistics(c):
                a = slice(c * CHUNK, (c + 1) * CHUNK)
                for t in range(c * CHUNK, (c + 1) * CHUNK):
                    ins = v.bn_stats(st[:, t, :], xn[:, t, :])
                step(ins)
                me, ve, mo, vo = (st[:, a, q] for q in (1, 2, 4, 5))
                v.tensor_tensor(small[:, 0, a], me, mo, ALU.add)
                v.tensor_tensor(small[:, 1, a], me, mo, ALU.subtract)
                step(v.tensor_tensor(small[:, 2, a], ve, vo, ALU.add))
                v.tensor_scalar(mean2[:, a], small[:, 0, a], 0.5, None, ALU.mult)
                step(v.scalar_tensor_tensor(small[:, 3, a], small[:, 1, a], 0.25, small[:, 1, a], ALU.mult, ALU.mult))
                step(v.scalar_tensor_tensor(raw2[:, a], small[:, 2, a], 1.0 / D, small[:, 3, a], ALU.mult, ALU.add))
                v.tensor_scalar(var[:, a], raw2[:, a], EPS, None, ALU.add).then_inc(var_ready, 1)

            def second_scales(c):
                a = slice(c * CHUNK, (c + 1) * CHUNK)
                dve.wait_ge(std_ready, NC + 4 + 2 * c)
                step(v.reciprocal(scale2[:, a], std[:, a]))
                v.scalar_tensor_tensor(bias2[:, a], mean2[:, a], -1.0, scale2[:, a], ALU.mult, ALU.mult)
                step(v.tensor_tensor(raw2[:, a], raw2[:, a], scale2[:, a], ALU.mult))
                step(v.tensor_tensor(raw2[:, a], raw2[:, a], scale2[:, a], ALU.mult))
                v.tensor_scalar(var_b[:, a], raw2[:, a], EPS, None, ALU.add).then_inc(var_ready, 1)

            def third_scales(c):
                a = slice(c * CHUNK, (c + 1) * CHUNK)
                dve.wait_ge(std_ready, NC + 5 + 2 * c)
                v.reciprocal(scale3[:, a], std_b[:, a]).then_inc(scale3_ready, 1)

            graph_branch(0)
            second_statistics(0)
            for c in range(1, NC):
                graph_branch(c)
                second_scales(c - 1)
                second_statistics(c)
                third_scales(c - 1)
            second_scales(NC - 1)
            third_scales(NC - 1)

            dve.wait_ge(lg_ready, NC)
            dve.wait_ge(x3_ready, NC)

            def per_tile(a):
                return a[:, :].unsqueeze(2).to_broadcast([P, T, E])

            io8 = iota_f[:, 0:E].unsqueeze(1).to_broadcast([P, T, E])
            step(v.tensor_reduce(r1[:, :], lg[:, :, :], AX_X, ALU.max))
            v.tensor_tensor(lg[:, :, :], lg[:, :, :], per_tile(r1), ALU.subtract).then_inc(rt_dve, 1)
            dve.wait_ge(rt_act, 1)
            step(v.tensor_reduce(r1[:, :], pr[:, :, :], AX_X, ALU.add))
            step(v.reciprocal(r1[:, :], r1[:, :]))
            step(v.tensor_tensor(pr[:, :, :], pr[:, :, :], per_tile(r1), ALU.mult))

            def largest(mask, top):
                step(v.tensor_reduce(top[:, :], pr[:, :, :], AX_X, ALU.max))
                step(v.tensor_tensor(tmpr, pr[:, :, :], per_tile(top), ALU.is_lt))
                step(v.scalar_tensor_tensor(tmpr, tmpr, float(E), io8, ALU.mult, ALU.add))
                step(v.tensor_reduce(r2[:, :], tmpr, AX_X, ALU.min))
                step(v.tensor_tensor(mask[:, :, :], io8, per_tile(r2), ALU.is_equal))

            largest(m1, w1c)
            step(v.scalar_tensor_tensor(pr[:, :, :], m1[:, :, :], -2.0, pr[:, :, :], ALU.mult, ALU.add))
            largest(m2, w2c)
            step(v.tensor_scalar(r1[:, :], iota_f[:, 0:T], float(P), None, ALU.mult))
            step(v.tensor_scalar(r1[:, :], r1[:, :], iotap[:, :], None, ALU.add))
            step(v.scalar_tensor_tensor(routed[:, :, D], r1[:, :], float(TOPK * E), r2[:, :], ALU.mult, ALU.add))
            step(v.tensor_tensor(r1[:, :], w1c[:, :], w2c[:, :], ALU.add))
            step(v.reciprocal(r1[:, :], r1[:, :]))
            v.tensor_tensor(w1c[:, :], w1c[:, :], r1[:, :], ALU.mult)
            v.tensor_tensor(w2c[:, :], w2c[:, :], r1[:, :], ALU.mult)
            v.tensor_scalar(m1[:, T - 1, :], m1[:, T - 1, :], valid[:, :], None, ALU.mult)
            step(v.tensor_scalar(m2[:, T - 1, :], m2[:, T - 1, :], valid[:, :], None, ALU.mult))
            v.tensor_tensor(tmpr, m1[:, :, :], m2[:, :, :], ALU.add).then_inc(rt_dve, 1)
            dve.wait_ge(rt_pe, 2)
            cv = bank[3][:, 0:T * E].rearrange("p (t e) -> p e t", t=T)
            step(v.tensor_copy(cnt, cv))
            for e in range(E):
                ins = v.tensor_tensor_scan(inc[:, e, :], ones[:, 0:T], cnt[:, e, :], 0.0, ALU.mult, ALU.add)
            step(ins)
            step(v.tensor_scalar(tl[:, 0, :], inc[:, :, T - 1], float(P - 1), None, ALU.add))
            step(v.tensor_copy(tl_i[:, :], tl[:, 0, :]))
            step(v.tensor_scalar(tl_i[:, :], tl_i[:, :], 7, None, ALU.logical_shift_right))
            step(v.tensor_copy(tl[:, 1, :], tl_i[:, :]))
            step(v.tensor_tensor_scan(tl[:, 2, :], ones[:, 0:E], tl[:, 1, :], 0.0, ALU.mult, ALU.add))
            step(v.tensor_tensor(tl[:, 3, :], tl[:, 2, :], tl[:, 1, :], ALU.subtract))
            step(v.tensor_tensor(inc, inc, cnt, ALU.subtract))
            step(v.scalar_tensor_tensor(inc, tl[:, 3, :].unsqueeze(2).to_broadcast([P, E, T]), float(P), inc, ALU.mult, ALU.add))
            step(v.tensor_tensor(pos, bank[2][:, 0:T * E].rearrange("p (t e) -> p t e", t=T),
                                 inc.rearrange("p e t -> p t e"), ALU.add))
            for j, m in enumerate((m1, m2)):
                step(v.tensor_tensor(m[:, :, :], m[:, :, :], pos, ALU.mult))
                step(v.tensor_reduce(r1[:, :], m[:, :, :], AX_X, ALU.add))
                step(v.tensor_copy(pos_i[:, j, :], r1[:, :]))
            step(v.tensor_scalar(tile_f[:, :], iota_f[:, 0:W], tl[:, 3, 1:2], None, ALU.is_ge))
            for e in range(2, E):
                step(v.scalar_tensor_tensor(tile_f[:, :], iota_f[:, 0:W], tl[:, 3, e:e + 1], tile_f[:, :], ALU.is_ge, ALU.add))
            v.tensor_copy(tile_e[:, :], tile_f[:, :]).then_inc(pos_ready, 1)

            dve.wait_ge(pos_ready, 1)
            with dve.Fori(0, PAIRS - EARLY_PAIRS) as i:
                split_pair(i + EARLY_PAIRS)

            lg_cols = vcol[:, VLG:VLG + E * K].rearrange("p (e k) -> p e k", k=K)
            lb_cols = vcol[:, VLB:VLB + E * K].rearrange("p (e k) -> p e k", k=K)
            dve.wait_ge(rows_routed, 16 * TOPK * T)

            def expert_input(w, a):
                e = dve.value_load(tile_e[0:1, bass.ds(w, 1)], min_val=0, max_val=E - 1)
                held(dve, passed, xe_transposed, w + 1)
                held(dve, passed, up_done, w + 1)
                v.tensor_copy(gcol[:, 0:K], lg_cols[:, e, :])
                v.tensor_copy(gcol[:, K:2 * K], lb_cols[:, e, :])
                v.tensor_copy(code_i, xe[:, D:D + 1]).then_inc(code_read, 1)
                held(dve, passed, code_read, w + 1)
                for q in range(K):
                    v.tensor_scalar(xeT_f[:, q * P:(q + 1) * P], bank[6][:, q * P:(q + 1) * P], gcol[:, q:q + 1],
                                    gcol[:, K + q:K + q + 1], ALU.mult, ALU.add)
                v.tensor_scalar(code_e[:, 0:1], code_i, E - 1, None, ALU.bitwise_and)
                step(v.tensor_scalar(code_e[:, 1:2], code_i, E.bit_length() - 1, None, ALU.logical_shift_right))
                v.tensor_copy(code_f, code_e)
                step(v.tensor_copy(xeT[a][0], xeT_f))
                v.tensor_tensor(xeT[a][1], xeT_f, xeT[a][0], ALU.subtract).then_inc(xeT_ready, 1)
                step(v.scalar_tensor_tensor(dest_f, code_f[:, 0:1], tile_f[:, bass.ds(w, 1)], code_f[:, 1:2], ALU.is_equal, ALU.add))
                v.tensor_copy(dest_all[:, bass.ds(w, 1)], dest_f)

            def low_part(w, a):
                held(dve, passed, hidden_hi, w + 1)
                v.tensor_tensor(h_pair[a][1], h_f[a], h_pair[a][0], ALU.subtract).then_inc(hidden_lo, 1)

            def finish_tile(w, a):
                held(dve, passed, down_done, w + AHEAD + 1)
                held(dve, passed, bias_in, 16 * w + 16)
                if not isinstance(w, int) or w:
                    held(dve, passed, y_stored, 16 * w)
                v.tensor_copy(dest_i[:, :], dest_all[:, bass.ds(w, 1)])
                v.scalar_tensor_tensor(ys, bank[4 + a][:, 0:D], 1.0 / UP, b2t[:, w % 2, :], ALU.mult, ALU.add).then_inc(y_ready, 1)

            for free in (up_done, activated, hidden_lo, down_done, y_ready):
                dve.sem_inc(free, AHEAD)
            expert_input(0, 0)
            expert_input(1, 1)
            expert_input(2, 0)
            low_part(0, 0)
            expert_input(3, 1)
            low_part(1, 1)
            finish_tile(0, 0)
            expert_input(4, 0)
            low_part(2, 0)
            with step.loop(W // 2 - 3, 6) as i:
                for b in range(2):
                    a = 1 - b
                    finish_tile(2 * i + (1 + b), a)
                    expert_input(2 * i + (5 + b), a)
                    low_part(2 * i + (3 + b), a)
            finish_tile(W - 5, 1)
            expert_input(W - 1, 1)
            low_part(W - 3, 1)
            for w in range(W - 2, W):
                finish_tile(w - 2, w % 2)
                low_part(w, w % 2)
            for w in range(W - 2, W):
                finish_tile(w, w % 2)

            for c in range(NC):
                dve.wait_ge(picked[c], 16 if c < NC - 1 else 32)
                for t in range(c * CHUNK, (c + 1) * CHUNK):
                    ins = v.scalar_tensor_tensor(xn[:, t, :], y12[:, t, 0, :], w1c[:, t:t + 1], xn[:, t, :], ALU.mult, ALU.add)
                step(ins)
                for t in range(c * CHUNK, (c + 1) * CHUNK):
                    ins = v.scalar_tensor_tensor(xn[:, t, :], y12[:, t, 1, :], w2c[:, t:t + 1], xn[:, t, :], ALU.mult, ALU.add)
                ins.then_inc(out_ready, 1)


INS = ['x', 'src', 'dst', 'L0_gnn_W', 'L0_gnn_b', 'L0_gnn_gamma', 'L0_gnn_beta', 'L0_mix_w_qkv', 'L0_mix_b_qkv',
       'L0_mix_norm_g', 'L0_mix_norm_b', 'L0_mix_w_fc1', 'L0_mix_b_fc1', 'L0_mix_w_fc2', 'L0_mix_b_fc2',
       'L0_ffn_Wr', 'L0_ffn_br', 'L0_ffn_ln_g', 'L0_ffn_ln_b', 'L0_ffn_W1', 'L0_ffn_b1', 'L0_ffn_W2', 'L0_ffn_b2']


def kernel(**inputs):
    import numpy as np
    import concourse.bacc as bacc
    from concourse.bass_utils import run_bass_kernel_spmd

    nc = bacc.Bacc("TRN2", target_bir_lowering=False, num_devices=1)
    arrays, args = {}, []
    for name in INS:
        a = np.ascontiguousarray(inputs[name])
        arrays[f"in_{name}"] = a
        args.append(nc.dram_tensor(f"in_{name}", a.shape, mybir.dt.from_np(a.dtype), kind="ExternalInput").ap())
    args.append(nc.dram_tensor("out_x", inputs["x"].shape, F32, kind="ExternalOutput").ap())
    gps_layer(nc, *args)
    r = run_bass_kernel_spmd(nc, [arrays], core_ids=[0])
    return r.results[0]["out_x"]
```
